# Optimizing a Trainium2 kernel written in Bass

```python
import numpy as np
import jax
import jax.numpy as jnp

def _softmax(x, axis=-1):
    return jax.nn.softmax(x, axis=axis)

def _gelu(x):
    return jax.nn.gelu(x, approximate=True)

def _silu(x):
    return jax.nn.silu(x)

def _sigmoid(x):
    return jax.nn.sigmoid(x)

def _layernorm(x, axis=-1, eps=1e-05):
    m = jnp.mean(x, axis=axis, keepdims=True)
    v = jnp.var(x, axis=axis, keepdims=True)
    return (x - m) / jnp.sqrt(v + eps)

def _scatter_add(tgt, idx, src, axis=0):
    return tgt.at[idx].add(src)

def _segment_sum(src, seg, n):
    return jax.ops.segment_sum(src, seg, n)
kernel_name = 'mk_flamingo_gated_d4_seqx_r4_e4d695'

def setup_inputs(seed: int=0):
    np.random.seed(seed)
    _w = jnp.asarray

    def _rec_inputs():
        import jax
        import jax.numpy as jnp
        _rk = jax.random.key(seed)
        x = 7.22e-05 + 1 * jax.random.normal(jax.random.fold_in(_rk, 1), (2, 1024, 256), jnp.float32)
        _lenS = 1024 - jax.random.randint(jax.random.fold_in(_rk, 7), (2,), 0, max(1, 1024 // 4) + 1, jnp.int32)
        _lenS2 = 77 - jax.random.randint(jax.random.fold_in(_rk, 8), (2,), 0, max(1, 77 // 4) + 1, jnp.int32)
        _ctx_1024P = jax.random.normal(jax.random.fold_in(_rk, 11), (2, 16, 256), jnp.float32)
        _ctx_1024c = jax.random.dirichlet(jax.random.fold_in(_rk, 511), 0.3 * jnp.ones((16,), jnp.float32), (2, 77))
        _ctx_1024t = jnp.einsum('bsk,bkd->bsd', _ctx_1024c, _ctx_1024P)
        _ctx_1024t = _ctx_1024t * jax.lax.rsqrt(jnp.mean(jnp.square(_ctx_1024t)) + 1e-12) * 0.953939
        ctx_1024 = 4.13588e-05 + 0.999923 * (_ctx_1024t + 0.3 * jax.random.normal(jax.random.fold_in(_rk, 611), (2, 77, 256), jnp.float32))
        _validS = jnp.arange(1024)[None, :] < _lenS[:, None]
        _validS2 = jnp.arange(77)[None, :] < _lenS2[:, None]
        _causal = jnp.tril(jnp.ones((1024, 1024), dtype=bool))
        mask_1x1xSxS2_bk1 = jnp.broadcast_to(_validS2[0:1, None, None, :], (1, 1, 1024, 77))
        mask_SxS2_ik0 = jnp.where(jnp.broadcast_to(_validS2[0:1, :], (1024, 77)), 0, 1).astype(jnp.int32)
        _g = jax.random.normal(jax.random.fold_in(_rk, 9001), (2, 4), jnp.float32)
        _g = jnp.sign(_g) * jnp.maximum(jnp.abs(_g), 1.0) + (_g == 0) * 1.0
        g_xattn = _g[0]
        g_ffn = _g[1]
        return (x, ctx_1024, mask_1x1xSxS2_bk1, mask_SxS2_ik0, g_xattn, g_ffn)
    x, ctx_1024, mask_1x1xSxS2_bk1, mask_SxS2_ik0, g_xattn, g_ffn = _rec_inputs()

    def _L0_xattn_setup():
        import jax, jax.numpy as jnp
        import numpy as np
        D_MODEL = 256
        NUM_HEADS = 16
        D_K = D_MODEL // NUM_HEADS

        def _split_heads(x):
            B, S, _ = x.shape
            return x.reshape(B, S, NUM_HEADS, D_K).transpose(0, 2, 1, 3)
        key = jax.random.key(seed)
        ks = jax.random.split(key, 11)
        B, S = (4, 512)
        scale = 1.0 / np.sqrt(D_MODEL)
        inp = {'Q': jax.random.normal(ks[0], (B, S, D_MODEL), jnp.float32), 'K': jax.random.normal(ks[1], (B, S, D_MODEL), jnp.float32), 'V': jax.random.normal(ks[2], (B, S, D_MODEL), jnp.float32), 'Wq': jax.random.normal(ks[3], (D_MODEL, D_MODEL), jnp.float32) * scale, 'bq': jnp.zeros((D_MODEL,), jnp.float32), 'Wk': jax.random.normal(ks[4], (D_MODEL, D_MODEL), jnp.float32) * scale, 'bk': jnp.zeros((D_MODEL,), jnp.float32), 'Wv': jax.random.normal(ks[5], (D_MODEL, D_MODEL), jnp.float32) * scale, 'bv': jnp.zeros((D_MODEL,), jnp.float32), 'Wo': jax.random.normal(ks[6], (D_MODEL, D_MODEL), jnp.float32) * scale, 'bo': jnp.zeros((D_MODEL,), jnp.float32)}
        return inp
    _L0_xattn_all = _L0_xattn_setup()
    _L0_xattn_in = {k: v for k, v in _L0_xattn_all.items() if k in ('Wq', 'bq', 'Wk', 'bk', 'Wv', 'bv', 'Wo', 'bo')}
    del _L0_xattn_all

    def _L0_ffn_setup():
        import jax, jax.numpy as jnp
        import numpy as np
        ALPHA = 1.702
        LIMIT = 7.0
        TOPK = 2
        D, I, E = (256, 512, 8)
        B, S = (2, 512)

        def swiglu(x):
            g = x[..., ::2]
            l = x[..., 1::2]
            g = jnp.minimum(g, LIMIT)
            l = jnp.clip(l, -LIMIT, LIMIT)
            return g * jax.nn.sigmoid(ALPHA * g) * (l + 1.0)
        key = jax.random.key(seed)
        ks = jax.random.split(key, 16)
        sc = 0.02
        n = lambda k, shape, s=sc: jax.random.normal(k, shape, dtype=jnp.float32) * s
        return {'x': jax.random.normal(ks[0], (B, S, D), dtype=jnp.float32), 'gate_w': n(ks[1], (E, D)), 'gate_b': n(ks[2], (E,)), 'w1': n(ks[3], (E, D, 2 * I)), 'b1': n(ks[4], (E, 2 * I)), 'w3': n(ks[5], (E, D, 2 * I)), 'b3': n(ks[6], (E, 2 * I)), 'w2': n(ks[7], (E, I, D)), 'b2': n(ks[8], (E, D)), 'sw1': n(ks[9], (D, 2 * I)), 'sb1': n(ks[10], (2 * I,)), 'sw3': n(ks[11], (D, 2 * I)), 'sb3': n(ks[12], (2 * I,)), 'sw2': n(ks[13], (I, D)), 'sb2': n(ks[14], (D,))}
    _L0_ffn_all = _L0_ffn_setup()
    _L0_ffn_in = {k: v for k, v in _L0_ffn_all.items() if k in ('gate_w', 'gate_b', 'w1', 'b1', 'w3', 'b3', 'w2', 'b2', 'sw1', 'sb1', 'sw3', 'sb3', 'sw2', 'sb2')}
    del _L0_ffn_all

    def _L1_xattn_setup():
        import jax, jax.numpy as jnp
        import numpy as np
        EMBED_DIM = 256
        B, LQ, LK = (4, 512, 512)
        key = jax.random.key(seed)
        ks = jax.random.split(key, 9)
        d = EMBED_DIM
        s = 1.0 / np.sqrt(d)
        return {'query': jax.random.normal(ks[0], (B, LQ, d), dtype=jnp.float32), 'key': jax.random.normal(ks[1], (B, LK, d), dtype=jnp.float32), 'value': jax.random.normal(ks[2], (B, LK, d), dtype=jnp.float32), 'Wq': jax.random.uniform(ks[3], (d, d), jnp.float32, -s, s), 'bq': jax.random.uniform(ks[4], (d,), jnp.float32, -s, s), 'Wk': jax.random.uniform(ks[5], (d, d), jnp.float32, -s, s), 'bk': jax.random.uniform(ks[6], (d,), jnp.float32, -s, s), 'Wv': jax.random.uniform(ks[7], (d, d), jnp.float32, -s, s), 'bv': jax.random.uniform(ks[8], (d,), jnp.float32, -s, s)}
    _L1_xattn_all = _L1_xattn_setup()
    _L1_xattn_in = {k: v for k, v in _L1_xattn_all.items() if k in ('Wq', 'bq', 'Wk', 'bk', 'Wv', 'bv')}
    del _L1_xattn_all

    def _L1_ffn_setup():
        import jax, jax.numpy as jnp
        import numpy as np
        key = jax.random.key(seed)
        k1, k2, k3, k4 = jax.random.split(key, 4)
        B, T, M = (4, 512, 256)
        E, F = (16, 1024)
        x = jax.random.normal(k1, (B, T, M), dtype=jnp.float32) * 0.02
        Wg = jax.random.normal(k2, (M, E), dtype=jnp.float32) * 0.02
        w1 = jax.random.normal(k3, (E, M, F), dtype=jnp.float32) * 0.02
        w2 = jax.random.normal(k4, (E, F, M), dtype=jnp.float32) * 0.02
        return {'x': x, 'Wg': Wg, 'w1': w1, 'w2': w2}
    _L1_ffn_all = _L1_ffn_setup()
    _L1_ffn_in = {k: v for k, v in _L1_ffn_all.items() if k in ('Wg', 'w1', 'w2')}
    del _L1_ffn_all

    def _L2_xattn_setup():
        import jax, jax.numpy as jnp
        import numpy as np
        B, S, D, H = (2, 512, 256, 16)
        DH = D // H

        def _rope(x):
            s, dh = (x.shape[2], x.shape[3])
            inv = jnp.exp(jnp.arange(0, dh, 2, dtype=jnp.float32) * (-(4.0 * jnp.log(jnp.float32(10.0))) / dh))
            pos = jnp.arange(s, dtype=jnp.float32)[:, None]
            sin = jnp.sin(pos * inv)
            cos = jnp.cos(pos * inv)
            x1 = x[..., 0::2]
            x2 = x[..., 1::2]
            out = jnp.stack([x1 * sin - x2 * cos, -x1 * cos - x2 * sin], axis=-1)
            return out.reshape(x.shape)
        key = jax.random.key(seed)
        ks = jax.random.split(key, 12)
        f = lambda k, sh: jax.random.normal(k, sh, dtype=jnp.float32)
        inp = {'q': f(ks[0], (B, S, D)), 'k': f(ks[1], (B, S, D)), 'v': f(ks[2], (B, S, D))}
        scale = 1.0 / np.sqrt(D)
        names = ['q', 'k', 'v', 'o']
        for i, n in enumerate(names):
            inp['W' + n] = f(ks[3 + i], (D, D)) * scale
            inp['b' + n] = f(ks[7 + i], (D,)) * scale
        inp['mask'] = jnp.triu(jnp.ones((S, S), dtype=bool), k=1)[None, None]
        return inp
    _L2_xattn_all = _L2_xattn_setup()
    _L2_xattn_in = {k: v for k, v in _L2_xattn_all.items() if k in ('Wq', 'bq', 'Wk', 'bk', 'Wv', 'bv', 'Wo', 'bo')}
    del _L2_xattn_all

    def _L2_ffn_setup():
        import jax, jax.numpy as jnp
        import numpy as np
        EPS = 1e-08

        def _ste(x, q):
            return x + jax.lax.stop_gradient(q - x)

        def quant_act_uint8(x):
            s = jax.lax.stop_gradient(jnp.maximum(jnp.max(x), EPS)) / 255.0
            q = jnp.clip(jnp.round(x / s), 0.0, 255.0) * s
            return (_ste(x, q), s)

        def quant_weight_int8_perchannel(w):
            s = jax.lax.stop_gradient(jnp.maximum(jnp.max(jnp.abs(w), axis=1, keepdims=True), EPS)) / 127.0
            q = jnp.clip(jnp.round(w / s), -128.0, 127.0) * s
            return (_ste(w, q), s[:, 0])

        def quant_bias_int32(b, s_in, s_w):
            s = jax.lax.stop_gradient(s_in * s_w)
            q = jnp.round(b / s) * s
            return _ste(b, q)

        def quant_linear(x, w, b):
            xq, s_in = quant_act_uint8(x)
            wq, s_w = quant_weight_int8_perchannel(w)
            bq = quant_bias_int32(b, s_in, s_w)
            return jnp.einsum('btd,fd->btf', xq, wq) + bq
        key = jax.random.key(seed)
        k1, k2, k3, k4, k5 = jax.random.split(key, 5)
        B, S, D, F = (4, 512, 256, 1024)
        return {'x': jax.random.normal(k1, (B, S, D), dtype=jnp.float32), 'w1': jax.random.normal(k2, (F, D), dtype=jnp.float32) * (1.0 / np.sqrt(D)), 'b1': jax.random.normal(k3, (F,), dtype=jnp.float32) * 0.01, 'w2': jax.random.normal(k4, (D, F), dtype=jnp.float32) * (1.0 / np.sqrt(F)), 'b2': jax.random.normal(k5, (D,), dtype=jnp.float32) * 0.01}
    _L2_ffn_all = _L2_ffn_setup()
    _L2_ffn_in = {k: v for k, v in _L2_ffn_all.items() if k in ('w1', 'b1', 'w2', 'b2')}
    del _L2_ffn_all

    def _L3_xattn_setup():
        import jax, jax.numpy as jnp
        import numpy as np
        D_MODEL = 256
        N_HEADS = 16
        D_K = D_MODEL // N_HEADS
        B, L = (4, 512)
        key = jax.random.key(seed)
        ks = jax.random.split(key, 12)
        s_in = 1.0 / np.sqrt(D_MODEL)
        inp = {'Q': jax.random.normal(ks[0], (B, L, D_MODEL), jnp.float32), 'K': jax.random.normal(ks[1], (B, L, D_MODEL), jnp.float32), 'V': jax.random.normal(ks[2], (B, L, D_MODEL), jnp.float32), 'attn_mask': jnp.tril(jnp.ones((L, L), jnp.int32)), 'Wq': jax.random.normal(ks[3], (D_MODEL, D_MODEL), jnp.float32) * s_in, 'bq': jnp.zeros((D_MODEL,), jnp.float32), 'Wk': jax.random.normal(ks[4], (D_MODEL, D_MODEL), jnp.float32) * s_in, 'bk': jnp.zeros((D_MODEL,), jnp.float32), 'Wv': jax.random.normal(ks[5], (D_MODEL, D_MODEL), jnp.float32) * s_in, 'bv': jnp.zeros((D_MODEL,), jnp.float32), 'Wo': jax.random.normal(ks[6], (D_MODEL, D_MODEL), jnp.float32) * s_in, 'bo': jnp.zeros((D_MODEL,), jnp.float32)}
        return inp
    _L3_xattn_all = _L3_xattn_setup()
    _L3_xattn_in = {k: v for k, v in _L3_xattn_all.items() if k in ('Wq', 'bq', 'Wk', 'bk', 'Wv', 'bv', 'Wo', 'bo')}
    del _L3_xattn_all

    def _L3_ffn_setup():
        import jax, jax.numpy as jnp
        import numpy as np
        TOP_K = 2
        N_GROUP = 4
        TOPK_GROUP = 2
        ROUTED_SCALE = 2.5

        def _gate(xf, gate_w, gate_bias):
            logits = xf.astype(jnp.float32) @ gate_w.astype(jnp.float32)
            scores = jax.nn.sigmoid(logits)
            sfc = scores + gate_bias.astype(jnp.float32)[None]
            T, E = sfc.shape
            e_g = E // N_GROUP
            group_feat = sfc.reshape(T, N_GROUP, e_g)
            group_scores = jax.lax.top_k(group_feat, 2)[0].sum(axis=-1)
            _, group_idx = jax.lax.top_k(group_scores, TOPK_GROUP)
            group_mask = jax.nn.one_hot(group_idx, N_GROUP, dtype=sfc.dtype).sum(axis=1)
            score_mask = jnp.broadcast_to(group_mask[..., None], (T, N_GROUP, e_g)).reshape(T, E)
            tmp_scores = jnp.where(score_mask > 0, sfc, 0.0)
            _, topk_idx = jax.lax.top_k(tmp_scores, TOP_K)
            topk_w = jnp.take_along_axis(sfc, topk_idx, axis=-1)
            topk_w = topk_w / (topk_w.sum(axis=-1, keepdims=True) + 1e-20)
            return (topk_idx, topk_w * ROUTED_SCALE)
        key = jax.random.key(seed)
        ks = jax.random.split(key, 9)
        B, N, H, I, E, SH_I = (2, 256, 256, 128, 8, 256)
        s = lambda k, shape, scale: jax.random.normal(k, shape, jnp.float32) * scale
        return {'x': s(ks[0], (B, N, H), 1.0), 'gate_w': s(ks[1], (H, E), 0.02), 'gate_bias': s(ks[2], (E,), 0.02), 'w_gate': s(ks[3], (E, H, I), 0.02), 'w_up': s(ks[4], (E, H, I), 0.02), 'w_down': s(ks[5], (E, I, H), 0.02), 'sw_gate': s(ks[6], (H, SH_I), 0.02), 'sw_up': s(ks[7], (H, SH_I), 0.02), 'sw_down': s(ks[8], (SH_I, H), 0.02)}
    _L3_ffn_all = _L3_ffn_setup()
    _L3_ffn_in = {k: v for k, v in _L3_ffn_all.items() if k in ('gate_w', 'gate_bias', 'w_gate', 'w_up', 'w_down', 'sw_gate', 'sw_up', 'sw_down')}
    del _L3_ffn_all
    return {'x': x, 'ctx_1024': ctx_1024, 'mask_1x1xSxS2_bk1': mask_1x1xSxS2_bk1, 'mask_SxS2_ik0': mask_SxS2_ik0, 'g_xattn': g_xattn, 'g_ffn': g_ffn, 'L0_xattn_Wq': _L0_xattn_in['Wq'], 'L0_xattn_bq': _L0_xattn_in['bq'], 'L0_xattn_Wk': _L0_xattn_in['Wk'], 'L0_xattn_bk': _L0_xattn_in['bk'], 'L0_xattn_Wv': _L0_xattn_in['Wv'], 'L0_xattn_bv': _L0_xattn_in['bv'], 'L0_xattn_Wo': _L0_xattn_in['Wo'], 'L0_xattn_bo': _L0_xattn_in['bo'], 'L0_ffn_gate_w': _L0_ffn_in['gate_w'], 'L0_ffn_gate_b': _L0_ffn_in['gate_b'], 'L0_ffn_w1': _L0_ffn_in['w1'], 'L0_ffn_b1': _L0_ffn_in['b1'], 'L0_ffn_w3': _L0_ffn_in['w3'], 'L0_ffn_b3': _L0_ffn_in['b3'], 'L0_ffn_w2': _L0_ffn_in['w2'], 'L0_ffn_b2': _L0_ffn_in['b2'], 'L0_ffn_sw1': _L0_ffn_in['sw1'], 'L0_ffn_sb1': _L0_ffn_in['sb1'], 'L0_ffn_sw3': _L0_ffn_in['sw3'], 'L0_ffn_sb3': _L0_ffn_in['sb3'], 'L0_ffn_sw2': _L0_ffn_in['sw2'], 'L0_ffn_sb2': _L0_ffn_in['sb2'], 'L1_xattn_Wq': _L1_xattn_in['Wq'], 'L1_xattn_bq': _L1_xattn_in['bq'], 'L1_xattn_Wk': _L1_xattn_in['Wk'], 'L1_xattn_bk': _L1_xattn_in['bk'], 'L1_xattn_Wv': _L1_xattn_in['Wv'], 'L1_xattn_bv': _L1_xattn_in['bv'], 'L1_ffn_Wg': _L1_ffn_in['Wg'], 'L1_ffn_w1': _L1_ffn_in['w1'], 'L1_ffn_w2': _L1_ffn_in['w2'], 'L2_xattn_Wq': _L2_xattn_in['Wq'], 'L2_xattn_bq': _L2_xattn_in['bq'], 'L2_xattn_Wk': _L2_xattn_in['Wk'], 'L2_xattn_bk': _L2_xattn_in['bk'], 'L2_xattn_Wv': _L2_xattn_in['Wv'], 'L2_xattn_bv': _L2_xattn_in['bv'], 'L2_xattn_Wo': _L2_xattn_in['Wo'], 'L2_xattn_bo': _L2_xattn_in['bo'], 'L2_ffn_w1': _L2_ffn_in['w1'], 'L2_ffn_b1': _L2_ffn_in['b1'], 'L2_ffn_w2': _L2_ffn_in['w2'], 'L2_ffn_b2': _L2_ffn_in['b2'], 'L3_xattn_Wq': _L3_xattn_in['Wq'], 'L3_xattn_bq': _L3_xattn_in['bq'], 'L3_xattn_Wk': _L3_xattn_in['Wk'], 'L3_xattn_bk': _L3_xattn_in['bk'], 'L3_xattn_Wv': _L3_xattn_in['Wv'], 'L3_xattn_bv': _L3_xattn_in['bv'], 'L3_xattn_Wo': _L3_xattn_in['Wo'], 'L3_xattn_bo': _L3_xattn_in['bo'], 'L3_ffn_gate_w': _L3_ffn_in['gate_w'], 'L3_ffn_gate_bias': _L3_ffn_in['gate_bias'], 'L3_ffn_w_gate': _L3_ffn_in['w_gate'], 'L3_ffn_w_up': _L3_ffn_in['w_up'], 'L3_ffn_w_down': _L3_ffn_in['w_down'], 'L3_ffn_sw_gate': _L3_ffn_in['sw_gate'], 'L3_ffn_sw_up': _L3_ffn_in['sw_up'], 'L3_ffn_sw_down': _L3_ffn_in['sw_down']}

def reference(x, ctx_1024, mask_1x1xSxS2_bk1, mask_SxS2_ik0, g_xattn, g_ffn, L0_xattn_Wq, L0_xattn_bq, L0_xattn_Wk, L0_xattn_bk, L0_xattn_Wv, L0_xattn_bv, L0_xattn_Wo, L0_xattn_bo, L0_ffn_gate_w, L0_ffn_gate_b, L0_ffn_w1, L0_ffn_b1, L0_ffn_w3, L0_ffn_b3, L0_ffn_w2, L0_ffn_b2, L0_ffn_sw1, L0_ffn_sb1, L0_ffn_sw3, L0_ffn_sb3, L0_ffn_sw2, L0_ffn_sb2, L1_xattn_Wq, L1_xattn_bq, L1_xattn_Wk, L1_xattn_bk, L1_xattn_Wv, L1_xattn_bv, L1_ffn_Wg, L1_ffn_w1, L1_ffn_w2, L2_xattn_Wq, L2_xattn_bq, L2_xattn_Wk, L2_xattn_bk, L2_xattn_Wv, L2_xattn_bv, L2_xattn_Wo, L2_xattn_bo, L2_ffn_w1, L2_ffn_b1, L2_ffn_w2, L2_ffn_b2, L3_xattn_Wq, L3_xattn_bq, L3_xattn_Wk, L3_xattn_bk, L3_xattn_Wv, L3_xattn_bv, L3_xattn_Wo, L3_xattn_bo, L3_ffn_gate_w, L3_ffn_gate_bias, L3_ffn_w_gate, L3_ffn_w_up, L3_ffn_w_down, L3_ffn_sw_gate, L3_ffn_sw_up, L3_ffn_sw_down):
    import jax
    import jax.numpy as jnp

    def _L0_xattn_ref(Q, K, V, Wq, bq, Wk, bk, Wv, bv, Wo, bo):
        import jax, jax.numpy as jnp
        import numpy as np
        D_MODEL = 256
        NUM_HEADS = 16
        D_K = D_MODEL // NUM_HEADS

        def _split_heads(x):
            B, S, _ = x.shape
            return x.reshape(B, S, NUM_HEADS, D_K).transpose(0, 2, 1, 3)
        q = _split_heads(Q @ Wq + bq)
        k = _split_heads(K @ Wk + bk)
        v = _split_heads(V @ Wv + bv)
        scores = jnp.einsum('bhqd,bhkd->bhqk', q, k) / jnp.sqrt(jnp.float32(D_K))
        probs = jax.nn.softmax(scores, axis=-1)
        attn = jnp.einsum('bhqk,bhkd->bhqd', probs, v)
        B, H, S, _ = attn.shape
        combined = attn.transpose(0, 2, 1, 3).reshape(B, S, D_MODEL)
        return combined @ Wo + bo

    def _L0_ffn_ref(x, gate_w, gate_b, w1, b1, w3, b3, w2, b2, sw1, sb1, sw3, sb3, sw2, sb2):
        import jax, jax.numpy as jnp
        import numpy as np
        ALPHA = 1.702
        LIMIT = 7.0
        TOPK = 2
        D, I, E = (256, 512, 8)
        B, S = (2, 512)

        def swiglu(x):
            g = x[..., ::2]
            l = x[..., 1::2]
            g = jnp.minimum(g, LIMIT)
            l = jnp.clip(l, -LIMIT, LIMIT)
            return g * jax.nn.sigmoid(ALPHA * g) * (l + 1.0)
        b, s, d = x.shape
        xt = x.reshape(-1, d)
        scores = jax.nn.softmax(xt @ gate_w.T, axis=-1)
        biased = scores + gate_b
        _, idx = jax.lax.top_k(biased, TOPK)
        weights = jnp.take_along_axis(scores, idx, axis=-1)
        comb = (weights[..., None] * jax.nn.one_hot(idx, E, dtype=xt.dtype)).sum(1)

        def body(acc, p):
            ew1, eb1, ew3, eb3, ew2, eb2, ce = p
            h = swiglu((xt @ ew1 + eb1) * (xt @ ew3 + eb3))
            return (acc + ce[:, None] * (h @ ew2 + eb2), None)
        routed, _ = jax.lax.scan(body, jnp.zeros_like(xt), (w1, b1, w3, b3, w2, b2, comb.T))
        shared = swiglu((xt @ sw1 + sb1) * (xt @ sw3 + sb3)) @ sw2 + sb2
        return (routed + shared).reshape(b, s, d)

    def _L1_xattn_ref(query, key, value, Wq, bq, Wk, bk, Wv, bv):
        import jax, jax.numpy as jnp
        import numpy as np
        EMBED_DIM = 256
        B, LQ, LK = (4, 512, 512)
        scale = jnp.asarray(EMBED_DIM ** 0.5, query.dtype)
        Q = jnp.einsum('bqd,ed->bqe', query, Wq) + bq
        K = jnp.einsum('bkd,ed->bke', key, Wk) + bk
        V = jnp.einsum('bkd,ed->bke', value, Wv) + bv
        scores = jnp.einsum('bqe,bke->bqk', Q, K) / scale
        weights = jax.nn.softmax(scores, axis=-1)
        return jnp.einsum('bqk,bke->bqe', weights, V)

    def _L1_ffn_ref(x, Wg, w1, w2):
        import jax, jax.numpy as jnp
        import numpy as np
        d = x.shape[-1]
        xr = x.reshape(-1, d)
        S = xr.shape[0]
        E = Wg.shape[1]
        C = (S + E - 1) // E
        gate = jax.nn.softmax(xr @ Wg, axis=-1)
        idx = jnp.argmax(gate, axis=1)
        gates_s = jnp.take_along_axis(gate, idx[:, None], axis=1)[:, 0]
        onehot = jax.nn.one_hot(idx, E, dtype=jnp.int32)
        loc = jnp.sum((jnp.cumsum(onehot, axis=0) - 1) * onehot, axis=1)
        valid = loc < C
        loc_pad = jnp.minimum(loc, C)
        dispatched = jnp.zeros((E, C + 1, d), dtype=x.dtype).at[idx, loc_pad].set(xr)
        dispatched = dispatched[:, :C]
        h = jax.nn.relu(jnp.einsum('ecm,emf->ecf', dispatched, w1))
        expert_out = jnp.einsum('ecf,efm->ecm', h, w2)
        gathered = expert_out[idx, jnp.minimum(loc, C - 1)]
        combined = gathered * (gates_s * valid.astype(x.dtype))[:, None]
        return combined.reshape(x.shape)

    def _L2_xattn_ref(q, k, v, Wq, bq, Wk, bk, Wv, bv, Wo, bo, mask):
        import jax, jax.numpy as jnp
        import numpy as np
        B, S, D, H = (2, 512, 256, 16)
        DH = D // H

        def _rope(x):
            s, dh = (x.shape[2], x.shape[3])
            inv = jnp.exp(jnp.arange(0, dh, 2, dtype=jnp.float32) * (-(4.0 * jnp.log(jnp.float32(10.0))) / dh))
            pos = jnp.arange(s, dtype=jnp.float32)[:, None]
            sin = jnp.sin(pos * inv)
            cos = jnp.cos(pos * inv)
            x1 = x[..., 0::2]
            x2 = x[..., 1::2]
            out = jnp.stack([x1 * sin - x2 * cos, -x1 * cos - x2 * sin], axis=-1)
            return out.reshape(x.shape)
        b, s, d = q.shape
        h, dh = (H, DH)

        def proj(x, W, bias):
            return (x @ W.T + bias).reshape(b, -1, h, dh).transpose(0, 2, 1, 3)
        Q = proj(q, Wq, bq)
        K = proj(k, Wk, bk)
        V = proj(v, Wv, bv)
        PQ = _rope(Q)
        PK = _rope(K)
        scores = jnp.einsum('bhqd,bhkd->bhqk', PQ, PK)
        neg = jnp.finfo(scores.dtype).min
        scores = jnp.where(mask, neg, scores)
        p = jax.nn.softmax(scores, axis=-1)
        p = jnp.where(mask, jnp.float32(0.0), p)
        out = jnp.einsum('bhqk,bhkd->bhqd', p, V)
        out = out.transpose(0, 2, 1, 3).reshape(b, s, d)
        return out @ Wo.T + bo

    def _L2_ffn_ref(x, w1, b1, w2, b2):
        import jax, jax.numpy as jnp
        import numpy as np
        EPS = 1e-08

        def _ste(x, q):
            return x + jax.lax.stop_gradient(q - x)

        def quant_act_uint8(x):
            s = jax.lax.stop_gradient(jnp.maximum(jnp.max(x), EPS)) / 255.0
            q = jnp.clip(jnp.round(x / s), 0.0, 255.0) * s
            return (_ste(x, q), s)

        def quant_weight_int8_perchannel(w):
            s = jax.lax.stop_gradient(jnp.maximum(jnp.max(jnp.abs(w), axis=1, keepdims=True), EPS)) / 127.0
            q = jnp.clip(jnp.round(w / s), -128.0, 127.0) * s
            return (_ste(w, q), s[:, 0])

        def quant_bias_int32(b, s_in, s_w):
            s = jax.lax.stop_gradient(s_in * s_w)
            q = jnp.round(b / s) * s
            return _ste(b, q)

        def quant_linear(x, w, b):
            xq, s_in = quant_act_uint8(x)
            wq, s_w = quant_weight_int8_perchannel(w)
            bq = quant_bias_int32(b, s_in, s_w)
            return jnp.einsum('btd,fd->btf', xq, wq) + bq
        h = jax.nn.relu(quant_linear(x, w1, b1))
        return quant_linear(h, w2, b2)

    def _L3_xattn_ref(Q, K, V, Wq, bq, Wk, bk, Wv, bv, Wo, bo, attn_mask):
        import jax, jax.numpy as jnp
        import numpy as np
        D_MODEL = 256
        N_HEADS = 16
        D_K = D_MODEL // N_HEADS
        B, L = (4, 512)
        Bq, Lq, D = Q.shape
        Lk = K.shape[1]
        q = (Q @ Wq.T + bq).reshape(Bq, Lq, N_HEADS, D_K).transpose(0, 2, 1, 3)
        k = (K @ Wk.T + bk).reshape(Bq, Lk, N_HEADS, D_K).transpose(0, 2, 1, 3)
        v = (V @ Wv.T + bv).reshape(Bq, Lk, N_HEADS, D_K).transpose(0, 2, 1, 3)
        scores = jnp.einsum('bhqd,bhkd->bhqk', q, k) / jnp.sqrt(jnp.float32(D_K))
        mask = attn_mask[None, None, :, :]
        scores = jnp.where(mask == 0, jnp.float32(-jnp.inf), scores)
        attn = jax.nn.softmax(scores, axis=-1)
        out = jnp.einsum('bhqk,bhkd->bhqd', attn, v)
        out = out.transpose(0, 2, 1, 3).reshape(Bq, Lq, D)
        return out @ Wo.T + bo

    def _L3_ffn_ref(x, gate_w, gate_bias, w_gate, w_up, w_down, sw_gate, sw_up, sw_down):
        import jax, jax.numpy as jnp
        import numpy as np
        TOP_K = 2
        N_GROUP = 4
        TOPK_GROUP = 2
        ROUTED_SCALE = 2.5

        def _gate(xf, gate_w, gate_bias):
            logits = xf.astype(jnp.float32) @ gate_w.astype(jnp.float32)
            scores = jax.nn.sigmoid(logits)
            sfc = scores + gate_bias.astype(jnp.float32)[None]
            T, E = sfc.shape
            e_g = E // N_GROUP
            group_feat = sfc.reshape(T, N_GROUP, e_g)
            group_scores = jax.lax.top_k(group_feat, 2)[0].sum(axis=-1)
            _, group_idx = jax.lax.top_k(group_scores, TOPK_GROUP)
            group_mask = jax.nn.one_hot(group_idx, N_GROUP, dtype=sfc.dtype).sum(axis=1)
            score_mask = jnp.broadcast_to(group_mask[..., None], (T, N_GROUP, e_g)).reshape(T, E)
            tmp_scores = jnp.where(score_mask > 0, sfc, 0.0)
            _, topk_idx = jax.lax.top_k(tmp_scores, TOP_K)
            topk_w = jnp.take_along_axis(sfc, topk_idx, axis=-1)
            topk_w = topk_w / (topk_w.sum(axis=-1, keepdims=True) + 1e-20)
            return (topk_idx, topk_w * ROUTED_SCALE)
        B, N, H = x.shape
        xf = x.reshape(-1, H)
        topk_idx, topk_w = _gate(xf, gate_w, gate_bias)
        g = jax.nn.silu(jnp.einsum('th,ehi->tei', xf, w_gate))
        u = jnp.einsum('th,ehi->tei', xf, w_up)
        experts_y = jnp.einsum('tei,eih->teh', g * u, w_down)
        masked_y = jnp.take_along_axis(experts_y, topk_idx[:, :, None], axis=1)
        y = jnp.einsum('tkh,tk->th', masked_y, topk_w.astype(x.dtype)).reshape(B, N, H)
        shared = jax.nn.silu(x @ sw_gate) * (x @ sw_up) @ sw_down
        return y + shared
    x = x + jnp.tanh(g_xattn[0]) * _L0_xattn_ref(_layernorm(x, axis=-1), ctx_1024, ctx_1024, L0_xattn_Wq, L0_xattn_bq, L0_xattn_Wk, L0_xattn_bk, L0_xattn_Wv, L0_xattn_bv, L0_xattn_Wo, L0_xattn_bo)
    x = x + jnp.tanh(g_ffn[0]) * _L0_ffn_ref(_layernorm(x, axis=-1), L0_ffn_gate_w, L0_ffn_gate_b, L0_ffn_w1, L0_ffn_b1, L0_ffn_w3, L0_ffn_b3, L0_ffn_w2, L0_ffn_b2, L0_ffn_sw1, L0_ffn_sb1, L0_ffn_sw3, L0_ffn_sb3, L0_ffn_sw2, L0_ffn_sb2)
    x = x + jnp.tanh(g_xattn[1]) * _L1_xattn_ref(_layernorm(x, axis=-1), ctx_1024, ctx_1024, L1_xattn_Wq, L1_xattn_bq, L1_xattn_Wk, L1_xattn_bk, L1_xattn_Wv, L1_xattn_bv)
    x = x + jnp.tanh(g_ffn[1]) * _L1_ffn_ref(_layernorm(x, axis=-1), L1_ffn_Wg, L1_ffn_w1, L1_ffn_w2)
    x = x + jnp.tanh(g_xattn[2]) * _L2_xattn_ref(_layernorm(x, axis=-1), ctx_1024, ctx_1024, L2_xattn_Wq, L2_xattn_bq, L2_xattn_Wk, L2_xattn_bk, L2_xattn_Wv, L2_xattn_bv, L2_xattn_Wo, L2_xattn_bo, mask_1x1xSxS2_bk1)
    x = x + jnp.tanh(g_ffn[2]) * _L2_ffn_ref(_layernorm(x, axis=-1), L2_ffn_w1, L2_ffn_b1, L2_ffn_w2, L2_ffn_b2)
    x = x + jnp.tanh(g_xattn[3]) * _L3_xattn_ref(_layernorm(x, axis=-1), ctx_1024, ctx_1024, L3_xattn_Wq, L3_xattn_bq, L3_xattn_Wk, L3_xattn_bk, L3_xattn_Wv, L3_xattn_bv, L3_xattn_Wo, L3_xattn_bo, mask_SxS2_ik0)
    x = x + jnp.tanh(g_ffn[3]) * _L3_ffn_ref(_layernorm(x, axis=-1), L3_ffn_gate_w, L3_ffn_gate_bias, L3_ffn_w_gate, L3_ffn_w_up, L3_ffn_w_down, L3_ffn_sw_gate, L3_ffn_sw_up, L3_ffn_sw_down)
    return x

_drawn_inputs = setup_inputs


def setup_inputs(seed=0):
    import zlib

    import numpy as np

    out = dict(_drawn_inputs(seed))
    spreads = {'L0_xattn_bq': (0.0, 0.546),
     'L0_xattn_bk': (0.0, 2.0),
     'L0_xattn_bv': (0.0, 0.1),
     'L0_xattn_bo': (0.0, 0.1),
     'L3_xattn_bq': (0.0, 2.0),
     'L3_xattn_bk': (0.0, 2.0),
     'L3_xattn_bv': (0.0, 2.0),
     'L3_xattn_bo': (0.0, 2.0)}
    factors = {'g_ffn': 8.0,
     'L0_ffn_gate_w': 8.0,
     'L0_ffn_gate_b': 8.0,
     'L0_ffn_w1': 8.0,
     'L0_ffn_b1': 8.0,
     'L0_ffn_w3': 8.0,
     'L0_ffn_b3': 8.0,
     'L0_ffn_w2': 8.0,
     'L0_ffn_b2': 57.825,
     'L0_ffn_sw1': 4.231,
     'L0_ffn_sb1': 8.0,
     'L0_ffn_sw3': 4.236,
     'L0_ffn_sb3': 8.0,
     'L0_ffn_sw2': 4.152,
     'L0_ffn_sb2': 25.28,
     'L1_xattn_bq': 64.0,
     'L1_xattn_bk': 200.0,
     'L1_ffn_Wg': 6.104,
     'L1_ffn_w1': 7.191,
     'L1_ffn_w2': 6.057,
     'L2_xattn_bk': 200.0,
     'L2_ffn_b1': 190.865,
     'L2_ffn_b2': 64.0,
     'L3_ffn_gate_w': 5.659,
     'L3_ffn_gate_bias': 8.0,
     'L3_ffn_w_gate': 5.182,
     'L3_ffn_w_up': 5.036,
     'L3_ffn_w_down': 5.121,
     'L3_ffn_sw_gate': 5.669,
     'L3_ffn_sw_up': 5.087,
     'L3_ffn_sw_down': 5.075,
     'L1_xattn_Wq': 8.0,
     'L1_xattn_Wk': 8.0,
     'L1_xattn_Wv': 2.92,
     'L1_xattn_bv': 25.511,
     'L2_xattn_Wq': 3.168,
     'L2_xattn_bq': 54.06,
     'L2_xattn_Wk': 8.553,
     'L2_xattn_bv': 25.766,
     'L2_xattn_bo': 25.967,
     'L2_ffn_w1': 3.073,
     'L3_xattn_Wq': 15.49,
     'L3_xattn_Wk': 11.657}
    for name, (base, spread) in spreads.items():
        noise = np.random.default_rng([zlib.crc32(name.encode()), seed]).standard_normal(out[name].shape)
        drawn = base * np.exp(spread * noise) if base else spread * noise
        out[name] = jnp.asarray(drawn.astype(out[name].dtype))
    for name, factor in factors.items():
        out[name] = (out[name] * factor).astype(out[name].dtype)
    return out
```

```python
from contextlib import ExitStack

import numpy as np

import concourse.bass as bass
from concourse import mybir

ALU = mybir.AluOpType
ACT = mybir.ActivationFunctionType
AX = mybir.AxisListType
F32 = mybir.dt.float32
BF16 = mybir.dt.bfloat16
I32 = mybir.dt.int32
U8 = mybir.dt.uint8
U32 = mybir.dt.uint32
ds = bass.ds
RMAX = bass.bass_isa.ReduceOp.max

P = 128
D = 256
KD = D // P
NB, S = 2, 1024
T = NB * S
CH = 512
NCH = T // CH
CPB = S // CH
TPC = CH // P
NT = T // P
KEYS = 77
KP = 80
JG = KP // 16
HH = 8
NEG = -3.0e38
EPS = 1e-5
LN_STAGES = 8

C_ID, C_MEAN, C_ONE = 0, 128, 256
C_BLK, C_MHALF, C_TIE, C_IDX, C_PAD, C_SEL = 384, 392, 408, 424, 440, 441
C_MAGIC = C_SEL + JG * P
C_TOK = C_MAGIC + 1
C_STEP = C_TOK + 16
C_LT = C_STEP + 16
C_TILE = C_LT + 64
C_N = C_TILE + 40
MAGIC = 12582912.0
B_ID, B_SEL, B_TRI, B_ONE = 0, 128, 128 + JG * P, 256 + JG * P
B_N = B_ONE + 128
V_Q, V_K, V_O, V_QS, V_KS = 0, 2, 4, 6, 8
V_ATT = 10
V_F0 = 4 * V_ATT
E0, I0 = 9, 512
V_F2 = V_F0 + 4 * (I0 // P) + KD
F2 = 1024
V_N = V_F2 + F2 // P + KD
R0 = 8
W0 = KD * 4 * I0 + (I0 // P) * D
BC0 = 4 * (I0 // P)
TILES0 = (2 * T) // P + R0 - 1
E1, F1, C1 = 16, 1024, T // 16
E3 = 10
ORDER3 = [8, 9] + list(range(8))
W_Q, W_K, W_V, W_O, W_QS, W_KS = range(6)


def host_constants():
    cf = np.zeros((P, C_N), np.float32)
    p = np.arange(P)
    cf[:, C_ID:C_ID + P] = np.eye(P)
    cf[:, C_MEAN:C_MEAN + P] = 1.0 / D
    cf[:, C_ONE:C_ONE + P] = 1.0
    cf[:, C_BLK:C_BLK + HH] = p[:, None] // 16 == np.arange(HH)
    cf[:, C_MHALF:C_MHALF + 16] = -0.5
    cf[:, C_TIE:C_TIE + 16] = 16 - np.arange(16)
    cf[:, C_IDX:C_IDX + 16] = np.arange(16)
    cf[:, C_PAD] = np.where(p % 16 >= KEYS - 16 * (JG - 1), -1e30, 0.0)
    cf[:, C_MAGIC] = MAGIC
    cf[:, C_TOK:C_TOK + NT] = T + np.arange(NT) * P + p[:, None]
    cf[:, C_STEP:C_STEP + 16] = np.arange(16) * P
    cf[:, C_LT:C_LT + 64] = np.tril(np.ones((8, 8)), -1).reshape(-1)
    cf[:, C_TILE:C_TILE + 40] = np.arange(40)
    cb = np.zeros((P, B_N), np.float32)
    cb[:, B_ID:B_ID + P] = np.eye(P)
    for j in range(JG):
        hit = np.arange(KP)[:, None] == 16 * j + p[None] % 16
        cb[:KP, B_SEL + j * P:B_SEL + (j + 1) * P] = hit
        cf[:KP, C_SEL + j * P:C_SEL + (j + 1) * P] = hit
    cb[:, B_TRI:B_TRI + P] = p[:, None] < p[None]
    cb[:, B_ONE:B_ONE + P] = 1.0
    freq = np.exp(np.arange(0, 16, 2, dtype=np.float32) * (-(np.float32(4.0) * np.log(np.float32(10.0))) / np.float32(16)))
    ang = np.arange(S, dtype=np.float32)[None, :] * freq.astype(np.float32)[(p % 16) // 2][:, None]
    sign = np.where(p % 2 == 0, 1.0, -1.0).astype(np.float32)
    rope = np.stack([np.sin(ang) * sign[:, None], -np.cos(ang)], 1).astype(np.float32)
    return cf, cb, rope


def host_layout(i):
    a = {k: np.asarray(v) for k, v in i.items()}

    def rows(w):
        return w.reshape(-1, P, w.shape[-1]).transpose(1, 0, 2)

    def col(v):
        return v.reshape(-1, P).T

    cf, cb, rope = host_constants()
    swap = np.arange(D) ^ 1
    pad = list(range(KEYS)) + list(range(KP - KEYS))
    o = {"cf": cf, "cb": cb, "rope": rope}
    o["x"] = rows(a["x"].reshape(T, D).T)
    o["ctx"] = rows(a["ctx_1024"][:, pad].reshape(NB * KP, D).T)
    L = lambda l, n: a[f"L{l}_xattn_{n}"]
    att = {0: [L(0, "Wq"), L(0, "Wk"), L(0, "Wv"), L(0, "Wo")],
           1: [L(1, "Wq").T, L(1, "Wk").T, L(1, "Wv").T],
           2: [L(2, "Wq").T, L(2, "Wk").T, L(2, "Wv").T, L(2, "Wo").T, L(2, "Wq").T[:, swap], L(2, "Wk").T[:, swap]],
           3: [L(3, "Wq").T, L(3, "Wk").T, L(3, "Wv").T, L(3, "Wo").T]}
    for l, ws in att.items():
        o[f"aw{l}"] = np.stack([rows(w) for w in ws], 1)
        o[f"bv{l}"] = L(l, "bv")[None]
    cols = []
    for l in range(4):
        bo = L(l, "bo") if l != 1 else L(l, "bq")
        cols += [col(L(l, "bq")), col(L(l, "bk")), col(bo), col(L(l, "bq")[swap]), col(L(l, "bk")[swap])]
    F = lambda l, n: a[f"L{l}_ffn_{n}"]
    w1 = np.concatenate([F(0, "w1"), F(0, "sw1")[None]])
    w3 = np.concatenate([F(0, "w3"), F(0, "sw3")[None]])
    w2 = np.concatenate([F(0, "w2"), F(0, "sw2")[None]])
    b1 = np.concatenate([F(0, "b1"), F(0, "sb1")[None]])
    b3 = np.concatenate([F(0, "b3"), F(0, "sb3")[None]])
    b2 = np.concatenate([F(0, "b2"), F(0, "sb2")[None]])
    o["f0w"] = np.stack([np.concatenate(
        [rows(w[e]).reshape(P, -1) for w in (w1[:, :, ::2], w3[:, :, ::2], w1[:, :, 1::2], w3[:, :, 1::2], w2)]
        + [col(v) for v in (b1[e, ::2], b3[e, ::2], b1[e, 1::2], b3[e, 1::2])], 1) for e in range(E0)])
    o["f0b"] = b2
    cols += [col(b1[R0, ::2]), col(b3[R0, ::2]), col(b1[R0, 1::2]), col(b3[R0, 1::2]), col(b2[R0])]
    cols += [col(F(2, "b1")), col(F(2, "b2"))]
    o["cols"] = np.concatenate(cols, 1)
    o["g"] = np.concatenate([a["g_xattn"], a["g_ffn"]])[None]
    o["gate0"] = rows(F(0, "gate_w").T)
    o["gb0"] = F(0, "gate_b")[None]
    o["gate1"] = rows(F(1, "Wg"))
    o["gate3"] = rows(F(3, "gate_w"))
    o["gb3"] = F(3, "gate_bias")[None]
    o["f1w"] = np.stack([np.concatenate([rows(F(1, "w1")[e]).reshape(P, -1), rows(F(1, "w2")[e]).reshape(P, -1)], 1)
                         for e in range(E1)])
    o["f2w1"] = rows(F(2, "w1"))
    o["f2w2"] = rows(F(2, "w2"))
    wg = list(F(3, "w_gate")) + [F(3, "sw_gate")[:, :P], F(3, "sw_gate")[:, P:]]
    wu = list(F(3, "w_up")) + [F(3, "sw_up")[:, :P], F(3, "sw_up")[:, P:]]
    wd = list(F(3, "w_down")) + [F(3, "sw_down")[:P], F(3, "sw_down")[P:]]
    o["f3w"] = np.stack([np.concatenate([rows(g).reshape(P, -1), rows(u).reshape(P, -1), d], 1)
                         for g, u, d in zip(wg, wu, wd)], 1)
    m2 = np.pad(a["mask_1x1xSxS2_bk1"][0, 0], ((0, 0), (0, KP - KEYS)), constant_values=True)
    m3 = np.pad(a["mask_SxS2_ik0"], ((0, 0), (0, KP - KEYS)))
    for n, m in (("2", m2), ("3", m3)):
        o["mtok" + n] = m.reshape(S // P, P, KP).transpose(1, 0, 2)
        o["mkey" + n] = m.T
    return {k: np.ascontiguousarray(v) for k, v in o.items()}


def program(nc, d, out, stages):
    with ExitStack() as ctx:
        def sb(name, shape, dt=F32):
            return ctx.enter_context(nc.sbuf_tensor(name, shape, dt))

        sems = {}

        def sem(name):
            sems[name] = ctx.enter_context(nc.semaphore(name))
            return sems[name]

        def carver(arena):
            at = [0]

            def take(shape, dt=F32, parts=P):
                n = int(np.prod(shape))
                words = n if dt in (F32, I32, U32) else (n + 1) // 2 if dt == BF16 else (n + 3) // 4
                v = arena[0:parts, at[0]:at[0] + words]
                at[0] += words
                assert at[0] <= arena.shape[1], (at[0], arena.shape)
                if dt != F32:
                    v = v.bitcast(dt)
                if len(shape) > 1:
                    names = "abcde"[:len(shape)]
                    v = v.rearrange(f"p ({' '.join(names)}) -> p {' '.join(names)}",
                                    **{c: s for c, s in zip(names[1:], shape[1:])})
                return v
            return take

        x = sb("x_res", [P, KD, T])
        xn = sb("x_norm", [P, KD, T])
        cf = sb("const_f", [P, C_N])
        cb = sb("const_b", [P, B_N], BF16)
        cols = sb("cols_sb", [P, V_N])
        ctxk = sb("ctx_sb", [P, KD, NB * KP])
        gts = sb("gates_tanh", [P, 8])
        gbo = sb("gated_bias", [P, 4, KD])
        aw_even = sb("aw_even", [P, 6 * KD * D + D])
        aw_odd = sb("aw_odd", [P, 4 * KD * D + D])
        gate_w = sb("gate_w", [P, 3, KD * 16])
        gate_b = sb("gate_b", [P, 2, 8])
        mtok = sb("mask_tok", [P, S // P, KP], BF16)
        mkey = sb("mask_key", [KP, S], BF16)
        big = sb("big", [P, 16384])
        work = sb("work", [P, 18900])
        zero = sb("zero", [P, D])

        aw, bv = {}, {}
        for l in range(4):
            arena, n = (aw_even, (4, 0, 6)[l]) if l % 2 == 0 else (aw_odd, (0, 3, 0, 4)[l])
            aw[l] = arena[:, 0:n * KD * D].rearrange("p (w k n) -> p w k n", w=n, k=KD)
            bv[l] = arena[0:1, arena.shape[1] - D:arena.shape[1]]

        ident = cf[:, C_ID:C_ID + P]
        mean_w = cf[:, C_MEAN:C_MEAN + P]
        ones_row = cf[0:1, C_ONE:C_ONE + P]
        blk = cf[:, C_BLK:C_BLK + HH]
        identb = cb[:, B_ID:B_ID + P]

        ps = ctx.enter_context(nc.psum_tensor("ps", [P, 8, CH], F32))

        take = carver(work)
        sq = take([KD, CH])
        stat = take([4, NT])
        osc = take([KD, CH])
        kbd = take([KD, NB, JG, HH * 16])
        vbd = take([NB, JG, D])
        v80 = take([NB, D])
        kt = take([KD, NB * KP])
        q = take([KD, CH])
        smax = take([TPC, 2 * HH])
        smaxe = take([TPC, KD * P])
        mb = take([KD, CH])
        dif = take([2, CH])
        rt = dif
        pr = take([JG, CH])
        psum_ = take([KD, CH])
        num = mb
        rd = take([TPC, 2 * HH])
        rde = smaxe
        neg4 = take([3, TPC])
        p1 = take([TPC, KP])
        pt = take([CH])
        o = take([KD, CH])
        take = carver(big)
        cb_raw = big[:, 0:B_N]
        rope = take([2, S])
        mtok_raw = {2: take([S // P, KP], U8), 3: take([S // P, KP], I32)}
        mkey_raw = {2: take([S], U8, KP), 3: take([S], I32, KP)}

        IM = I0 // P
        ring = carver(big)
        w0 = [ring([W0 + BC0]) for _ in range(3)]
        w1m = [w[:, 0:4096] for w in w0]
        hbig = big[:, 0:16384].rearrange("p (m t) -> p m t", m=F2 // P)
        combb = big[:, 0:16384].rearrange("p (e t) -> p e t", e=8)
        wq_raw = big[:, 4096:8192]
        rope_words = 2 * S

        take = carver(work)
        take([KD, CH]), take([4, NT]), take([KD, CH])
        xc = osc
        rows_ = take([NT, D])
        ra = [take([NT * 16]) for _ in range(6)]
        rv = [take([NT]) for _ in range(8)]
        oh1, oh2 = take([NT * 16]), take([NT * 16])
        mb16 = take([NT, 16], BF16)
        wt1, wt2 = take([NT]), take([NT])
        gix1, gix2 = take([NT], U32), take([NT], U32)
        six = take([NT], U32)
        e8 = [take([8]) for _ in range(4)]
        cmp8 = take([8, 16])
        cmpt = take([TILES0, 8])
        texf, tex = take([TILES0]), take([TILES0], I32)
        b2row = [take([D]) for _ in range(3)]
        xs = [take([D]) for _ in range(3)]
        xst = [take([KD * P]).rearrange("p (k n) -> p k n", k=KD) for _ in range(3)]
        os_ = [take([D]) for _ in range(3)]
        tail = take([6 * CH + 3 * F1])
        ag, al, pg, pl, sig, uu = (tail[:, n * CH:(n + 1) * CH] for n in range(6))
        hall = tail[:, 6 * CH:]
        hh = [hall[:, n * F1:(n + 1) * F1] for n in range(3)]
        hs = hall[:, 0:IM * CH].rearrange("p (m n) -> p m n", m=IM)
        ga = rows_
        gb = tail[:, 0:NT * D].rearrange("p (t n) -> p t n", t=NT)
        ya = hall[:, F1:2 * F1].rearrange("p (t n) -> p t n", t=TPC)
        yb = hall[:, 2 * F1:3 * F1].rearrange("p (t n) -> p t n", t=TPC)

        take = carver(work)
        take([KD, CH]), take([4, NT]), take([KD, CH])
        wq1, wq2 = take([F2 // P, D], BF16), take([KD, F2], BF16)
        wt1q, wt2q = take([KD, F2], BF16), take([F2 // P, D], BF16)
        xq = take([KD, T], BF16)
        hq = take([F2 // P, T], BF16)
        qs = take([8, F2 // P])
        qv = take([12])
        take = carver(work)
        take([KD, CH]), take([4, NT]), take([KD, CH])
        w3 = take([E3, 3 * D])
        lg3 = [take([NT, 8]) for _ in range(8)]
        rv3 = [take([NT]) for _ in range(8)]
        gr = [take([NT, 4]) for _ in range(7)]
        combt = take([8, NT])
        combT = take([P])
        sg3, t3, u3, h3 = take([2, CH]), take([CH]), take([CH]), take([2, CH])

        disp = nc.dram_tensor("dispatched", (TILES0 * P, D), F32, kind="Internal").ap()
        outs = nc.dram_tensor("expert_out", (TILES0 * P, D), F32, kind="Internal").ap()
        disp1 = nc.dram_tensor("dispatched1", (2 * T, D), F32, kind="Internal").ap()
        outs1 = nc.dram_tensor("expert_out1", (T, D), F32, kind="Internal").ap()
        comb3 = nc.dram_tensor("comb3", (P, P), F32, kind="Internal").ap()

        CREDIT = 1
        loop_sems = [sem(n) for n in (
            "x_done mean_done cent_done sq_done var_done rstdb_done xn_done "
            "q_done qsb_done score_done max_done maxe_done mb_done mbsb_done st_done sub_done exp_done pv_done "
            "padd_done den_done rd_done rde_done rb_done num_done o_done proj_done osc_done rope_done clamp_done "
            "q1_done qsb1_done score1_done max1_done neg1_done exp1_done rd1_done p1_done pt_done ptsb_done att1_done osc1_done "
            "xc_done front_done rows_done "
            "sa_done sp_done spm_done spc_done su_done sh_done ssig_done spair_done so_done sosc_done sx_done "
            "xt_done xst_done g_done ag_done pg_done pgm_done l_done al_done pl_done plc_done u_done h_done sig_done o2_done "
            "os_done ya_done yb_done y_done comb_done "
            "m1_done hact_done hrnd_done m2_done osc2_done xrnd_done xclip_done xq_done hq_done hmax_done "
            
            ).split()]
        (x_done, mean_done, cent_done, sq_done, var_done, rstdb_done, xn_done,
         q_done, qsb_done, score_done, max_done, maxe_done, mb_done, mbsb_done, st_done, sub_done, exp_done, pv_done,
         padd_done, den_done, rd_done, rde_done, rb_done, num_done, o_done, proj_done, osc_done, rope_done, clamp_done,
         q1_done, qsb1_done, score1_done, max1_done, neg1_done, exp1_done, rd1_done, p1_done, pt_done, ptsb_done,
         att1_done, osc1_done,
         xc_done, front_done, rows_done,
         sa_done, sp_done, spm_done, spc_done, su_done, sh_done, ssig_done, spair_done, so_done, sosc_done, sx_done,
         xt_done, xst_done, g_done, ag_done, pg_done, pgm_done, l_done, al_done, pl_done, plc_done, u_done, h_done,
         sig_done, o2_done, os_done, ya_done, yb_done, y_done, comb_done,
         m1_done, hact_done, hrnd_done, m2_done, osc2_done, xrnd_done, xclip_done, xq_done, hq_done, hmax_done,
         ) = loop_sems
        const_in = sem("const_in")
        x_in = sem("x_in")
        aw_in = [sem("aw_in_even"), sem("aw_in_odd")] * 2
        mask_in = sem("mask_in")
        rope_in = sem("rope_in")
        x_out = sem("x_out")
        tanh_done = sem("tanh_done")
        step = sem("dve_step")
        gbo_done, eps_done, rstd_done = sem("gbo_done"), sem("eps_done"), sem("rstd_done")
        pow_done = sem("pow_done")
        k_done, kt_done, v80_done, v80sb_done, vrep_done, kbd_done, vbd_done, mask_done = (
            sem(n) for n in "k_done kt_done v80_done v80sb_done vrep_done kbd_done vbd_done mask_done".split())
        kv1_done, kv1sb_done = sem("kv1_done"), sem("kv1sb_done")

        zero_set, zeros_in = sem("zero_set"), sem("zeros_in")
        shared_in = sem("shared_in")
        w_in = [sem(f"w_in{n}") for n in range(3)]
        out_in = [sem(f"out_in{n}") for n in range(3)]
        smax_sub, smax_exp = sem("route_sub"), sem("route_exp")
        pick_done, rank_done, rank_read, index_done, texp_done = (
            sem(n) for n in "pick_done rank_done rank_read index_done tile_expert_done".split())
        scat_in = sem("scat_in")
        gath_in = [sem(f"gath_in{c}") for c in range(NCH)]

        wq_in, wround_done, wturn_done, wturned_done = (sem(n) for n in "wq_in wround_done wturn_done wturned_done".split())
        tmax_done, allmax_done, xscale_done, hscale_done = (
            sem(n) for n in "tmax_done allmax_done xscale_done hscale_done".split())
        w3_in, sig3_done, comb3_done, combturn_done, combsb_done, comb3_in, combb_in = (
            sem(n) for n in "w3_in sig3_done comb3_done combturn_done combsb_done comb3_in combb_in".split())

        MHA = (0, 2, 3)
        mb16f = [mb16.rearrange("p t e -> p (t e)")[:, 0:NT * n].rearrange("p (t e) -> p t e", e=n) for n in (R0, E1)]
        block = ctx.enter_context(nc.Block())

        def chunk(c):
            return ds(c * CH, CH)

        def over_tiles(eng, n, first, body, last):
            first(0, 0, 0)
            loops = (n - 2) // 3
            with eng.Fori(0, loops) as it:
                for r in range(3):
                    body(3 * it + 1 + r, (1 + r) % 3, it + (1 + r) // 3)
            for t in range(1 + 3 * loops, n - 1):
                body(t, t % 3, t // 3)
            last(n - 1, (n - 1) % 3, (n - 1) // 3)

        def stage_ready(eng, s):
            if s:
                eng.wait_ge(x_done, CREDIT + NCH * s)

        @block.sync
        def _(sp):
            for s_ in loop_sems:
                sp.sem_inc(s_, CREDIT)
            sp.sem_inc(hact_done, 4)
            consts = [(cf[:], d["cf"]), (cb_raw, d["cb"]), (cols[:], d["cols"]), (ctxk[:], d["ctx"]),
                      (gts[:], d["g"].partition_broadcast(P)),
                      (gate_w[:, 0, 0:16], d["gate0"].rearrange("p k e -> p (k e)")),
                      (gate_w[:, 1, :], d["gate1"].rearrange("p k e -> p (k e)")),
                      (gate_w[:, 2, 0:16], d["gate3"].rearrange("p k e -> p (k e)")),
                      (gate_b[:, 0, :], d["gb0"].partition_broadcast(P)), (gate_b[:, 1, :], d["gb3"].partition_broadcast(P))]
            for dst, src in consts:
                sp.dma_start(dst, src).then_inc(const_in, 16)
            sp.dma_start(x[:], d["x"]).then_inc(x_in, 16)
            for l in (0, 1):
                sp.dma_start(aw[l], d[f"aw{l}"]).then_inc(aw_in[l], 16)
                sp.dma_start(bv[l], d[f"bv{l}"]).then_inc(aw_in[l], 16)

            def reload(l):
                sp.wait_ge(x_done, CREDIT + NCH * (2 * (l - 2) + 1))
                sp.dma_start(aw[l], d[f"aw{l}"]).then_inc(aw_in[l], 16)
                sp.dma_start(bv[l], d[f"bv{l}"]).then_inc(aw_in[l], 16)

            def masks(l):
                sp.wait_ge(x_done, CREDIT + NCH * 2 * l)
                sp.dma_start(mtok_raw[l], d[f"mtok{l}"]).then_inc(mask_in, 16)
                sp.dma_start(mkey_raw[l], d[f"mkey{l}"]).then_inc(mask_in, 16)
                if l == 2:
                    sp.dma_start(rope, d["rope"]).then_inc(rope_in, 16)

            def feed_tiles(n, base, load):
                dst = outs1 if base else outs

                def store(t, slot):
                    sp.wait_ge(os_done, CREDIT + base + t + 1)
                    sp.dma_start(dst[ds(t * P, P), :], os_[slot]).then_inc(out_in[slot], 16)

                def both(t, slot):
                    sp.wait_ge(o2_done, CREDIT + base + t - 2)
                    load(t, slot)
                    store(t - 3, slot)

                for t in range(3):
                    load(t, t)
                with sp.Fori(1, n // 3) as it:
                    for r in range(3):
                        both(3 * it + r, r)
                for t in range(3 * (n // 3), n):
                    both(t, t % 3)
                for t in range(n - 3, n):
                    store(t, t % 3)

            if stages > 1:
                sp.wait_ge(zero_set, 1)
                for dst in (disp, disp1):
                    sp.dma_start(dst.rearrange("(n p) d -> p n d", p=P),
                                 zero[:, :].unsqueeze(1).broadcast_to([P, dst.shape[0] // P, D])).then_inc(zeros_in, 16)
                sp.dma_start(w0[2], d["f0w"][R0]).then_inc(shared_in, 16)
                sp.wait_ge(texp_done, 1)
                sp.wait_ge(scat_in, 16 * 2 * NT)

                def load0(t, slot):
                    if isinstance(t, int) and t == 2:
                        sp.wait_ge(sx_done, CREDIT + NCH)
                    e = sp.value_load(tex[0:1, ds(t, 1)], min_val=0, max_val=R0 - 1)
                    sp.dma_start(w0[slot], d["f0w"][ds(e, 1)].rearrange("e p n -> (e p) n")).then_inc(w_in[slot], 16)
                    sp.dma_start(b2row[slot][0:1, :], d["f0b"][ds(e, 1)]).then_inc(w_in[slot], 16)
                    sp.dma_start(xs[slot], disp[ds(t * P, P), :]).then_inc(w_in[slot], 16)

                feed_tiles(TILES0, 0, load0)
            if stages > 3:
                sp.wait_ge(x_done, CREDIT + NCH * 2)
                sp.wait_ge(scat_in, 16 * 3 * NT)

                def load1(t, slot):
                    sp.dma_start(w1m[slot], d["f1w"][ds(t, 1)].rearrange("e p n -> (e p) n")).then_inc(w_in[slot], 16)
                    sp.dma_start(xs[slot], disp1[ds(t * P, P), :]).then_inc(w_in[slot], 16)

                feed_tiles(E1, TILES0, load1)
            if stages > 4:
                reload(2)
                masks(2)
                sp.dma_start(wq_raw[:, 0:2048], d["f2w1"].rearrange("p a b -> p (a b)")).then_inc(wq_in, 16)
                sp.dma_start(wq_raw[:, 2048:4096], d["f2w2"].rearrange("p a b -> p (a b)")).then_inc(wq_in, 16)
            if stages == 5:
                sp.wait_ge(wq_in, 32)
            if stages > 6:
                reload(3)
                masks(3)
            if stages > 7:
                sp.wait_ge(x_done, CREDIT + NCH * 7)
                sp.dma_start(w3, d["f3w"]).then_inc(w3_in, 16)
                sp.wait_ge(combsb_done, 1)
                sp.dma_start(comb3, combT).then_inc(comb3_in, 16)
                sp.wait_ge(comb3_in, 16)
                rows3 = comb3.rearrange("(e c t) p -> e c (t p)", e=8, c=NCH)
                for c in range(NCH):
                    for e in range(8):
                        sp.dma_start(combb[:, e, c * CH:(c + 1) * CH], rows3[e:e + 1, c, :].partition_broadcast(P)
                                     ).then_inc(combb_in, 16)
                    sp.wait_ge(combb_in, 16 * 8 * (c + 1))
            sp.wait_ge(aw_in[1], 32)
            sp.wait_ge(x_done, CREDIT + NCH * stages)
            sp.dma_start(out, x[:]).then_inc(x_out, 16)
            sp.wait_ge(x_out, 16)

        @block.tensor
        def _(pe):
            mm = nc.tensor.matmul

            def layer_norm(s):
                b0 = CREDIT + NCH * s
                stage_ready(pe, s)
                if s == 0:
                    pe.wait_ge(const_in, 16 * 10)
                    pe.wait_ge(x_in, 16)
                if s // 2 in MHA and s % 2 == 0:
                    pe.wait_ge(vbd_done, NB * JG * (1 + MHA.index(s // 2)))
                with pe.Fori(0, NCH) as c:
                    for k in range(KD):
                        last = mm(ps[:, c, :], mean_w, x[:, k, chunk(c)], start=k == 0, stop=k == KD - 1)
                    last.then_inc(mean_done, 1)
                with pe.Fori(0, NCH) as c:
                    pe.wait_ge(sq_done, b0 + c + 1)
                    for t in range(TPC):
                        for k in range(KD):
                            last = mm(ps[:, 4, ds(c * TPC + t, 1)], sq[:, k, t * P:(t + 1) * P], mean_w[:, 0:1],
                                      start=k == 0, stop=k == KD - 1)
                    last.then_inc(var_done, 1)
                pe.wait_ge(rstd_done, s + 1)
                for c in range(NCH):
                    for t in range(TPC):
                        n = c * TPC + t
                        last = mm(ps[:, 4 + c, t * P:(t + 1) * P], stat[:, 1, n:n + 1].broadcast_to([P, P]), ident,
                                  start=True, stop=True)
                    last.then_inc(rstdb_done, 1)

            def kv(l):
                a = MHA.index(l)
                stage_ready(pe, 2 * l)
                if l == 0:
                    pe.wait_ge(const_in, 16 * 10)
                pe.wait_ge(aw_in[l], 32 * (1 + l // 2))
                ks = [(W_K, 0)] + ([(W_KS, 2)] if l == 2 else [])
                for w, bank in ks:
                    for m in range(KD):
                        for k in range(KD):
                            last = mm(ps[:, bank + m, 0:NB * KP], aw[l][:, w, k, m * P:(m + 1) * P], ctxk[:, k, :],
                                      start=k == 0, stop=k == KD - 1)
                last.then_inc(k_done, 1)
                for b in range(NB):
                    for k in range(KD):
                        mm(ps[0:KP, 4 + b, 0:D], ctxk[:, k, b * KP:(b + 1) * KP], aw[l][:, W_V, k, :],
                           start=k == 0, stop=False)
                    last = mm(ps[0:KP, 4 + b, 0:D], ones_row[:, 0:KP], bv[l], start=False, stop=True)
                last.then_inc(v80_done, 1)
                pe.wait_ge(kt_done, a + 1)
                pe.wait_ge(v80sb_done, a + 1)
                for n in range(NB * JG):
                    b, j = divmod(n, JG)
                    bank, half = (6, 7, 4, 5, 0)[n // 2], n % 2
                    mm(ps[:, bank, half * D:(half + 1) * D], cf[0:KP, C_SEL + j * P:C_SEL + (j + 1) * P],
                       v80[0:KP, b, :], start=True, stop=True).then_inc(vrep_done, 1)

            def heads(l):
                a = MHA.index(l)
                rot, masked = l == 2, l != 0
                pe.wait_ge(kbd_done, a + 1)
                if masked:
                    pe.wait_ge(mask_done, a)
                for b in range(NB):
                    with pe.Fori(0, CPB) as cc:
                        i = NCH * a + CPB * b + cc
                        c = CPB * b + cc
                        if b == 0:
                            pe.wait_ge(xn_done, CREDIT + NCH * (2 * l + 1))
                        pe.wait_ge(osc_done, CREDIT + i)
                        for w, bank in [(W_Q, 0)] + ([(W_QS, 2)] if rot else []):
                            for m in range(KD):
                                for k in range(KD):
                                    last = mm(ps[:, bank + m, :], aw[l][:, w, k, m * P:(m + 1) * P], xn[:, k, chunk(c)],
                                              start=k == 0, stop=k == KD - 1)
                        last.then_inc(q_done, 1)
                        pe.wait_ge(qsb_done, CREDIT + i + 1)
                        for n in range(TPC * 4):
                            t, g = divmod(n, 4)
                            pe.wait_ge(max_done, CREDIT + 16 * i + max(n - 3, 0))
                            hf = g // 2
                            keys = kbd[:, hf, b, :, 64 * (g % 2):64 * (g % 2) + 64]
                            last = mm(ps[:, 4 + g, 0:4 * KP], q[:, hf, t * P:(t + 1) * P], keys,
                                      start=True, stop=not masked)
                            if masked:
                                m_ = mtok[:, ds(cc * TPC + t, 1), :].rearrange("p o (j i) -> p (o j) i", i=16)
                                last = mm(ps[:, 4 + g, 0:4 * KP], identb,
                                          m_.unsqueeze(2).broadcast_to([P, JG, 4, 16]), start=False, stop=True)
                            last.then_inc(score_done, 1)
                        pe.wait_ge(maxe_done, CREDIT + i + 1)
                        for hf in range(KD):
                            for t in range(TPC):
                                last = mm(ps[:, hf, t * P:(t + 1) * P], smaxe[:, t, hf * P:(hf + 1) * P], ident,
                                          start=True, stop=True)
                        last.then_inc(mb_done, 1)

                        def scores(n):
                            hf, j = divmod(n, JG)
                            pe.wait_ge(sub_done, CREDIT + 10 * i + max(n - 1, 0))
                            last = mm(ps[:, 2 + n % 2, :], kbd[:, hf, b, j, :], q[:, hf, :], start=True, stop=not masked)
                            if masked:
                                last = mm(ps[:, 2 + n % 2, :], cb[0:KP, B_SEL + j * P:B_SEL + (j + 1) * P],
                                          mkey[:, ds(cc * CH, CH)], start=False, stop=True)
                            last.then_inc(st_done, 1)

                        scores(0)
                        for n in range(2 * JG):
                            if n + 1 < 2 * JG:
                                scores(n + 1)
                            hf, j = divmod(n, JG)
                            pe.wait_ge(exp_done, CREDIT + 10 * i + n + 1)
                            mm(ps[:, 4 + hf, :], vbd[:, b, j, hf * P:(hf + 1) * P], pr[:, j, :],
                               start=j == 0, stop=j == JG - 1).then_inc(pv_done, 1)
                        pe.wait_ge(padd_done, CREDIT + 8 * i + 8)
                        for t in range(TPC):
                            for hf in range(KD):
                                last = mm(ps[:, 6, t * 16 + hf * HH:t * 16 + (hf + 1) * HH],
                                          psum_[:, hf, t * P:(t + 1) * P], blk, start=True, stop=True)
                        last.then_inc(den_done, 1)
                        pe.wait_ge(rde_done, CREDIT + i + 1)
                        for hf in range(KD):
                            for t in range(TPC):
                                last = mm(ps[:, (7, 2)[hf], t * P:(t + 1) * P], rde[:, t, hf * P:(hf + 1) * P], ident,
                                          start=True, stop=True)
                        last.then_inc(rb_done, 1)
                        pe.wait_ge(o_done, CREDIT + i + 1)
                        for m in range(KD):
                            for k in range(KD):
                                last = mm(ps[:, m, :], aw[l][:, W_O, k, m * P:(m + 1) * P], o[:, k, :],
                                          start=k == 0, stop=k == KD - 1)
                        last.then_inc(proj_done, 1)

            def kv_single():
                stage_ready(pe, 2)
                pe.wait_ge(aw_in[1], 32)
                for m in range(KD):
                    for k in range(KD):
                        last = mm(ps[:, m, 0:NB * KP], aw[1][:, W_K, k, m * P:(m + 1) * P], ctxk[:, k, :],
                                  start=k == 0, stop=k == KD - 1)
                for b in range(NB):
                    for k in range(KD):
                        mm(ps[0:KP, 4 + b, 0:D], ctxk[:, k, b * KP:(b + 1) * KP], aw[1][:, W_V, k, :],
                           start=k == 0, stop=False)
                    last = mm(ps[0:KP, 4 + b, 0:D], ones_row[:, 0:KP], bv[1], start=False, stop=True)
                last.then_inc(kv1_done, 1)
                pe.wait_ge(kv1sb_done, 2)

            def single():
                pe.wait_ge(xn_done, CREDIT + NCH * 3)
                for b in range(NB):
                    with pe.Fori(0, CPB) as cc:
                        i = CPB * b + cc
                        pe.wait_ge(qsb1_done, CREDIT + i)
                        for m in range(KD):
                            for k in range(KD):
                                last = mm(ps[:, m, :], aw[1][:, W_Q, k, m * P:(m + 1) * P], xn[:, k, chunk(i)],
                                          start=k == 0, stop=k == KD - 1)
                        last.then_inc(q1_done, 1)
                        pe.wait_ge(qsb1_done, CREDIT + i + 1)
                        pe.wait_ge(exp1_done, CREDIT + i)
                        for t in range(TPC):
                            for k in range(KD):
                                last = mm(ps[:, 2, t * KP:t * KP + KEYS], q[:, k, t * P:(t + 1) * P],
                                          kt[:, k, b * KP:b * KP + KEYS], start=k == 0, stop=k == KD - 1)
                        last.then_inc(score1_done, 1)
                        pe.wait_ge(p1_done, CREDIT + i + 1)
                        for t in range(TPC):
                            last = nc.tensor.transpose(ps[0:KEYS, 3, t * P:(t + 1) * P], p1[:, t, 0:KEYS], ident)
                        last.then_inc(pt_done, 1)
                        pe.wait_ge(ptsb_done, CREDIT + i + 1)
                        pe.wait_ge(osc1_done, CREDIT + i)
                        for m in range(KD):
                            last = mm(ps[:, 4 + m, :], v80[0:KEYS, b, m * P:(m + 1) * P], pt[0:KEYS, :],
                                      start=True, stop=True)
                        last.then_inc(att1_done, 1)

            def front(f, n_exp, with_rows):
                w = gate_w[:, f, 0:KD * n_exp].rearrange("p (k e) -> p k e", k=KD)
                with pe.Fori(0, NCH) as c:
                    pe.wait_ge(xc_done, CREDIT + NCH * f + c + 1)
                    if with_rows:
                        pe.wait_ge(rows_done, CREDIT + NCH * f + c)
                    for t in range(TPC):
                        for k in range(KD):
                            last = mm(ps[:, 0, ds((c * TPC + t) * n_exp, n_exp)], xc[:, k, t * P:(t + 1) * P], w[:, k, :],
                                      start=k == 0, stop=k == KD - 1)
                        if with_rows:
                            for k in range(KD):
                                last = nc.tensor.transpose(ps[:, 1 + t // 2, (t % 2) * D + k * P:(t % 2) * D + (k + 1) * P],
                                                           xc[:, k, t * P:(t + 1) * P], ident)
                    last.then_inc(front_done, 1)

            def ranks(f, n_exp):
                pe.wait_ge(pick_done, f + 1)
                picks = mb16f[f]
                n = NT * n_exp
                mm(ps[:, 3, 0:n], cb[:, B_TRI:B_TRI + P], picks.rearrange("p t e -> p (t e)"), start=True, stop=False)
                for t in range(NT - 1):
                    mm(ps[:, 3, (t + 1) * n_exp:n].rearrange("p (t e) -> p t e", e=n_exp), cb[:, B_ONE:B_ONE + P],
                       picks[:, t:t + 1, :].broadcast_to([P, NT - 1 - t, n_exp]), start=False, stop=t == NT - 2)
                for t in range(NT):
                    last = mm(ps[:, 4, 0:n_exp], cb[:, B_ONE:B_ONE + P], picks[:, t, :], start=t == 0, stop=t == NT - 1)
                last.then_inc(rank_done, 1)
                pe.wait_ge(rank_read, f + 1)

            def part(w, n, k, m):
                at = (n * KD + k) * I0 + m * P
                return w[:, at:at + P]

            def down0(w, k):
                at = 4 * KD * I0 + k * D
                return w[:, at:at + D]

            def shared0():
                w = w0[2]
                pe.wait_ge(shared_in, 16)
                with pe.Fori(0, NCH) as c:
                    for n in range(2 * IM):
                        m, lin = divmod(n, 2)
                        pe.wait_ge(sp_done, CREDIT + 8 * c + max(n - 1, 0))
                        for w_ in range(2):
                            for k in range(KD):
                                last = mm(ps[:, 2 * lin + w_, :], part(w, 2 * lin + w_, k, m), xn[:, k, chunk(c)],
                                          start=k == 0, stop=k == KD - 1)
                        last.then_inc(spair_done, 1)
                    pe.wait_ge(sh_done, CREDIT + IM * c + IM)
                    pe.wait_ge(sosc_done, CREDIT + c)
                    for m in range(KD):
                        for k in range(IM):
                            last = mm(ps[:, 6 + m, :], down0(w, k)[:, m * P:(m + 1) * P], hs[:, k, :],
                                      start=k == 0, stop=k == IM - 1)
                    last.then_inc(so_done, 1)

            def tile_rows(t, slot, use, uses0, b0):
                pe.wait_ge(w_in[slot], uses0 + (32 if b0 else 48) * (use + 1))
                for k in range(KD):
                    last = nc.tensor.transpose(ps[:, 5, k * P:(k + 1) * P], xs[slot][:, k * P:(k + 1) * P], ident)
                last.then_inc(xt_done, 1)

            def tiles0():
                def up(t, slot, lin):
                    for w_ in range(2):
                        for m in range(IM):
                            for k in range(KD):
                                last = mm(ps[:, 2 * lin + w_, m * P:(m + 1) * P], part(w0[slot], 2 * lin + w_, k, m),
                                          xst[slot][:, k, :], start=k == 0, stop=k == KD - 1)
                    last.then_inc(l_done if lin else g_done, 1)

                def down(t, slot):
                    pe.wait_ge(h_done, CREDIT + t + 1)
                    pe.wait_ge(os_done, CREDIT + t)
                    mm(ps[:, 4, 0:D], ones_row, b2row[slot][0:1, :], start=True, stop=False)
                    for k in range(IM):
                        last = mm(ps[:, 4, 0:D], hh[slot][:, k * P:(k + 1) * P], down0(w0[slot], k),
                                  start=False, stop=k == IM - 1)
                    last.then_inc(o2_done, 1)

                def body(t, slot, use, before=True, after=True):
                    pe.wait_ge(xst_done, CREDIT + t + 1)
                    pe.wait_ge(pg_done, CREDIT + t)
                    up(t, slot, 0)
                    if before:
                        down(t - 1, (slot + 2) % 3)
                    pe.wait_ge(pl_done, CREDIT + t)
                    up(t, slot, 1)
                    if after:
                        tile_rows(t + 1, (slot + 1) % 3, use + (slot == 2), 0, 0)

                tile_rows(0, 0, 0, 0, 0)
                over_tiles(pe, TILES0, lambda t, s_, u: body(t, s_, u, before=False), body,
                           lambda t, s_, u: body(t, s_, u, after=False))
                down(TILES0 - 1, (TILES0 - 1) % 3)

            def tiles1():
                uses0 = 48 * (TILES0 // 3)

                def up(t, slot, half):
                    for m in range(4):
                        for k in range(KD):
                            at = k * F1 + (4 * half + m) * P
                            last = mm(ps[:, 2 * half, m * P:(m + 1) * P], w1m[slot][:, at:at + P], xst[slot][:, k, :],
                                      start=k == 0, stop=k == KD - 1)
                    last.then_inc(l_done if half else g_done, 1)

                def down(t, slot):
                    pe.wait_ge(ag_done, CREDIT + TILES0 + t + 1)
                    pe.wait_ge(pl_done, CREDIT + TILES0 + t + 1)
                    pe.wait_ge(os_done, CREDIT + TILES0 + t)
                    for k in range(F1 // P):
                        last = mm(ps[:, 4, 0:D], hh[slot][:, k * P:(k + 1) * P],
                                  w1m[slot][:, KD * F1 + k * D:KD * F1 + (k + 1) * D], start=k == 0, stop=k == F1 // P - 1)
                    last.then_inc(o2_done, 1)

                def body(t, slot, use, before=True, after=True):
                    pe.wait_ge(xst_done, CREDIT + TILES0 + t + 1)
                    pe.wait_ge(ag_done, CREDIT + TILES0 + t)
                    up(t, slot, 0)
                    if before:
                        down(t - 1, (slot + 2) % 3)
                    pe.wait_ge(pl_done, CREDIT + TILES0 + t)
                    up(t, slot, 1)
                    if after:
                        tile_rows(t + 1, (slot + 1) % 3, use + (slot == 2), uses0, 1)

                tile_rows(0, 0, 0, uses0, 1)
                over_tiles(pe, E1, lambda t, s_, u: body(t, s_, u, before=False), body,
                           lambda t, s_, u: body(t, s_, u, after=False))
                down(E1 - 1, (E1 - 1) % 3)

            def combine(f):
                with pe.Fori(0, NCH) as c:
                    pe.wait_ge(y_done, CREDIT + NCH * f + c + 1)
                    pe.wait_ge(x_done, CREDIT + NCH * (1 + 2 * f) + c)
                    for m in range(KD):
                        for t in range(TPC):
                            last = mm(ps[:, m, t * P:(t + 1) * P], ya[:, t, m * P:(m + 1) * P], ident, start=True, stop=True)
                    last.then_inc(comb_done, 1)

            def turn_weights():
                pe.wait_ge(wround_done, 1)
                for k in range(KD):
                    for m in range(F2 // P):
                        nc.tensor.transpose(ps[:, k, :].bitcast(BF16)[:, m * P:(m + 1) * P],
                                            wq1[:, m, k * P:(k + 1) * P], identb)
                for k in range(F2 // P):
                    for m in range(KD):
                        at = k * D + m * P
                        last = nc.tensor.transpose(ps[:, 2 + at // 1024, :].bitcast(BF16)[:, at % 1024:at % 1024 + P],
                                                   wq2[:, m, k * P:(k + 1) * P], identb)
                last.then_inc(wturn_done, 1)
                pe.wait_ge(wturned_done, 1)

            def quantized():
                with pe.Fori(0, NCH) as c:
                    pe.wait_ge(xq_done, CREDIT + c + 1)
                    for m in range(F2 // P):
                        if m % 4 == 0:
                            pe.wait_ge(hact_done, CREDIT + 8 * c + m)
                        for k in range(KD):
                            last = mm(ps[:, m, :], wt1q[:, k, m * P:(m + 1) * P], xq[:, k, chunk(c)],
                                      start=k == 0, stop=k == KD - 1)
                        last.then_inc(m1_done, 1)
                pe.wait_ge(hact_done, CREDIT + 4 + 8 * NCH)
                with pe.Fori(0, NCH) as c:
                    pe.wait_ge(hq_done, CREDIT + c + 1)
                    pe.wait_ge(osc2_done, CREDIT + c)
                    for m in range(KD):
                        for k in range(F2 // P):
                            last = mm(ps[:, m, :], wt2q[:, k, m * P:(m + 1) * P], hq[:, k, chunk(c)],
                                      start=k == 0, stop=k == F2 // P - 1)
                    last.then_inc(m2_done, 1)

            def experts3():
                pe.wait_ge(comb3_done, 1)
                nc.tensor.transpose(ps[:, 1, 0:P], combt.rearrange("p e t -> p (e t)"), ident).then_inc(combturn_done, 1)
                pe.wait_ge(w3_in, 16)
                pe.wait_ge(combsb_done, 1)
                with pe.Fori(0, NCH) as c:
                    def up(n):
                        pe.wait_ge(su_done, CREDIT + IM * NCH + E3 * c + max(n - 1, 0))
                        for w_ in range(2):
                            for k in range(KD):
                                last = mm(ps[:, 2 * (n % 2) + w_, :], w3[:, ORDER3[n], (w_ * KD + k) * P:(w_ * KD + k + 1) * P],
                                          xn[:, k, chunk(c)], start=k == 0, stop=k == KD - 1)
                        last.then_inc(spair_done, 1)

                    up(0)
                    for n in range(E3):
                        if n + 1 < E3:
                            up(n + 1)
                        pe.wait_ge(sh_done, CREDIT + IM * NCH + E3 * c + n + 1)
                        if n == 0:
                            pe.wait_ge(x_done, CREDIT + NCH * 7 + c)
                        for m in range(KD):
                            last = mm(ps[:, 4 + m, :], w3[:, ORDER3[n], 2 * D + m * P:2 * D + (m + 1) * P], h3[:, n % 2, :],
                                      start=n == 0, stop=n == E3 - 1)
                        last.then_inc(so_done, 1)

            pe.wait_ge(tanh_done, 1)
            for s in range(stages):
                l = s // 2
                if s % 2 == 0 and l in MHA:
                    kv(l)
                if s == 2:
                    kv_single()
                if s == 5:
                    turn_weights()
                layer_norm(s)
                if s % 2 == 0 and l in MHA:
                    heads(l)
                if s == 2:
                    single()
                if s == 5:
                    quantized()
                if s == 7:
                    pe.wait_ge(xn_done, CREDIT + NCH * 8)
                    front(2, 8, False)
                    experts3()
                if s == 1:
                    pe.wait_ge(xn_done, CREDIT + NCH * 2)
                    front(0, R0, True)
                    ranks(0, R0)
                    shared0()
                    tiles0()
                    combine(0)
                if s == 3:
                    pe.wait_ge(xn_done, CREDIT + NCH * 4)
                    front(1, E1, True)
                    ranks(1, E1)
                    tiles1()
                    combine(1)

        @block.scalar
        def _(act):
            A = nc.scalar.activation

            def layer_norm(s):
                b0 = CREDIT + NCH * s
                with act.Fori(0, NCH) as c:
                    act.wait_ge(cent_done, b0 + c + 1)
                    act.wait_ge(var_done, b0 + c)
                    A(sq[:, :, :], xn[:, :, chunk(c)], ACT.Square).then_inc(sq_done, 1)

            def gated_out(l, banks):
                for m in range(KD):
                    last = A(osc[:, m, :], ps[:, banks + m, :], ACT.Identity, bias=gbo[:, l, m:m + 1],
                             scale=gts[:, l:l + 1])
                last.then_inc(osc_done, 1)

            def heads(l):
                a = MHA.index(l)
                for b in range(NB):
                    with act.Fori(0, CPB) as cc:
                        i = NCH * a + CPB * b + cc
                        if l != 2:
                            act.wait_ge(q_done, CREDIT + i + 1)
                            for m in range(KD):
                                last = A(q[:, m, :], ps[:, m, :], ACT.Identity,
                                         bias=cols[:, V_ATT * l + V_Q + m:V_ATT * l + V_Q + m + 1])
                            last.then_inc(qsb_done, 1)
                        act.wait_ge(mb_done, CREDIT + i + 1)
                        A(mb[:, :, :], ps[:, 0:2, :], ACT.Copy).then_inc(mbsb_done, 1)
                        for n in range(2 * JG):
                            act.wait_ge(sub_done, CREDIT + 10 * i + n + 1)
                            act.wait_ge(pv_done, CREDIT + 10 * i + max(n - JG + 1, 0))
                            act.wait_ge(padd_done, CREDIT + 8 * i + (0 if n < JG else max(n - JG, 1)))
                            bias = cf[:, C_PAD:C_PAD + 1] if n % JG == JG - 1 else 0.0
                            A(pr[:, n % JG, :], dif[:, n % 2, :], ACT.Exp, bias=bias).then_inc(exp_done, 1)
                        act.wait_ge(pv_done, CREDIT + 10 * i + 10)
                        A(num[:, :, :], ps[:, 4:6, :], ACT.Copy).then_inc(num_done, 1)
                        act.wait_ge(rd_done, CREDIT + i + 1)
                        A(rde[:, :, :].rearrange("p t (h i) -> p t h i", i=16),
                          rd[:, :, :].unsqueeze(3).broadcast_to([P, TPC, 2 * HH, 16]), ACT.Copy).then_inc(rde_done, 1)
                        act.wait_ge(proj_done, CREDIT + i + 1)
                        act.wait_ge(x_done, CREDIT + NCH * 2 * l + CPB * b + cc)
                        gated_out(l, 0)

            def single():
                for b in range(NB):
                    with act.Fori(0, CPB) as cc:
                        i = CPB * b + cc
                        act.wait_ge(q1_done, CREDIT + i + 1)
                        for m in range(KD):
                            last = A(q[:, m, :], ps[:, m, :], ACT.Identity,
                                     bias=cols[:, V_ATT + V_Q + m:V_ATT + V_Q + m + 1])
                        last.then_inc(qsb1_done, 1)
                        act.wait_ge(neg1_done, CREDIT + i + 1)
                        act.wait_ge(pt_done, CREDIT + i)
                        for t in range(TPC):
                            last = A(p1[:, t, 0:KEYS], ps[:, 2, t * KP:t * KP + KEYS], ACT.Exp, bias=neg4[:, 0, t:t + 1],
                                     scale=1.0 / 16, accum_out=neg4[:, 1, t:t + 1])
                        last.then_inc(exp1_done, 1)
                        act.wait_ge(pt_done, CREDIT + i + 1)
                        A(pt[0:KEYS, :], ps[0:KEYS, 3, :], ACT.Copy).then_inc(ptsb_done, 1)
                        act.wait_ge(att1_done, CREDIT + i + 1)
                        act.wait_ge(x_done, CREDIT + NCH * 2 + i)
                        for m in range(KD):
                            last = A(osc[:, m, :], ps[:, 4 + m, :], ACT.Copy, scale=gts[:, 1:2])
                        last.then_inc(osc1_done, 1)

            def front(s, f, with_rows):
                with act.Fori(0, NCH) as c:
                    act.wait_ge(xn_done, CREDIT + NCH * s + c + 1)
                    act.wait_ge(front_done, CREDIT + NCH * f + c)
                    A(xc[:, :, :], xn[:, :, chunk(c)], ACT.Copy).then_inc(xc_done, 1)
                    if with_rows:
                        act.wait_ge(front_done, CREDIT + NCH * f + c + 1)
                        A(rows_[:, ds(c * TPC, TPC), :].rearrange("p t n -> p (t n)"),
                          ps[:, 1:3, :].rearrange("p b n -> p (b n)"), ACT.Copy).then_inc(rows_done, 1)

            def shared0():
                with act.Fori(0, NCH) as c:
                    for n in range(2 * IM):
                        m, lin = divmod(n, 2)
                        at = V_F0 + 2 * IM * lin + m
                        act.wait_ge(spair_done, CREDIT + 8 * c + n + 1)
                        A((al if lin else ag), ps[:, 2 * lin, :], ACT.Identity, bias=cols[:, at:at + 1]).then_inc(sa_done, 1)
                        if not lin:
                            act.wait_ge(spm_done, CREDIT + IM * c + m + 1)
                            act.wait_ge(sh_done, CREDIT + IM * c + m)
                            A(sig, pg, ACT.Sigmoid, scale=1.702).then_inc(ssig_done, 1)
                    act.wait_ge(so_done, CREDIT + c + 1)
                    act.wait_ge(sx_done, CREDIT + c)
                    for m in range(KD):
                        last = A(osc[:, m, :], ps[:, 6 + m, :], ACT.Identity, bias=gbo[:, 1, m:m + 1], scale=gts[:, 4:5])
                    last.then_inc(sosc_done, 1)

            def tile_rows(t, slot):
                act.wait_ge(xt_done, CREDIT + t + 1)
                A(xst[slot].rearrange("p k n -> p (k n)"), ps[:, 5, 0:KD * P], ACT.Copy).then_inc(xst_done, 1)

            def tiles0():
                def biased(dst, slot, lin, done, made):
                    act.wait_ge(done, made)
                    for m in range(IM):
                        at = W0 + 2 * IM * lin + m
                        last = A(dst[:, m * P:(m + 1) * P], ps[:, 2 * lin, m * P:(m + 1) * P], ACT.Identity,
                                 bias=w0[slot][:, at:at + 1])
                    last.then_inc(al_done if lin else ag_done, 1)

                def out(t, slot, use):
                    act.wait_ge(o2_done, CREDIT + t + 1)
                    if not (isinstance(use, int) and use == 0):
                        act.wait_ge(out_in[slot], 16 * use)
                    A(os_[slot], ps[:, 4, 0:D], ACT.Copy).then_inc(os_done, 1)

                def body(t, slot, use, before=True, after=True):
                    biased(ag, slot, 0, g_done, CREDIT + t + 1)
                    act.wait_ge(pgm_done, CREDIT + t + 1)
                    A(sig, pg, ACT.Sigmoid, scale=1.702).then_inc(sig_done, 1)
                    if before:
                        out(t - 1, (slot + 2) % 3, use - (slot == 0))
                    biased(al, slot, 1, l_done, CREDIT + t + 1)
                    if after:
                        tile_rows(t + 1, (slot + 1) % 3)

                tile_rows(0, 0)
                over_tiles(act, TILES0, lambda t, s_, u: body(t, s_, u, before=False), body,
                           lambda t, s_, u: body(t, s_, u, after=False))
                out(TILES0 - 1, (TILES0 - 1) % 3, (TILES0 - 1) // 3)

            def tiles1():
                def out(t, slot, use):
                    act.wait_ge(o2_done, CREDIT + TILES0 + t + 1)
                    act.wait_ge(out_in[slot], 16 * (TILES0 // 3 + use))
                    A(os_[slot], ps[:, 4, 0:D], ACT.Copy).then_inc(os_done, 1)

                def body(t, slot, use, before=True, after=True):
                    act.wait_ge(g_done, CREDIT + TILES0 + t + 1)
                    A(hh[slot][:, 0:CH], ps[:, 0, :], ACT.Relu).then_inc(ag_done, 1)
                    if before:
                        out(t - 1, (slot + 2) % 3, use - (slot == 0))
                    if after:
                        tile_rows(TILES0 + t + 1, (slot + 1) % 3)

                tile_rows(TILES0, 0)
                over_tiles(act, E1, lambda t, s_, u: body(t, s_, u, before=False), body,
                           lambda t, s_, u: body(t, s_, u, after=False))
                out(E1 - 1, (E1 - 1) % 3, (E1 - 1) // 3)

            def quantized():
                magic = cf[:, C_MAGIC:C_MAGIC + 1]
                act.wait_ge(xscale_done, 1)
                with act.Fori(0, NCH) as c:
                    A(xn[:, :, chunk(c)], xn[:, :, chunk(c)], ACT.Identity, bias=magic, scale=qv[:, 3:4]).then_inc(xrnd_done, 1)
                with act.Fori(0, NCH) as c:
                    for m in range(F2 // P):
                        act.wait_ge(m1_done, CREDIT + 8 * c + m + 1)
                        A(hbig[:, m, chunk(c)], ps[:, m, :], ACT.Relu, bias=qs[:, 4, m:m + 1], scale=qs[:, 2, m:m + 1]
                          ).then_inc(hact_done, 1)
                act.wait_ge(hscale_done, 1)
                with act.Fori(0, NCH) as c:
                    A(hbig[:, :, chunk(c)], hbig[:, :, chunk(c)], ACT.Identity, bias=magic, scale=qv[:, 7:8]).then_inc(hrnd_done, 1)
                with act.Fori(0, NCH) as c:
                    act.wait_ge(m2_done, CREDIT + c + 1)
                    act.wait_ge(x_done, CREDIT + NCH * 5 + c)
                    for m in range(KD):
                        last = A(osc[:, m, :], ps[:, m, :], ACT.Identity, bias=qs[:, 7, 2 + m:3 + m], scale=qs[:, 7, m:m + 1])
                    last.then_inc(osc2_done, 1)

            def experts3():
                act.wait_ge(front_done, CREDIT + NCH * 3)
                A(lg3[1].rearrange("p t e -> p (t e)"), ps[:, 0, 0:NT * 8], ACT.Sigmoid).then_inc(sig3_done, 1)
                act.wait_ge(combturn_done, 1)
                A(combT, ps[:, 1, 0:P], ACT.Copy).then_inc(combsb_done, 1)
                with act.Fori(0, NCH) as c:
                    for n in range(E3):
                        act.wait_ge(spair_done, CREDIT + 8 * NCH + E3 * c + n + 1)
                        A(sg3[:, n % 2, :], ps[:, 2 * (n % 2), :], ACT.Sigmoid).then_inc(ssig_done, 1)

            def route_exp(f, n_exp):
                act.wait_ge(smax_sub, f + 1)
                A(ra[1][:, 0:NT * n_exp], ra[0][:, 0:NT * n_exp], ACT.Exp).then_inc(smax_exp, 1)

            act.wait_ge(const_in, 16 * 10)
            A(gts[:, :], gts[:, :], ACT.Tanh).then_inc(tanh_done, 1)
            act.wait_ge(gbo_done, 1)
            for s in range(stages):
                l = s // 2
                if s % 2 == 0 and l in MHA:
                    act.wait_ge(v80_done, MHA.index(l) + 1)
                    A(v80[0:KP, :, :], ps[0:KP, 4:6, 0:D], ACT.Copy).then_inc(v80sb_done, 1)
                if s == 5:
                    act.wait_ge(wturn_done, 1)
                    A(wt1q.rearrange("p k n -> p (k n)"), ps[:, 0:2, :].rearrange("p b n -> p (b n)").bitcast(BF16), ACT.Copy)
                    A(wt2q.rearrange("p k n -> p (k n)"), ps[:, 2:4, :].rearrange("p b n -> p (b n)").bitcast(BF16), ACT.Copy
                      ).then_inc(wturned_done, 1)
                if s == 2:
                    act.wait_ge(kv1_done, 1)
                    A(v80[0:KP, :, :], ps[0:KP, 4:6, 0:D], ACT.Copy).then_inc(kv1sb_done, 1)
                layer_norm(s)
                if s == 2:
                    single()
                if s % 2 == 0 and l in MHA:
                    heads(l)
                if s == 5:
                    quantized()
                if s == 7:
                    front(7, 2, False)
                    experts3()
                if s == 1:
                    front(1, 0, True)
                    route_exp(0, R0)
                    shared0()
                    tiles0()
                if s == 3:
                    front(3, 1, True)
                    route_exp(1, E1)
                    tiles1()

        @block.gpsimd
        def _(pool):
            def heads(l):
                a = MHA.index(l)
                for b in range(NB):
                    with pool.Fori(0, CPB) as cc:
                        i = NCH * a + CPB * b + cc
                        for hf in range(KD):
                            for j in range(1, JG):
                                pool.wait_ge(exp_done, CREDIT + 10 * i + JG * hf + j + 1)
                                n = 4 * hf + j - 1
                                pool.wait_ge(padd_done, CREDIT + 8 * i + n)
                                if hf == 0 and j == 1:
                                    pool.wait_ge(den_done, CREDIT + i)
                                nc.gpsimd.tensor_tensor(psum_[:, hf, :], pr[:, j, :],
                                                        pr[:, 0, :] if j == 1 else psum_[:, hf, :],
                                                        ALU.add).then_inc(padd_done, 1)

            def scatter(dst, index, rest):
                for t in range(NT):
                    nc.gpsimd.indirect_dma_start(dst, bass.IndirectOffsetOnAxis(index[:, t:t + 1], 0), rows_[:, t, :], None
                                                 ).then_inc(scat_in, 16)

            def gather(dst, src, index, c):
                for t in range(c * TPC, (c + 1) * TPC):
                    nc.gpsimd.indirect_dma_start(dst[:, t, :], None, src, bass.IndirectOffsetOnAxis(index[:, t:t + 1], 0)
                                                 ).then_inc(gath_in[c], 16)

            nc.gpsimd.memset(zero[:, :], 0.0).then_inc(zero_set, 1)
            for s in range(stages):
                l = s // 2
                pool.wait_ge(eps_done, s + 1)
                nc.gpsimd.tensor_tensor(stat[:, 1, :], stat[:, 0, :], cf[:, C_MHALF:C_MHALF + NT],
                                        ALU.pow).then_inc(pow_done, 1)
                if s % 2 == 0 and l in MHA:
                    heads(l)
                if s == 5:
                    for n in range(2):
                        pool.wait_ge(tmax_done, n + 1)
                        nc.gpsimd.partition_all_reduce(qv[:, 1 + 4 * n:2 + 4 * n], qv[:, 4 * n:1 + 4 * n], P, RMAX
                                                       ).then_inc(allmax_done, 1)
                if s == 1:
                    pool.wait_ge(zeros_in, 32)
                    pool.wait_ge(rows_done, CREDIT + NCH)
                    pool.wait_ge(index_done, 1)
                    scatter(disp, gix1, 0)
                    scatter(disp, gix2, 0)
                    pool.wait_ge(scat_in, 16 * 2 * NT)
                    for n in range(3):
                        pool.wait_ge(out_in[n], 16 * (TILES0 // 3))
                    for c in range(NCH):
                        gather(ga, outs, gix1, c)
                        gather(gb, outs, gix2, c)
                if s == 3:
                    pool.wait_ge(rows_done, CREDIT + NCH * 2)
                    pool.wait_ge(index_done, 2)
                    scatter(disp1, six, 0)
                    pool.wait_ge(scat_in, 16 * 3 * NT)
                    for n in range(3):
                        pool.wait_ge(out_in[n], 16 * (TILES0 // 3 + (E1 + 2 - n) // 3))
                    for c in range(NCH):
                        gather(ga, outs1, gix1, c)

        @block.vector
        def _(dve):
            V = nc.vector
            count = [0]

            def link(ins):
                count[0] += 1
                ins.then_inc(step, 1)
                dve.wait_ge(step, count[0])

            def layer_norm(s):
                b0 = CREDIT + NCH * s
                with dve.Fori(0, NCH) as c:
                    dve.wait_ge(mean_done, b0 + c + 1)
                    V.tensor_tensor(xn[:, :, chunk(c)], x[:, :, chunk(c)],
                                    ps[:, ds(c, 1), :].broadcast_to([P, KD, CH]), ALU.subtract).then_inc(cent_done, 1)
                dve.wait_ge(var_done, b0 + NCH)
                V.tensor_scalar(stat[:, 0, :], ps[:, 4, 0:NT], EPS, None, ALU.add).then_inc(eps_done, 1)
                dve.wait_ge(pow_done, s + 1)
                link(V.tensor_tensor(stat[:, 2, :], stat[:, 1, :], stat[:, 1, :], ALU.mult))
                link(V.tensor_tensor(stat[:, 3, :], stat[:, 2, :], stat[:, 0, :], ALU.mult))
                link(V.tensor_scalar(stat[:, 2, :], stat[:, 3, :], -0.5, 1.5, ALU.mult, ALU.add))
                V.tensor_tensor(stat[:, 1, :], stat[:, 1, :], stat[:, 2, :], ALU.mult).then_inc(rstd_done, 1)
                with dve.Fori(0, NCH) as c:
                    dve.wait_ge(rstdb_done, b0 + c + 1)
                    V.tensor_tensor(xn[:, :, chunk(c)], xn[:, :, chunk(c)],
                                    ps[:, ds(c + 4, 1), :].broadcast_to([P, KD, CH]), ALU.mult).then_inc(xn_done, 1)

            def kv(l):
                a = MHA.index(l)
                v0 = V_ATT * l
                if l != 0:
                    dve.wait_ge(mask_in, 32 * (l - 1))
                    how = (NEG, None, ALU.mult) if l == 2 else (0.0, NEG, ALU.is_equal, ALU.mult)
                    V.tensor_scalar(mtok[:, :, :], mtok_raw[l], *how)
                    V.tensor_scalar(mkey[0:KP, :], mkey_raw[l], *how).then_inc(mask_done, 1)
                if l == 2:
                    dve.wait_ge(rope_in, 16)
                dve.wait_ge(k_done, a + 1)
                for m in range(KD):
                    if l == 2:
                        r = [rt[:, n, 0:NB * KP].rearrange("p (b k) -> p b k", b=NB) for n in range(2)]
                        for n, w in enumerate((V_K, V_KS)):
                            link(V.tensor_scalar(r[n], ps[:, 2 * n + m, 0:NB * KP].rearrange("p (b k) -> p b k", b=NB),
                                                 cols[:, v0 + w + m:v0 + w + m + 1], None, ALU.add))
                            link(V.tensor_tensor(r[n], r[n], rope[:, n:n + 1, 0:KP].broadcast_to([P, NB, KP]), ALU.mult))
                        link(V.tensor_tensor(kt[:, m, :], rt[:, 0, 0:NB * KP], rt[:, 1, 0:NB * KP], ALU.add))
                    else:
                        link(V.tensor_scalar(kt[:, m, :], ps[:, m, 0:NB * KP], cols[:, v0 + V_K + m:v0 + V_K + m + 1],
                                             0.25, ALU.add, ALU.mult))
                V.sem_inc(kt_done, 1)
                for m in range(KD):
                    for b in range(NB):
                        k_ = kt[:, m, b * KP:(b + 1) * KP].rearrange("p (j i) -> p j i", i=16)
                        last = V.tensor_tensor(kbd[:, m, b, :, :].rearrange("p j (h i) -> p j h i", i=16),
                                               k_.unsqueeze(2).broadcast_to([P, JG, HH, 16]),
                                               blk.unsqueeze(1).unsqueeze(3).broadcast_to([P, JG, HH, 16]), ALU.mult)
                last.then_inc(kbd_done, 1)
                for n in range(NB * JG):
                    b, j = divmod(n, JG)
                    bank, half = (6, 7, 4, 5, 0)[n // 2], n % 2
                    dve.wait_ge(vrep_done, NB * JG * a + n - half + 2)
                    V.tensor_tensor(vbd[:, b, j, :].rearrange("p (m h i) -> p m h i", m=KD, i=16),
                                    ps[:, bank, half * D:(half + 1) * D].rearrange("p (m h i) -> p m h i", m=KD, i=16),
                                    blk.unsqueeze(1).unsqueeze(3).broadcast_to([P, KD, HH, 16]),
                                    ALU.mult).then_inc(vbd_done, 1)

            def heads(l):
                a = MHA.index(l)
                for b in range(NB):
                    with dve.Fori(0, CPB) as cc:
                        i = NCH * a + CPB * b + cc
                        c = CPB * b + cc
                        if l == 2:
                            dve.wait_ge(q_done, CREDIT + i + 1)
                            for m in range(KD):
                                for n, w in enumerate((V_Q, V_QS)):
                                    k_ = V_ATT * l + w + m
                                    if m:
                                        dve.wait_ge(rope_done, CREDIT + 6 * (i - NCH) + 3)
                                    V.scalar_tensor_tensor(rt[:, n, :], ps[:, 2 * n + m, :], cols[:, k_:k_ + 1],
                                                           rope[:, n, ds(cc * CH, CH)], ALU.add, ALU.mult
                                                           ).then_inc(rope_done, 1)
                                dve.wait_ge(rope_done, CREDIT + 6 * (i - NCH) + 3 * m + 2)
                                V.tensor_tensor(q[:, m, :], rt[:, 0, :], rt[:, 1, :], ALU.add).then_inc(rope_done, 1)
                            dve.wait_ge(rope_done, CREDIT + 6 * (i - NCH) + 6)
                            V.sem_inc(qsb_done, 1)
                        for n in range(TPC * 4):
                            t, g = divmod(n, 4)
                            dve.wait_ge(score_done, CREDIT + 16 * i + n + 1)
                            sc = ps[:, 4 + g, 0:4 * KP].rearrange("p (j h i) -> p h j i", j=JG, h=4)
                            V.tensor_reduce(smax[:, t, 4 * g:4 * g + 4], sc, AX.XY, ALU.max).then_inc(max_done, 1)
                        dve.wait_ge(max_done, CREDIT + 16 * i + 16)
                        V.tensor_scalar(smaxe[:, :, :].rearrange("p t (h i) -> p t h i", i=16),
                                        smax[:, :, :].unsqueeze(3).broadcast_to([P, TPC, 2 * HH, 16]), -1e30, None,
                                        ALU.max).then_inc(maxe_done, 1)
                        dve.wait_ge(mbsb_done, CREDIT + i + 1)
                        for n in range(2 * JG):
                            dve.wait_ge(st_done, CREDIT + 10 * i + n + 1)
                            dve.wait_ge(exp_done, CREDIT + 10 * i + max(n - 1, 0))
                            V.tensor_tensor(dif[:, n % 2, :], ps[:, 2 + n % 2, :], mb[:, n // JG, :],
                                            ALU.subtract).then_inc(sub_done, 1)
                        dve.wait_ge(den_done, CREDIT + i + 1)
                        V.tensor_scalar(smax[:, :, :], ps[:, 6, 0:TPC * 16].rearrange("p (t h) -> p t h", t=TPC),
                                        1e-30 if l == 2 else 0.0, None, ALU.max).then_inc(clamp_done, 1)
                        dve.wait_ge(clamp_done, CREDIT + i + 1)
                        V.reciprocal(rd[:, :, :], smax[:, :, :]).then_inc(rd_done, 1)
                        dve.wait_ge(rb_done, CREDIT + i + 1)
                        dve.wait_ge(num_done, CREDIT + i + 1)
                        V.tensor_tensor(o[:, 0, :], num[:, 0, :], ps[:, 7, :], ALU.mult)
                        V.tensor_tensor(o[:, 1, :], num[:, 1, :], ps[:, 2, :], ALU.mult).then_inc(o_done, 1)
                        dve.wait_ge(osc_done, CREDIT + i + 1)
                        add_residual(c)

            def single():
                for b in range(NB):
                    with dve.Fori(0, CPB) as cc:
                        i = CPB * b + cc
                        dve.wait_ge(score1_done, CREDIT + i + 1)
                        sc = ps[:, 2, 0:TPC * KP].rearrange("p (t k) -> p t k", t=TPC)
                        V.tensor_reduce(neg4[:, 2, :], sc[:, :, 0:KEYS], AX.X, ALU.max).then_inc(max1_done, 1)
                        dve.wait_ge(max1_done, CREDIT + i + 1)
                        V.tensor_scalar(neg4[:, 0, :], neg4[:, 2, :], -1.0 / 16, None, ALU.mult).then_inc(neg1_done, 1)
                        dve.wait_ge(exp1_done, CREDIT + i + 1)
                        V.reciprocal(neg4[:, 2, :], neg4[:, 1, :]).then_inc(rd1_done, 1)
                        dve.wait_ge(rd1_done, CREDIT + i + 1)
                        V.tensor_tensor(p1[:, :, 0:KEYS], p1[:, :, 0:KEYS],
                                        neg4[:, 2, :].unsqueeze(2).broadcast_to([P, TPC, KEYS]), ALU.mult).then_inc(p1_done, 1)
                        dve.wait_ge(osc1_done, CREDIT + i + 1)
                        add_residual(i)

            def add_residual(c):
                V.tensor_tensor(x[:, :, chunk(c)], x[:, :, chunk(c)], osc[:, :, :], ALU.add).then_inc(x_done, 1)

            def kv_single():
                dve.wait_ge(kv1_done, 1)
                for m in range(KD):
                    last = V.tensor_scalar(kt[:, m, :], ps[:, m, 0:NB * KP],
                                           cols[:, V_ATT + V_K + m:V_ATT + V_K + m + 1], None, ALU.add)
                last.then_inc(kv1sb_done, 1)

            def wide(v, n):
                return v.unsqueeze(2).broadcast_to([P, v.shape[1], n])

            def top(val, oh, n, t1, t2, m):
                link(V.tensor_reduce(m, val, AX.X, ALU.max))
                link(V.tensor_tensor(t1, val, wide(m, n), ALU.is_equal))
                link(V.tensor_tensor(t2, t1, cf[:, C_TIE:C_TIE + n].unsqueeze(1).broadcast_to([P, NT, n]), ALU.mult))
                link(V.tensor_reduce(m, t2, AX.X, ALU.max))
                link(V.tensor_tensor(oh, t2, wide(m, n), ALU.is_equal))

            def dot(dst, a_, b_, tmp):
                link(V.tensor_tensor(tmp, a_, b_, ALU.mult))
                link(V.tensor_reduce(dst, tmp, AX.X, ALU.add))

            def views(n_exp):
                return [a_[:, 0:NT * n_exp].rearrange("p (t e) -> p t e", e=n_exp) for a_ in ra + [oh1, oh2]]

            def bias_row(v, n):
                return v.unsqueeze(1).broadcast_to([P, NT, n])

            def probabilities(f, n_exp, r):
                logits = ps[:, 0, 0:NT * n_exp].rearrange("p (t e) -> p t e", e=n_exp)
                dve.wait_ge(front_done, CREDIT + NCH * (f + 1))
                link(V.tensor_reduce(rv[0], logits, AX.X, ALU.max))
                V.tensor_tensor(r[0], logits, wide(rv[0], n_exp), ALU.subtract).then_inc(smax_sub, 1)
                dve.wait_ge(smax_exp, f + 1)
                link(V.tensor_reduce(rv[1], r[1], AX.X, ALU.add))
                link(V.reciprocal(rv[1], rv[1]))

            def route0():
                n = R0
                r = views(n)
                o1, o2 = r[6], r[7]
                probabilities(0, n, r)
                link(V.tensor_tensor(r[2], r[1], wide(rv[1], n), ALU.mult))
                link(V.tensor_tensor(r[3], r[2], bias_row(gate_b[:, 0, :], n), ALU.add))
                top(r[3], o1, n, r[4], r[5], rv[2])
                link(V.scalar_tensor_tensor(r[0], o1, NEG, r[3], ALU.mult, ALU.add))
                top(r[0], o2, n, r[4], r[5], rv[2])
                V.tensor_tensor(mb16f[0], o1, o2, ALU.add).then_inc(pick_done, 1)
                for w, o_ in ((wt1, o1), (wt2, o2)):
                    dot(rv[3], r[2], o_, r[4])
                    link(V.tensor_scalar(w, rv[3], gts[:, 4:5], None, ALU.mult))
                dve.wait_ge(rank_done, 1)
                link(V.tensor_copy(e8[0], ps[:, 4, 0:n]))
                link(V.tensor_tensor(cmp8, e8[0].unsqueeze(2).broadcast_to([P, n, 16]),
                                     cf[:, C_STEP:C_STEP + 16].unsqueeze(1).broadcast_to([P, n, 16]), ALU.is_gt))
                link(V.tensor_reduce(e8[1], cmp8, AX.X, ALU.add))
                link(V.tensor_tensor(cmp8[:, :, 0:8], cf[:, C_LT:C_LT + 64].rearrange("p (a b) -> p a b", a=8),
                                     e8[1].unsqueeze(1).broadcast_to([P, 8, 8]), ALU.mult))
                link(V.tensor_reduce(e8[2], cmp8[:, :, 0:8], AX.X, ALU.add))
                link(V.tensor_scalar(e8[3], e8[2], float(P), None, ALU.mult))
                V.tensor_tensor(r[0], ps[:, 3, 0:NT * n].rearrange("p (t e) -> p t e", e=n), bias_row(e8[3], n),
                                ALU.add).then_inc(rank_read, 1)
                dve.wait_ge(rank_read, 1)
                dot(rv[4], r[0], o1, r[4])
                dot(rv[5], r[0], o2, r[4])
                link(V.tensor_copy(gix1, rv[4]))
                V.tensor_copy(gix2, rv[5]).then_inc(index_done, 1)
                link(V.tensor_tensor(e8[0], e8[1], e8[2], ALU.add))
                link(V.tensor_tensor(cmpt, e8[0].unsqueeze(1).broadcast_to([P, TILES0, 8]),
                                     cf[:, C_TILE:C_TILE + TILES0].unsqueeze(2).broadcast_to([P, TILES0, 8]), ALU.is_le))
                link(V.tensor_reduce(texf, cmpt, AX.X, ALU.add))
                V.tensor_scalar(tex, texf, float(R0 - 1), None, ALU.min).then_inc(texp_done, 1)

            def route1():
                n = E1
                r = views(n)
                o1 = r[6]
                probabilities(1, n, r)
                link(V.tensor_scalar(r[2], r[0], 0.0, None, ALU.add))
                top(r[2], o1, n, r[4], r[5], rv[2])
                V.tensor_copy(mb16f[1], o1).then_inc(pick_done, 1)
                dot(rv[3], o1, bias_row(cf[:, C_IDX:C_IDX + n], n), r[4])
                dve.wait_ge(rank_done, 2)
                V.tensor_tensor(r[3], ps[:, 3, 0:NT * n].rearrange("p (t e) -> p t e", e=n), o1, ALU.mult
                                ).then_inc(rank_read, 1)
                dve.wait_ge(rank_read, 2)
                link(V.tensor_reduce(rv[4], r[3], AX.X, ALU.add))
                link(V.tensor_scalar(rv[5], rv[4], float(C1), None, ALU.is_lt))
                link(V.tensor_scalar(rv[4], rv[4], float(C1 - 1), None, ALU.min))
                link(V.scalar_tensor_tensor(rv[6], rv[3], float(C1), rv[4], ALU.mult, ALU.add))
                link(V.tensor_copy(gix1, rv[6]))
                tok = cf[:, C_TOK:C_TOK + NT]
                link(V.tensor_tensor(rv[7], rv[6], tok, ALU.subtract))
                link(V.tensor_tensor(rv[7], rv[7], rv[5], ALU.mult))
                link(V.tensor_tensor(rv[7], rv[7], tok, ALU.add))
                V.tensor_copy(six, rv[7]).then_inc(index_done, 1)
                link(V.tensor_tensor(rv[5], rv[5], rv[1], ALU.mult))
                link(V.tensor_scalar(wt1, rv[5], gts[:, 5:6], None, ALU.mult))

            def round_weights():
                dve.wait_ge(wq_in, 32)
                for i, (dst, n, w) in enumerate(((wq1, F2 // P, D), (wq2, KD, F2))):
                    raw = wq_raw[:, 2048 * i:2048 * (i + 1)].rearrange("p (a b) -> p a b", a=n)
                    sw, inv = qs[:, i, 0:n], qs[:, 3, 0:n]
                    link(V.tensor_reduce(sw, raw, AX.X, ALU.max, apply_absolute_value=True))
                    link(V.tensor_scalar(sw, sw, 1e-8, 1.0 / 127, ALU.max, ALU.mult))
                    link(V.reciprocal(inv, sw))
                    link(V.tensor_tensor(raw, raw, wide(inv, w), ALU.mult))
                    link(V.tensor_scalar(raw, raw, MAGIC, MAGIC, ALU.add, ALU.subtract))
                    link(V.tensor_scalar(dst, raw, 127.0, -128.0, ALU.min, ALU.max))
                V.sem_inc(wround_done, 1)

            def scales(n, width, bias_at, sw, ss, qb):
                dve.wait_ge(allmax_done, n + 1)
                o_ = 4 * n
                link(V.tensor_scalar(qv[:, o_ + 2:o_ + 3], qv[:, o_ + 1:o_ + 2], 1e-8, 1.0 / 255, ALU.max, ALU.mult))
                link(V.reciprocal(qv[:, o_ + 3:o_ + 4], qv[:, o_ + 2:o_ + 3]))
                inv = qs[:, 3, 0:width]
                link(V.tensor_scalar(ss, sw, qv[:, o_ + 2:o_ + 3], None, ALU.mult))
                link(V.reciprocal(inv, ss))
                link(V.tensor_tensor(inv, inv, cols[:, bias_at:bias_at + width], ALU.mult))
                link(V.tensor_scalar(inv, inv, MAGIC, MAGIC, ALU.add, ALU.subtract))
                link(V.tensor_tensor(qb, inv, ss, ALU.mult))

            def quantized():
                dve.wait_ge(xn_done, CREDIT + NCH * 6)
                V.tensor_reduce(qv[:, 0:1], xn[:, :, :], AX.XY, ALU.max).then_inc(tmax_done, 1)
                scales(0, F2 // P, V_F2, qs[:, 0, :], qs[:, 2, :], qs[:, 4, :])
                V.sem_inc(xscale_done, 1)
                with dve.Fori(0, NCH) as c:
                    dve.wait_ge(xrnd_done, CREDIT + c + 1)
                    V.tensor_scalar(xn[:, :, chunk(c)], xn[:, :, chunk(c)], MAGIC, MAGIC + 255, ALU.max, ALU.min
                                    ).then_inc(xclip_done, 1)
                    dve.wait_ge(xclip_done, CREDIT + c + 1)
                    V.tensor_scalar(xq[:, :, chunk(c)], xn[:, :, chunk(c)], MAGIC, None, ALU.subtract).then_inc(xq_done, 1)
                with dve.Fori(0, NCH) as c:
                    dve.wait_ge(hact_done, CREDIT + 4 + 8 * c + 8)
                    last = V.tensor_reduce(qs[:, 5, ds(c, 1)], hbig[:, :, chunk(c)], AX.XY, ALU.max).then_inc(hmax_done, 1)
                dve.wait_ge(hmax_done, CREDIT + NCH)
                V.tensor_reduce(qv[:, 4:5], qs[:, 5, 0:NCH], AX.X, ALU.max).then_inc(tmax_done, 1)
                scales(1, KD, V_F2 + F2 // P, qs[:, 1, 0:KD], qs[:, 6, 0:KD], qs[:, 6, KD:2 * KD])
                link(V.tensor_scalar(qs[:, 7, 0:2 * KD], qs[:, 6, 0:2 * KD], gts[:, 6:7], None, ALU.mult))
                V.sem_inc(hscale_done, 1)
                with dve.Fori(0, NCH) as c:
                    dve.wait_ge(hrnd_done, CREDIT + c + 1)
                    V.tensor_scalar(hq[:, :, chunk(c)], hbig[:, :, chunk(c)], MAGIC, 255.0, ALU.subtract, ALU.min
                                    ).then_inc(hq_done, 1)
                with dve.Fori(0, NCH) as c:
                    dve.wait_ge(osc2_done, CREDIT + c + 1)
                    add_residual(c)

            def route3():
                n, half = 8, 4
                sf, tmp, o1, rest, o2, ta, tb = lg3[2], lg3[3], lg3[4], lg3[5], lg3[6], lg3[7], lg3[0]
                dve.wait_ge(sig3_done, 1)
                link(V.tensor_tensor(sf, lg3[1], bias_row(gate_b[:, 1, :], n), ALU.add))
                pairs = sf.rearrange("p t (g i) -> p (t g) i", i=2)
                link(V.tensor_reduce(gr[0].rearrange("p t g -> p (t g)"), pairs, AX.X, ALU.add))
                top(gr[0], gr[1], half, gr[5], gr[6], rv3[0])
                link(V.scalar_tensor_tensor(gr[2], gr[1], NEG, gr[0], ALU.mult, ALU.add))
                top(gr[2], gr[3], half, gr[5], gr[6], rv3[0])
                link(V.tensor_tensor(gr[4], gr[1], gr[3], ALU.add))
                link(V.tensor_tensor(tmp.rearrange("p t (g i) -> p (t g) i", i=2), pairs,
                                     wide(gr[4].rearrange("p t g -> p (t g)"), 2), ALU.mult))
                top(tmp, o1, n, ta, tb, rv3[0])
                link(V.scalar_tensor_tensor(rest, o1, NEG, tmp, ALU.mult, ALU.add))
                top(rest, o2, n, ta, tb, rv3[0])
                dot(rv3[1], sf, o1, ta)
                dot(rv3[2], sf, o2, ta)
                link(V.tensor_tensor(rv3[3], rv3[1], rv3[2], ALU.add))
                link(V.tensor_scalar(rv3[3], rv3[3], 1e-20, None, ALU.add))
                link(V.reciprocal(rv3[4], rv3[3]))
                link(V.tensor_scalar(rv3[4], rv3[4], 2.5, gts[:, 7:8], ALU.mult, ALU.mult))
                link(V.tensor_tensor(rv3[1], rv3[1], rv3[4], ALU.mult))
                link(V.tensor_tensor(rv3[2], rv3[2], rv3[4], ALU.mult))
                link(V.tensor_tensor(ta, o1, wide(rv3[1], n), ALU.mult))
                link(V.tensor_tensor(tb, o2, wide(rv3[2], n), ALU.mult))
                V.tensor_tensor(combt.rearrange("p e t -> p t e"), ta, tb, ALU.add).then_inc(comb3_done, 1)

            def experts3():
                with dve.Fori(0, NCH) as c:
                    for n in range(E3):
                        i = E3 * c + n
                        e = ORDER3[n]
                        dve.wait_ge(ssig_done, CREDIT + IM * NCH + i + 1)
                        V.tensor_tensor(t3, sg3[:, n % 2, :], ps[:, 2 * (n % 2), :], ALU.mult).then_inc(spc_done, 1)
                        dve.wait_ge(spc_done, CREDIT + IM * NCH + i + 1)
                        V.tensor_tensor(u3, t3, ps[:, 2 * (n % 2) + 1, :], ALU.mult).then_inc(su_done, 1)
                        dve.wait_ge(su_done, CREDIT + IM * NCH + i + 1)
                        dve.wait_ge(so_done, CREDIT + NCH + E3 * c + max(n - 1, 0))
                        if e == 0:
                            dve.wait_ge(combb_in, 16 * 8 * (c + 1))
                        if e < 8:
                            V.tensor_tensor(h3[:, n % 2, :], u3, combb[:, e, chunk(c)], ALU.mult).then_inc(sh_done, 1)
                        else:
                            V.tensor_scalar(h3[:, n % 2, :], u3, gts[:, 7:8], None, ALU.mult).then_inc(sh_done, 1)
                    dve.wait_ge(so_done, CREDIT + NCH + E3 * c + E3)
                    V.tensor_tensor(x[:, :, chunk(c)], x[:, :, chunk(c)], ps[:, 4:6, :], ALU.add).then_inc(x_done, 1)

            def shared0():
                with dve.Fori(0, NCH) as c:
                    for n in range(2 * IM):
                        m, lin = divmod(n, 2)
                        at = V_F0 + 2 * IM * lin + IM + m
                        dve.wait_ge(sa_done, CREDIT + 8 * c + n + 1)
                        V.scalar_tensor_tensor((pl if lin else pg), ps[:, 2 * lin + 1, :], cols[:, at:at + 1],
                                               (al if lin else ag), ALU.add, ALU.mult).then_inc(sp_done, 1)
                        dve.wait_ge(sp_done, CREDIT + 8 * c + n + 1)
                        if not lin:
                            V.tensor_scalar(pg, pg, 7.0, None, ALU.min).then_inc(spm_done, 1)
                        else:
                            i = IM * c + m
                            V.tensor_scalar(pl, pl, 7.0, -7.0, ALU.min, ALU.max).then_inc(spc_done, 1)
                            dve.wait_ge(spc_done, CREDIT + i + 1)
                            V.scalar_tensor_tensor(uu, pl, 1.0, pg, ALU.add, ALU.mult).then_inc(su_done, 1)
                            dve.wait_ge(su_done, CREDIT + i + 1)
                            dve.wait_ge(ssig_done, CREDIT + i + 1)
                            V.tensor_tensor(hs[:, m, :], uu, sig, ALU.mult).then_inc(sh_done, 1)
                    dve.wait_ge(sosc_done, CREDIT + c + 1)
                    V.tensor_tensor(x[:, :, chunk(c)], x[:, :, chunk(c)], osc[:, :, :], ALU.add).then_inc(sx_done, 1)

            def tiles0():
                def products(dst, a_, slot, lin, done):
                    for m in range(IM):
                        at = W0 + 2 * IM * lin + IM + m
                        last = V.scalar_tensor_tensor(dst[:, m * P:(m + 1) * P], ps[:, 2 * lin + 1, m * P:(m + 1) * P],
                                                      w0[slot][:, at:at + 1], a_[:, m * P:(m + 1) * P], ALU.add, ALU.mult)
                    last.then_inc(done, 1)

                def body(t, slot, use):
                    dve.wait_ge(ag_done, CREDIT + t + 1)
                    products(pg, ag, slot, 0, pg_done)
                    dve.wait_ge(pg_done, CREDIT + t + 1)
                    V.tensor_scalar(pg, pg, 7.0, None, ALU.min).then_inc(pgm_done, 1)
                    dve.wait_ge(al_done, CREDIT + t + 1)
                    products(pl, al, slot, 1, pl_done)
                    dve.wait_ge(pl_done, CREDIT + t + 1)
                    V.tensor_scalar(pl, pl, 7.0, -7.0, ALU.min, ALU.max).then_inc(plc_done, 1)
                    dve.wait_ge(plc_done, CREDIT + t + 1)
                    V.scalar_tensor_tensor(uu, pl, 1.0, pg, ALU.add, ALU.mult).then_inc(u_done, 1)
                    dve.wait_ge(u_done, CREDIT + t + 1)
                    dve.wait_ge(sig_done, CREDIT + t + 1)
                    V.tensor_tensor(hh[slot][:, 0:CH], uu, sig, ALU.mult).then_inc(h_done, 1)

                over_tiles(dve, TILES0, body, body, body)

            def tiles1():
                def body(t, slot, use):
                    dve.wait_ge(l_done, CREDIT + TILES0 + t + 1)
                    V.tensor_scalar(hh[slot][:, CH:F1], ps[:, 2, :], 0.0, None, ALU.max).then_inc(pl_done, 1)

                over_tiles(dve, E1, body, body, body)

            def combine(f):
                for c in range(NCH):
                    n = NCH * f + c
                    sl = slice(c * TPC, (c + 1) * TPC)
                    dve.wait_ge(gath_in[c], 16 * TPC * (2 if f == 0 else 3))
                    if n:
                        dve.wait_ge(comb_done, CREDIT + n)
                    if f == 0:
                        link(V.tensor_tensor(yb, gb[:, sl, :], wide(wt2[:, sl], D), ALU.mult))
                        link(V.tensor_tensor(ya, ga[:, sl, :], wide(wt1[:, sl], D), ALU.mult))
                        V.tensor_tensor(ya, ya, yb, ALU.add).then_inc(y_done, 1)
                    else:
                        V.tensor_tensor(ya, ga[:, sl, :], wide(wt1[:, sl], D), ALU.mult).then_inc(y_done, 1)
                    dve.wait_ge(comb_done, CREDIT + n + 1)
                    V.tensor_tensor(x[:, :, c * CH:(c + 1) * CH], x[:, :, c * CH:(c + 1) * CH], ps[:, 0:2, :],
                                    ALU.add).then_inc(x_done, 1)

            dve.wait_ge(const_in, 16 * 10)
            V.tensor_copy(cb[:, :], cb_raw)
            dve.wait_ge(tanh_done, 1)
            for l in MHA:
                last = V.tensor_scalar(gbo[:, l, :], cols[:, V_ATT * l + V_O:V_ATT * l + V_O + KD], gts[:, l:l + 1], None,
                                       ALU.mult)
            last = V.tensor_scalar(gbo[:, 1, :], cols[:, V_F0 + 4 * IM:V_F0 + 4 * IM + KD], gts[:, 4:5], None, ALU.mult)
            last.then_inc(gbo_done, 1)
            for s in range(stages):
                l = s // 2
                if s % 2 == 0 and l in MHA:
                    kv(l)
                if s == 2:
                    kv_single()
                if s == 5:
                    round_weights()
                layer_norm(s)
                if s % 2 == 0 and l in MHA:
                    heads(l)
                if s == 2:
                    single()
                if s == 5:
                    quantized()
                if s == 7:
                    route3()
                    experts3()
                if s == 1:
                    route0()
                    shared0()
                    tiles0()
                    combine(0)
                if s == 3:
                    route1()
                    tiles1()
                    combine(1)


STAGES = 8


def kernel(**inputs):
    import concourse.bacc as bacc
    from concourse.bass_utils import run_bass_kernel_spmd

    arrays = host_layout(inputs)
    nc = bacc.Bacc("TRN2", target_bir_lowering=False, num_devices=1)
    dram = {n: nc.dram_tensor(f"in_{n}", a.shape, mybir.dt.from_np(a.dtype), kind="ExternalInput").ap()
            for n, a in arrays.items()}
    out = nc.dram_tensor("out_x", (P, KD, T), F32, kind="ExternalOutput").ap()
    program(nc, dram, out, STAGES)
    r = run_bass_kernel_spmd(nc, [{f"in_{n}": a for n, a in arrays.items()}], core_ids=[0])
    y = r.results[0]["out_x"]
    return np.ascontiguousarray(y.transpose(1, 0, 2).reshape(D, T).T.reshape(NB, S, D))
```

```python
from contextlib import ExitStack

import numpy as np

import concourse.bass as bass
from concourse import mybir

ALU = mybir.AluOpType
ACT = mybir.ActivationFunctionType
AX = mybir.AxisListType
F32 = mybir.dt.float32
BF16 = mybir.dt.bfloat16
I32 = mybir.dt.int32
U8 = mybir.dt.uint8
U32 = mybir.dt.uint32
ds = bass.ds
RMAX = bass.bass_isa.ReduceOp.max

P = 128
D = 256
KD = D // P
NB, S = 2, 1024
T = NB * S
CH = 512
NCH = T // CH
CPB = S // CH
TPC = CH // P
NT = T // P
KEYS = 77
KP = 80
JG = KP // 16
HH = 8
NEG = -3.0e38
FLOOR = -1.0e30
SL = 4 * KP
EPS = 1e-5
LN_STAGES = 8

C_ID, C_MEAN, C_ONE = 0, 128, 256
C_BLK, C_MHALF, C_TIE, C_IDX, C_SEL = 384, 392, 408, 424, 440
C_MAGIC = C_SEL + JG * P
C_TOK = C_MAGIC + 1
C_STEP = C_TOK + 16
C_LT = C_STEP + 16
C_TILE = C_LT + 64
C_N = C_TILE + 40
MAGIC = 12582912.0
B_ID, B_TRI, B_ONE = 0, 128, 256
B_N = B_ONE + 128
V_Q, V_K, V_O, V_QS, V_KS = 0, 2, 4, 6, 8
V_ATT = 10
V_F0 = 4 * V_ATT
E0, I0 = 9, 512
V_F2 = V_F0 + 4 * (I0 // P) + KD
F2 = 1024
V_N = V_F2 + F2 // P + KD
R0 = 8
W0 = KD * 4 * I0 + (I0 // P) * D
BC0 = 4 * (I0 // P)
TILES0 = (2 * T) // P + R0 - 1
E1, F1, C1 = 16, 1024, T // 16
E3 = 10
ORDER3 = [8, 9] + list(range(8))
W_Q, W_K, W_V, W_O, W_QS, W_KS = range(6)


def host_constants():
    cf = np.zeros((P, C_N), np.float32)
    p = np.arange(P)
    cf[:, C_ID:C_ID + P] = np.eye(P)
    cf[:, C_MEAN:C_MEAN + P] = 1.0 / D
    cf[:, C_ONE:C_ONE + P] = 1.0
    cf[:, C_BLK:C_BLK + HH] = p[:, None] // 16 == np.arange(HH)
    cf[:, C_MHALF:C_MHALF + 16] = -0.5
    cf[:, C_TIE:C_TIE + 16] = 16 - np.arange(16)
    cf[:, C_IDX:C_IDX + 16] = np.arange(16)
    cf[:, C_MAGIC] = MAGIC
    cf[:, C_TOK:C_TOK + NT] = T + np.arange(NT) * P + p[:, None]
    cf[:, C_STEP:C_STEP + 16] = np.arange(16) * P
    cf[:, C_LT:C_LT + 64] = np.tril(np.ones((8, 8)), -1).reshape(-1)
    cf[:, C_TILE:C_TILE + 40] = np.arange(40)
    cb = np.zeros((P, B_N), np.float32)
    cb[:, B_ID:B_ID + P] = np.eye(P)
    for j in range(JG):
        hit = np.arange(KP)[:, None] == 16 * j + p[None] % 16
        cf[:KP, C_SEL + j * P:C_SEL + (j + 1) * P] = hit
    cb[:, B_TRI:B_TRI + P] = p[:, None] < p[None]
    cb[:, B_ONE:B_ONE + P] = 1.0
    freq = np.exp(np.arange(0, 16, 2, dtype=np.float32) * (-(np.float32(4.0) * np.log(np.float32(10.0))) / np.float32(16)))
    ang = np.arange(S, dtype=np.float32)[None, :] * freq.astype(np.float32)[(p % 16) // 2][:, None]
    sign = np.where(p % 2 == 0, 1.0, -1.0).astype(np.float32)
    rope = np.stack([np.sin(ang) * sign[:, None], -np.cos(ang)], 1).astype(np.float32)
    return cf, cb, rope


def host_layout(i):
    a = {k: np.asarray(v) for k, v in i.items()}

    def rows(w):
        return w.reshape(-1, P, w.shape[-1]).transpose(1, 0, 2)

    def col(v):
        return v.reshape(-1, P).T

    cf, cb, rope = host_constants()
    swap = np.arange(D) ^ 1
    pad = list(range(KEYS)) + list(range(KP - KEYS))
    o = {"cf": cf, "cb": cb, "rope": rope}
    o["x"] = rows(a["x"].reshape(T, D).T)
    o["ctx"] = rows(a["ctx_1024"][:, pad].reshape(NB * KP, D).T)
    L = lambda l, n: a[f"L{l}_xattn_{n}"]
    att = {0: [L(0, "Wq"), L(0, "Wk"), L(0, "Wv"), L(0, "Wo")],
           1: [L(1, "Wq").T, L(1, "Wk").T, L(1, "Wv").T],
           2: [L(2, "Wq").T, L(2, "Wk").T, L(2, "Wv").T, L(2, "Wo").T, L(2, "Wq").T[:, swap], L(2, "Wk").T[:, swap]],
           3: [L(3, "Wq").T, L(3, "Wk").T, L(3, "Wv").T, L(3, "Wo").T]}
    for l, ws in att.items():
        o[f"aw{l}"] = np.stack([rows(w) for w in ws], 1)
        o[f"bv{l}"] = L(l, "bv")[None]
    cols = []
    for l in range(4):
        bo = L(l, "bo") if l != 1 else L(l, "bq")
        cols += [col(L(l, "bq")), col(L(l, "bk")), col(bo), col(L(l, "bq")[swap]), col(L(l, "bk")[swap])]
    F = lambda l, n: a[f"L{l}_ffn_{n}"]
    w1 = np.concatenate([F(0, "w1"), F(0, "sw1")[None]])
    w3 = np.concatenate([F(0, "w3"), F(0, "sw3")[None]])
    w2 = np.concatenate([F(0, "w2"), F(0, "sw2")[None]])
    b1 = np.concatenate([F(0, "b1"), F(0, "sb1")[None]])
    b3 = np.concatenate([F(0, "b3"), F(0, "sb3")[None]])
    b2 = np.concatenate([F(0, "b2"), F(0, "sb2")[None]])
    o["f0w"] = np.stack([np.concatenate(
        [rows(w[e]).reshape(P, -1) for w in (w1[:, :, ::2], w3[:, :, ::2], w1[:, :, 1::2], w3[:, :, 1::2], w2)]
        + [col(v) for v in (b1[e, ::2], b3[e, ::2], b1[e, 1::2], b3[e, 1::2])], 1) for e in range(E0)])
    o["f0b"] = b2
    cols += [col(b1[R0, ::2]), col(b3[R0, ::2]), col(b1[R0, 1::2]), col(b3[R0, 1::2]), col(b2[R0])]
    cols += [col(F(2, "b1")), col(F(2, "b2"))]
    o["cols"] = np.concatenate(cols, 1)
    o["g"] = np.concatenate([a["g_xattn"], a["g_ffn"]])[None]
    o["gate0"] = rows(F(0, "gate_w").T)
    o["gb0"] = F(0, "gate_b")[None]
    o["gate1"] = rows(F(1, "Wg"))
    o["gate3"] = rows(F(3, "gate_w"))
    o["gb3"] = F(3, "gate_bias")[None]
    o["f1w"] = np.stack([np.concatenate([rows(F(1, "w1")[e]).reshape(P, -1), rows(F(1, "w2")[e]).reshape(P, -1)], 1)
                         for e in range(E1)])
    o["f2w1"] = rows(F(2, "w1"))
    o["f2w2"] = rows(F(2, "w2"))
    wg = list(F(3, "w_gate")) + [F(3, "sw_gate")[:, :P], F(3, "sw_gate")[:, P:]]
    wu = list(F(3, "w_up")) + [F(3, "sw_up")[:, :P], F(3, "sw_up")[:, P:]]
    wd = list(F(3, "w_down")) + [F(3, "sw_down")[:P], F(3, "sw_down")[P:]]
    o["f3w"] = np.stack([np.concatenate([rows(g).reshape(P, -1), rows(u).reshape(P, -1), d], 1)
                         for g, u, d in zip(wg, wu, wd)], 1)
    m2 = np.pad(a["mask_1x1xSxS2_bk1"][0, 0], ((0, 0), (0, KP - KEYS)), constant_values=True)
    m3 = np.pad(a["mask_SxS2_ik0"], ((0, 0), (0, KP - KEYS)))
    for n, m in (("2", m2), ("3", m3)):
        o["mtok" + n] = m.reshape(S // P, P, KP).transpose(1, 0, 2)
    return {k: np.ascontiguousarray(v) for k, v in o.items()}


def program(nc, d, out, stages):
    with ExitStack() as ctx:
        def sb(name, shape, dt=F32):
            return ctx.enter_context(nc.sbuf_tensor(name, shape, dt))

        sems = {}

        def sem(name):
            sems[name] = ctx.enter_context(nc.semaphore(name))
            return sems[name]

        def carver(arena):
            at = [0]

            def take(shape, dt=F32, parts=P):
                n = int(np.prod(shape))
                words = n if dt in (F32, I32, U32) else (n + 1) // 2 if dt == BF16 else (n + 3) // 4
                v = arena[0:parts, at[0]:at[0] + words]
                at[0] += words
                assert at[0] <= arena.shape[1], (at[0], arena.shape)
                if dt != F32:
                    v = v.bitcast(dt)
                if len(shape) > 1:
                    names = "abcde"[:len(shape)]
                    v = v.rearrange(f"p ({' '.join(names)}) -> p {' '.join(names)}",
                                    **{c: s for c, s in zip(names[1:], shape[1:])})
                return v
            return take

        x = sb("x_res", [P, KD, T])
        xn = sb("x_norm", [P, KD, T])
        cf = sb("const_f", [P, C_N])
        cb = sb("const_b", [P, B_N], BF16)
        cols = sb("cols_sb", [P, V_N])
        ctxk = sb("ctx_sb", [P, KD, NB * KP])
        gts = sb("gates_tanh", [P, 8])
        gbo = sb("gated_bias", [P, 4, KD])
        aw_even = sb("aw_even", [P, 6 * KD * D + D])
        aw_odd = sb("aw_odd", [P, 4 * KD * D + D])
        gate_w = sb("gate_w", [P, 3, KD * 16])
        gate_b = sb("gate_b", [P, 2, 8])
        mtok = sb("mask_tok", [P, S // P, KP], BF16)
        big = sb("big", [P, 16384])
        work = sb("work", [P, 18900])
        zero = sb("zero", [P, D])

        aw, bv = {}, {}
        for l in range(4):
            arena, n = (aw_even, (4, 0, 6)[l]) if l % 2 == 0 else (aw_odd, (0, 3, 0, 4)[l])
            aw[l] = arena[:, 0:n * KD * D].rearrange("p (w k n) -> p w k n", w=n, k=KD)
            bv[l] = arena[0:1, arena.shape[1] - D:arena.shape[1]]

        ident = cf[:, C_ID:C_ID + P]
        mean_w = cf[:, C_MEAN:C_MEAN + P]
        ones_row = cf[0:1, C_ONE:C_ONE + P]
        blk = cf[:, C_BLK:C_BLK + HH]
        identb = cb[:, B_ID:B_ID + P]

        ps = ctx.enter_context(nc.psum_tensor("ps", [P, 8, CH], F32))

        take = carver(work)
        sq = take([KD, CH])
        stat = take([4, NT])
        osc = take([KD, CH])
        kbd = take([KD, NB, HH, KP])
        vbd = take([NB, JG, D])
        v80 = take([NB, D])
        kt = take([KD, NB * KP])
        q = take([KD, CH])
        smax = take([TPC, 2 * HH])
        psum_ = take([KD, 2, CH])
        ssum = take([TPC, 2 * HH])
        rd = take([TPC, 2 * HH])
        rde = take([TPC, KD * P])
        dif = take([2, HH, KP])
        pm = take([2, JG, HH * 16])
        rt = take([2, CH])
        num = take([KD, CH])
        neg4 = take([3, TPC])
        p1 = take([TPC, KP])
        pt = take([CH])
        o = take([KD, CH])
        take = carver(big)
        ptk = take([KD, JG, CH])
        cb_raw = big[:, KD * JG * CH:KD * JG * CH + B_N]
        rope = take([2, S])
        mtok_raw = {2: take([S // P, KP], U8), 3: take([S // P, KP], I32)}

        IM = I0 // P
        ring = carver(big)
        w0 = [ring([W0 + BC0]) for _ in range(3)]
        w1m = [w[:, 0:4096] for w in w0]
        hbig = big[:, 0:16384].rearrange("p (m t) -> p m t", m=F2 // P)
        combb = big[:, 0:16384].rearrange("p (e t) -> p e t", e=8)
        wq_raw = big[:, 8192:12288]

        take = carver(work)
        take([KD, CH]), take([4, NT]), take([KD, CH])
        xc = osc
        rows_ = take([NT, D])
        ra = [take([NT * 16]) for _ in range(6)]
        rv = [take([NT]) for _ in range(8)]
        oh1, oh2 = take([NT * 16]), take([NT * 16])
        mb16 = take([NT, 16], BF16)
        wt1, wt2 = take([NT]), take([NT])
        gix1, gix2 = take([NT], U32), take([NT], U32)
        six = take([NT], U32)
        e8 = [take([8]) for _ in range(4)]
        cmp8 = take([8, 16])
        cmpt = take([TILES0, 8])
        texf, tex = take([TILES0]), take([TILES0], I32)
        b2row = [take([D]) for _ in range(3)]
        xs = [take([D]) for _ in range(3)]
        xst = [take([KD * P]).rearrange("p (k n) -> p k n", k=KD) for _ in range(3)]
        os_ = [take([D]) for _ in range(3)]
        tail = take([6 * CH + 3 * F1])
        ag, al, pg, pl, sig, uu = (tail[:, n * CH:(n + 1) * CH] for n in range(6))
        hall = tail[:, 6 * CH:]
        hh = [hall[:, n * F1:(n + 1) * F1] for n in range(3)]
        hs = hall[:, 0:IM * CH].rearrange("p (m n) -> p m n", m=IM)
        ga = rows_
        gb = tail[:, 0:NT * D].rearrange("p (t n) -> p t n", t=NT)
        ya = hall[:, F1:2 * F1].rearrange("p (t n) -> p t n", t=TPC)
        yb = hall[:, 2 * F1:3 * F1].rearrange("p (t n) -> p t n", t=TPC)

        take = carver(work)
        take([KD, CH]), take([4, NT]), take([KD, CH])
        wq1, wq2 = take([F2 // P, D], BF16), take([KD, F2], BF16)
        wt1q, wt2q = take([KD, F2], BF16), take([F2 // P, D], BF16)
        xq = take([KD, T], BF16)
        hq = take([F2 // P, T], BF16)
        qs = take([8, F2 // P])
        qv = take([12])
        take = carver(work)
        take([KD, CH]), take([4, NT]), take([KD, CH])
        w3 = take([E3, 3 * D])
        lg3 = [take([NT, 8]) for _ in range(8)]
        rv3 = [take([NT]) for _ in range(8)]
        gr = [take([NT, 4]) for _ in range(7)]
        combt = take([8, NT])
        combT = take([P])
        sg3, t3, u3, h3 = take([2, CH]), take([CH]), take([CH]), take([2, CH])

        disp = nc.dram_tensor("dispatched", (TILES0 * P, D), F32, kind="Internal").ap()
        outs = nc.dram_tensor("expert_out", (TILES0 * P, D), F32, kind="Internal").ap()
        disp1 = nc.dram_tensor("dispatched1", (2 * T, D), F32, kind="Internal").ap()
        outs1 = nc.dram_tensor("expert_out1", (T, D), F32, kind="Internal").ap()
        comb3 = nc.dram_tensor("comb3", (P, P), F32, kind="Internal").ap()

        CREDIT = 1
        loop_sems = [sem(n) for n in (
            "x_done mean_done cent_done sq_done var_done rstdb_done xn_done "
            "q_done qsb_done score_done max_done sub_done exp_done padd_done den_done turn_done turned_done pv_done "
            "rd_done rde_done rb_done num_done o_done proj_done osc_done rope_done clamp_done "
            "q1_done qsb1_done score1_done max1_done neg1_done exp1_done rd1_done p1_done pt_done ptsb_done att1_done osc1_done "
            "xc_done front_done rows_done "
            "sa_done sp_done spm_done spc_done su_done sh_done ssig_done spair_done so_done sosc_done sx_done "
            "xt_done xst_done g_done ag_done pg_done pgm_done l_done al_done pl_done plc_done u_done h_done sig_done o2_done "
            "os_done ya_done yb_done y_done comb_done "
            "m1_done hact_done hrnd_done m2_done osc2_done xrnd_done xclip_done xq_done hq_done hmax_done "
            
            ).split()]
        (x_done, mean_done, cent_done, sq_done, var_done, rstdb_done, xn_done,
         q_done, qsb_done, score_done, max_done, sub_done, exp_done, padd_done, den_done, turn_done, turned_done, pv_done,
         rd_done, rde_done, rb_done, num_done, o_done, proj_done, osc_done, rope_done, clamp_done,
         q1_done, qsb1_done, score1_done, max1_done, neg1_done, exp1_done, rd1_done, p1_done, pt_done, ptsb_done,
         att1_done, osc1_done,
         xc_done, front_done, rows_done,
         sa_done, sp_done, spm_done, spc_done, su_done, sh_done, ssig_done, spair_done, so_done, sosc_done, sx_done,
         xt_done, xst_done, g_done, ag_done, pg_done, pgm_done, l_done, al_done, pl_done, plc_done, u_done, h_done,
         sig_done, o2_done, os_done, ya_done, yb_done, y_done, comb_done,
         m1_done, hact_done, hrnd_done, m2_done, osc2_done, xrnd_done, xclip_done, xq_done, hq_done, hmax_done,
         ) = loop_sems
        const_in = sem("const_in")
        x_in = sem("x_in")
        aw_in = [sem("aw_in_even"), sem("aw_in_odd")] * 2
        mask_in = sem("mask_in")
        rope_in = sem("rope_in")
        x_out = sem("x_out")
        tanh_done = sem("tanh_done")
        step = sem("dve_step")
        gbo_done, eps_done, rstd_done = sem("gbo_done"), sem("eps_done"), sem("rstd_done")
        pow_done = sem("pow_done")
        k_done, kt_done, v80_done, v80sb_done, vrep_done, kbd_done, vbd_done, mask_done = (
            sem(n) for n in "k_done kt_done v80_done v80sb_done vrep_done kbd_done vbd_done mask_done".split())
        kv1_done, kv1sb_done = sem("kv1_done"), sem("kv1sb_done")

        zero_set, zeros_in = sem("zero_set"), sem("zeros_in")
        shared_in = sem("shared_in")
        w_in = [sem(f"w_in{n}") for n in range(3)]
        out_in = [sem(f"out_in{n}") for n in range(3)]
        smax_sub, smax_exp = sem("route_sub"), sem("route_exp")
        pick_done, rank_done, rank_read, index_done, texp_done = (
            sem(n) for n in "pick_done rank_done rank_read index_done tile_expert_done".split())
        scat_in = sem("scat_in")
        gath_in = [sem(f"gath_in{c}") for c in range(NCH)]

        wq_in, wround_done, wturn_done, wturned_done = (sem(n) for n in "wq_in wround_done wturn_done wturned_done".split())
        tmax_done, allmax_done, xscale_done, hscale_done = (
            sem(n) for n in "tmax_done allmax_done xscale_done hscale_done".split())
        w3_in, sig3_done, comb3_done, combturn_done, combsb_done, comb3_in, combb_in = (
            sem(n) for n in "w3_in sig3_done comb3_done combturn_done combsb_done comb3_in combb_in".split())

        MHA = (0, 2, 3)
        mb16f = [mb16.rearrange("p t e -> p (t e)")[:, 0:NT * n].rearrange("p (t e) -> p t e", e=n) for n in (R0, E1)]
        block = ctx.enter_context(nc.Block())

        def chunk(c):
            return ds(c * CH, CH)

        def over_tiles(eng, n, first, body, last):
            first(0, 0, 0)
            loops = (n - 2) // 3
            with eng.Fori(0, loops) as it:
                for r in range(3):
                    body(3 * it + 1 + r, (1 + r) % 3, it + (1 + r) // 3)
            for t in range(1 + 3 * loops, n - 1):
                body(t, t % 3, t // 3)
            last(n - 1, (n - 1) % 3, (n - 1) // 3)

        def over_chunks(eng, body):
            body(0, 0, before=False)
            with eng.Fori(1, CPB) as cc:
                body(0, cc)
            for b in range(1, NB):
                with eng.Fori(0, CPB - (b == NB - 1)) as cc:
                    body(b, cc)
            body(NB - 1, CPB - 1, after=False)

        def stage_ready(eng, s):
            if s:
                eng.wait_ge(x_done, CREDIT + NCH * s)

        @block.sync
        def _(sp):
            for s_ in loop_sems:
                sp.sem_inc(s_, CREDIT)
            sp.sem_inc(hact_done, 4)
            consts = [(cf[:], d["cf"]), (cb_raw, d["cb"]), (cols[:], d["cols"]), (ctxk[:], d["ctx"]),
                      (gts[:], d["g"].partition_broadcast(P)),
                      (gate_w[:, 0, 0:16], d["gate0"].rearrange("p k e -> p (k e)")),
                      (gate_w[:, 1, :], d["gate1"].rearrange("p k e -> p (k e)")),
                      (gate_w[:, 2, 0:16], d["gate3"].rearrange("p k e -> p (k e)")),
                      (gate_b[:, 0, :], d["gb0"].partition_broadcast(P)), (gate_b[:, 1, :], d["gb3"].partition_broadcast(P))]
            for dst, src in consts:
                sp.dma_start(dst, src).then_inc(const_in, 16)
            sp.dma_start(x[:], d["x"]).then_inc(x_in, 16)
            for l in (0, 1):
                sp.dma_start(aw[l], d[f"aw{l}"]).then_inc(aw_in[l], 16)
                sp.dma_start(bv[l], d[f"bv{l}"]).then_inc(aw_in[l], 16)

            def reload(l):
                sp.wait_ge(x_done, CREDIT + NCH * (2 * (l - 2) + 1))
                sp.dma_start(aw[l], d[f"aw{l}"]).then_inc(aw_in[l], 16)
                sp.dma_start(bv[l], d[f"bv{l}"]).then_inc(aw_in[l], 16)

            def masks(l):
                sp.wait_ge(x_done, CREDIT + NCH * 2 * l)
                sp.dma_start(mtok_raw[l], d[f"mtok{l}"]).then_inc(mask_in, 16)
                if l == 2:
                    sp.dma_start(rope, d["rope"]).then_inc(rope_in, 16)

            def feed_tiles(n, base, load):
                dst = outs1 if base else outs

                def store(t, slot):
                    sp.wait_ge(os_done, CREDIT + base + t + 1)
                    sp.dma_start(dst[ds(t * P, P), :], os_[slot]).then_inc(out_in[slot], 16)

                def both(t, slot):
                    sp.wait_ge(o2_done, CREDIT + base + t - 2)
                    load(t, slot)
                    store(t - 3, slot)

                for t in range(3):
                    load(t, t)
                with sp.Fori(1, n // 3) as it:
                    for r in range(3):
                        both(3 * it + r, r)
                for t in range(3 * (n // 3), n):
                    both(t, t % 3)
                for t in range(n - 3, n):
                    store(t, t % 3)

            if stages > 1:
                sp.wait_ge(zero_set, 1)
                for dst in (disp, disp1):
                    sp.dma_start(dst.rearrange("(n p) d -> p n d", p=P),
                                 zero[:, :].unsqueeze(1).broadcast_to([P, dst.shape[0] // P, D])).then_inc(zeros_in, 16)
                sp.dma_start(w0[2], d["f0w"][R0]).then_inc(shared_in, 16)
                sp.wait_ge(texp_done, 1)
                sp.wait_ge(scat_in, 16 * 2 * NT)

                def load0(t, slot):
                    if isinstance(t, int) and t == 2:
                        sp.wait_ge(sx_done, CREDIT + NCH)
                    e = sp.value_load(tex[0:1, ds(t, 1)], min_val=0, max_val=R0 - 1)
                    sp.dma_start(w0[slot], d["f0w"][ds(e, 1)].rearrange("e p n -> (e p) n")).then_inc(w_in[slot], 16)
                    sp.dma_start(b2row[slot][0:1, :], d["f0b"][ds(e, 1)]).then_inc(w_in[slot], 16)
                    sp.dma_start(xs[slot], disp[ds(t * P, P), :]).then_inc(w_in[slot], 16)

                feed_tiles(TILES0, 0, load0)
            if stages > 3:
                sp.wait_ge(x_done, CREDIT + NCH * 2)
                sp.wait_ge(scat_in, 16 * 3 * NT)

                def load1(t, slot):
                    sp.dma_start(w1m[slot], d["f1w"][ds(t, 1)].rearrange("e p n -> (e p) n")).then_inc(w_in[slot], 16)
                    sp.dma_start(xs[slot], disp1[ds(t * P, P), :]).then_inc(w_in[slot], 16)

                feed_tiles(E1, TILES0, load1)
            if stages > 4:
                reload(2)
                masks(2)
                sp.dma_start(wq_raw[:, 0:2048], d["f2w1"].rearrange("p a b -> p (a b)")).then_inc(wq_in, 16)
                sp.dma_start(wq_raw[:, 2048:4096], d["f2w2"].rearrange("p a b -> p (a b)")).then_inc(wq_in, 16)
            if stages == 5:
                sp.wait_ge(wq_in, 32)
            if stages > 6:
                reload(3)
                masks(3)
            if stages > 7:
                sp.wait_ge(x_done, CREDIT + NCH * 7)
                sp.dma_start(w3, d["f3w"]).then_inc(w3_in, 16)
                sp.wait_ge(combsb_done, 1)
                sp.dma_start(comb3, combT).then_inc(comb3_in, 16)
                sp.wait_ge(comb3_in, 16)
                rows3 = comb3.rearrange("(e c t) p -> e c (t p)", e=8, c=NCH)
                for c in range(NCH):
                    for e in range(8):
                        sp.dma_start(combb[:, e, c * CH:(c + 1) * CH], rows3[e:e + 1, c, :].partition_broadcast(P)
                                     ).then_inc(combb_in, 16)
                    sp.wait_ge(combb_in, 16 * 8 * (c + 1))
            sp.wait_ge(aw_in[1], 32)
            sp.wait_ge(x_done, CREDIT + NCH * stages)
            sp.dma_start(out, x[:]).then_inc(x_out, 16)
            sp.wait_ge(x_out, 16)

        @block.tensor
        def _(pe):
            mm = nc.tensor.matmul

            def layer_norm(s):
                b0 = CREDIT + NCH * s
                stage_ready(pe, s)
                if s == 0:
                    pe.wait_ge(const_in, 16 * 10)
                    pe.wait_ge(x_in, 16)
                if s // 2 in MHA and s % 2 == 0:
                    pe.wait_ge(vbd_done, NB * JG * (1 + MHA.index(s // 2)))
                with pe.Fori(0, NCH) as c:
                    for k in range(KD):
                        last = mm(ps[:, c, :], mean_w, x[:, k, chunk(c)], start=k == 0, stop=k == KD - 1)
                    last.then_inc(mean_done, 1)
                with pe.Fori(0, NCH) as c:
                    pe.wait_ge(sq_done, b0 + c + 1)
                    for t in range(TPC):
                        for k in range(KD):
                            last = mm(ps[:, 4, ds(c * TPC + t, 1)], sq[:, k, t * P:(t + 1) * P], mean_w[:, 0:1],
                                      start=k == 0, stop=k == KD - 1)
                    last.then_inc(var_done, 1)
                pe.wait_ge(rstd_done, s + 1)
                for c in range(NCH):
                    for t in range(TPC):
                        n = c * TPC + t
                        last = nc.tensor.transpose(ps[:, 4 + c, t * P:(t + 1) * P], stat[:, 1, n:n + 1].broadcast_to([P, P]),
                                                   ident)
                    last.then_inc(rstdb_done, 1)

            def kv(l):
                a = MHA.index(l)
                stage_ready(pe, 2 * l)
                if l == 0:
                    pe.wait_ge(const_in, 16 * 10)
                pe.wait_ge(aw_in[l], 32 * (1 + l // 2))
                ks = [(W_K, 0)] + ([(W_KS, 2)] if l == 2 else [])
                for w, bank in ks:
                    for m in range(KD):
                        for k in range(KD):
                            last = mm(ps[:, bank + m, 0:NB * KP], aw[l][:, w, k, m * P:(m + 1) * P], ctxk[:, k, :],
                                      start=k == 0, stop=k == KD - 1)
                last.then_inc(k_done, 1)
                for b in range(NB):
                    for k in range(KD):
                        mm(ps[0:KP, 4 + b, 0:D], ctxk[:, k, b * KP:(b + 1) * KP], aw[l][:, W_V, k, :],
                           start=k == 0, stop=False)
                    last = mm(ps[0:KP, 4 + b, 0:D], ones_row[:, 0:KP], bv[l], start=False, stop=True)
                last.then_inc(v80_done, 1)
                pe.wait_ge(kt_done, a + 1)
                pe.wait_ge(v80sb_done, a + 1)
                for n in range(NB * JG):
                    b, j = divmod(n, JG)
                    bank, half = (6, 7, 4, 5, 0)[n // 2], n % 2
                    mm(ps[:, bank, half * D:(half + 1) * D], cf[0:KP, C_SEL + j * P:C_SEL + (j + 1) * P],
                       v80[0:KP, b, :], start=True, stop=True).then_inc(vrep_done, 1)

            def heads(l):
                a = MHA.index(l)
                rot, masked = l == 2, l != 0

                def queries(i, c):
                    pe.wait_ge(sub_done, CREDIT + 8 * i)
                    for w, bank in [(W_Q, 2)] + ([(W_QS, 0)] if rot else []):
                        for m in range(KD):
                            for k in range(KD):
                                last = mm(ps[:, bank + m, :], aw[l][:, w, k, m * P:(m + 1) * P], xn[:, k, chunk(c)],
                                          start=k == 0, stop=k == KD - 1)
                    last.then_inc(q_done, 1)

                def scores(i, cc, b, n):
                    hf, t = divmod(n, TPC)
                    bank = 2 * ((n + 1) % 2)
                    if n > 1:
                        pe.wait_ge(sub_done, CREDIT + 8 * i + n - 1)
                    for g in range(2):
                        last = mm(ps[:, bank + g, 0:SL], q[:, hf, t * P:(t + 1) * P],
                                  kbd[:, hf, b, 4 * g:4 * (g + 1), :].rearrange("p h k -> p (h k)"),
                                  start=True, stop=not masked)
                    if masked:
                        for g in range(2):
                            last = mm(ps[:, bank + g, 0:SL], identb,
                                      mtok[:, ds(cc * TPC + t, 1), :].broadcast_to([P, 4, KP]), start=False, stop=True)
                    last.then_inc(score_done, 1)

                def turn(i, n):
                    pe.wait_ge(exp_done, CREDIT + 8 * i + n + 1)
                    pe.wait_ge(turned_done, CREDIT + 8 * i + n)
                    wide_ = ps[:, 4:6, :].rearrange("p b n -> p (b n)")
                    for j in range(JG):
                        last = nc.tensor.transpose(wide_[:, j * P:(j + 1) * P], pm[:, n % 2, j, :], ident)
                    last.then_inc(turn_done, 1)

                def values(i, b, hf):
                    pe.wait_ge(turned_done, CREDIT + 8 * i + TPC * (hf + 1))
                    for j in range(JG):
                        last = mm(ps[:, 6 + hf, :], vbd[:, b, j, hf * P:(hf + 1) * P], ptk[:, hf, j, :],
                                  start=j == 0, stop=j == JG - 1)
                    last.then_inc(pv_done, 1)

                def denominators(i):
                    pe.wait_ge(num_done, CREDIT + 2 * i + 2)
                    pe.wait_ge(padd_done, CREDIT + 6 * i + 6)
                    for t in range(TPC):
                        for hf in range(KD):
                            last = mm(ps[:, 6, t * 16 + hf * HH:t * 16 + (hf + 1) * HH],
                                      psum_[:, hf, 0, t * P:(t + 1) * P], blk, start=True, stop=True)
                    last.then_inc(den_done, 1)

                def inverses(i):
                    pe.wait_ge(rde_done, CREDIT + i + 1)
                    for hf in range(KD):
                        for t in range(TPC):
                            last = nc.tensor.transpose(ps[:, 6 + hf, t * P:(t + 1) * P], rde[:, t, hf * P:(hf + 1) * P], ident)
                    last.then_inc(rb_done, 1)

                def project(i):
                    pe.wait_ge(o_done, CREDIT + i + 1)
                    for m in range(KD):
                        for k in range(KD):
                            last = mm(ps[:, 6 + m, :], aw[l][:, W_O, k, m * P:(m + 1) * P], o[:, k, :],
                                      start=k == 0, stop=k == KD - 1)
                    last.then_inc(proj_done, 1)

                def body(b, cc, before=True, after=True):
                    c = CPB * b + cc
                    i = NCH * a + c
                    pe.wait_ge(qsb_done, CREDIT + i + 1)
                    scores(i, cc, b, 0)
                    scores(i, cc, b, 1)
                    if before:
                        denominators(i - 1)
                    for n in range(2, 8):
                        scores(i, cc, b, n)
                        turn(i, n - 2)
                        if n == 4 and before:
                            inverses(i - 1)
                        if n == 5 and before:
                            project(i - 1)
                    pe.wait_ge(osc_done, CREDIT + i)
                    values(i, b, 0)
                    turn(i, 6)
                    turn(i, 7)
                    if after:
                        queries(i + 1, c + 1)
                    values(i, b, 1)

                pe.wait_ge(kbd_done, a + 1)
                if masked:
                    pe.wait_ge(mask_done, a)
                pe.wait_ge(xn_done, CREDIT + NCH * (2 * l + 1))
                queries(NCH * a, 0)
                over_chunks(pe, body)
                i = NCH * (a + 1) - 1
                denominators(i)
                inverses(i)
                project(i)

            def kv_single():
                stage_ready(pe, 2)
                pe.wait_ge(aw_in[1], 32)
                for m in range(KD):
                    for k in range(KD):
                        last = mm(ps[:, m, 0:NB * KP], aw[1][:, W_K, k, m * P:(m + 1) * P], ctxk[:, k, :],
                                  start=k == 0, stop=k == KD - 1)
                for b in range(NB):
                    for k in range(KD):
                        mm(ps[0:KP, 4 + b, 0:D], ctxk[:, k, b * KP:(b + 1) * KP], aw[1][:, W_V, k, :],
                           start=k == 0, stop=False)
                    last = mm(ps[0:KP, 4 + b, 0:D], ones_row[:, 0:KP], bv[1], start=False, stop=True)
                last.then_inc(kv1_done, 1)
                pe.wait_ge(kv1sb_done, 2)

            def single():
                pe.wait_ge(xn_done, CREDIT + NCH * 3)
                for b in range(NB):
                    with pe.Fori(0, CPB) as cc:
                        i = CPB * b + cc
                        pe.wait_ge(qsb1_done, CREDIT + i)
                        for m in range(KD):
                            for k in range(KD):
                                last = mm(ps[:, m, :], aw[1][:, W_Q, k, m * P:(m + 1) * P], xn[:, k, chunk(i)],
                                          start=k == 0, stop=k == KD - 1)
                        last.then_inc(q1_done, 1)
                        pe.wait_ge(qsb1_done, CREDIT + i + 1)
                        pe.wait_ge(exp1_done, CREDIT + i)
                        for t in range(TPC):
                            for k in range(KD):
                                last = mm(ps[:, 2, t * KP:t * KP + KEYS], q[:, k, t * P:(t + 1) * P],
                                          kt[:, k, b * KP:b * KP + KEYS], start=k == 0, stop=k == KD - 1)
                        last.then_inc(score1_done, 1)
                        pe.wait_ge(p1_done, CREDIT + i + 1)
                        for t in range(TPC):
                            last = nc.tensor.transpose(ps[0:KEYS, 3, t * P:(t + 1) * P], p1[:, t, 0:KEYS], ident)
                        last.then_inc(pt_done, 1)
                        pe.wait_ge(ptsb_done, CREDIT + i + 1)
                        pe.wait_ge(osc1_done, CREDIT + i)
                        for m in range(KD):
                            last = mm(ps[:, 4 + m, :], v80[0:KEYS, b, m * P:(m + 1) * P], pt[0:KEYS, :],
                                      start=True, stop=True)
                        last.then_inc(att1_done, 1)

            def front(f, n_exp, with_rows):
                w = gate_w[:, f, 0:KD * n_exp].rearrange("p (k e) -> p k e", k=KD)
                with pe.Fori(0, NCH) as c:
                    pe.wait_ge(xc_done, CREDIT + NCH * f + c + 1)
                    if with_rows:
                        pe.wait_ge(rows_done, CREDIT + NCH * f + c)
                    for t in range(TPC):
                        for k in range(KD):
                            last = mm(ps[:, 0, ds((c * TPC + t) * n_exp, n_exp)], xc[:, k, t * P:(t + 1) * P], w[:, k, :],
                                      start=k == 0, stop=k == KD - 1)
                        if with_rows:
                            for k in range(KD):
                                last = nc.tensor.transpose(ps[:, 1 + t // 2, (t % 2) * D + k * P:(t % 2) * D + (k + 1) * P],
                                                           xc[:, k, t * P:(t + 1) * P], ident)
                    last.then_inc(front_done, 1)

            def ranks(f, n_exp):
                pe.wait_ge(pick_done, f + 1)
                picks = mb16f[f]
                n = NT * n_exp
                mm(ps[:, 3, 0:n], cb[:, B_TRI:B_TRI + P], picks.rearrange("p t e -> p (t e)"), start=True, stop=False)
                for t in range(NT - 1):
                    mm(ps[:, 3, (t + 1) * n_exp:n].rearrange("p (t e) -> p t e", e=n_exp), cb[:, B_ONE:B_ONE + P],
                       picks[:, t:t + 1, :].broadcast_to([P, NT - 1 - t, n_exp]), start=False, stop=t == NT - 2)
                for t in range(NT):
                    last = mm(ps[:, 4, 0:n_exp], cb[:, B_ONE:B_ONE + P], picks[:, t, :], start=t == 0, stop=t == NT - 1)
                last.then_inc(rank_done, 1)
                pe.wait_ge(rank_read, f + 1)

            def part(w, n, k, m):
                at = (n * KD + k) * I0 + m * P
                return w[:, at:at + P]

            def down0(w, k):
                at = 4 * KD * I0 + k * D
                return w[:, at:at + D]

            def shared0():
                w = w0[2]
                pe.wait_ge(shared_in, 16)
                with pe.Fori(0, NCH) as c:
                    for n in range(2 * IM):
                        m, lin = divmod(n, 2)
                        pe.wait_ge(sp_done, CREDIT + 8 * c + max(n - 1, 0))
                        for w_ in range(2):
                            for k in range(KD):
                                last = mm(ps[:, 2 * lin + w_, :], part(w, 2 * lin + w_, k, m), xn[:, k, chunk(c)],
                                          start=k == 0, stop=k == KD - 1)
                        last.then_inc(spair_done, 1)
                    pe.wait_ge(sh_done, CREDIT + IM * c + IM)
                    pe.wait_ge(sosc_done, CREDIT + c)
                    for m in range(KD):
                        for k in range(IM):
                            last = mm(ps[:, 6 + m, :], down0(w, k)[:, m * P:(m + 1) * P], hs[:, k, :],
                                      start=k == 0, stop=k == IM - 1)
                    last.then_inc(so_done, 1)

            def tile_rows(t, slot, use, uses0, b0):
                pe.wait_ge(w_in[slot], uses0 + (32 if b0 else 48) * (use + 1))
                for k in range(KD):
                    last = nc.tensor.transpose(ps[:, 5, k * P:(k + 1) * P], xs[slot][:, k * P:(k + 1) * P], ident)
                last.then_inc(xt_done, 1)

            def tiles0():
                def up(t, slot, lin):
                    for w_ in range(2):
                        for m in range(IM):
                            for k in range(KD):
                                last = mm(ps[:, 2 * lin + w_, m * P:(m + 1) * P], part(w0[slot], 2 * lin + w_, k, m),
                                          xst[slot][:, k, :], start=k == 0, stop=k == KD - 1)
                    last.then_inc(l_done if lin else g_done, 1)

                def down(t, slot):
                    pe.wait_ge(h_done, CREDIT + t + 1)
                    pe.wait_ge(os_done, CREDIT + t)
                    mm(ps[:, 4, 0:D], ones_row, b2row[slot][0:1, :], start=True, stop=False)
                    for k in range(IM):
                        last = mm(ps[:, 4, 0:D], hh[slot][:, k * P:(k + 1) * P], down0(w0[slot], k),
                                  start=False, stop=k == IM - 1)
                    last.then_inc(o2_done, 1)

                def body(t, slot, use, before=True, after=True):
                    pe.wait_ge(xst_done, CREDIT + t + 1)
                    pe.wait_ge(pg_done, CREDIT + t)
                    up(t, slot, 0)
                    if before:
                        down(t - 1, (slot + 2) % 3)
                    pe.wait_ge(pl_done, CREDIT + t)
                    up(t, slot, 1)
                    if after:
                        tile_rows(t + 1, (slot + 1) % 3, use + (slot == 2), 0, 0)

                tile_rows(0, 0, 0, 0, 0)
                over_tiles(pe, TILES0, lambda t, s_, u: body(t, s_, u, before=False), body,
                           lambda t, s_, u: body(t, s_, u, after=False))
                down(TILES0 - 1, (TILES0 - 1) % 3)

            def tiles1():
                uses0 = 48 * (TILES0 // 3)

                def up(t, slot, half):
                    for m in range(4):
                        for k in range(KD):
                            at = k * F1 + (4 * half + m) * P
                            last = mm(ps[:, 2 * half, m * P:(m + 1) * P], w1m[slot][:, at:at + P], xst[slot][:, k, :],
                                      start=k == 0, stop=k == KD - 1)
                    last.then_inc(l_done if half else g_done, 1)

                def down(t, slot):
                    pe.wait_ge(ag_done, CREDIT + TILES0 + t + 1)
                    pe.wait_ge(pl_done, CREDIT + TILES0 + t + 1)
                    pe.wait_ge(os_done, CREDIT + TILES0 + t)
                    for k in range(F1 // P):
                        last = mm(ps[:, 4, 0:D], hh[slot][:, k * P:(k + 1) * P],
                                  w1m[slot][:, KD * F1 + k * D:KD * F1 + (k + 1) * D], start=k == 0, stop=k == F1 // P - 1)
                    last.then_inc(o2_done, 1)

                def body(t, slot, use, before=True, after=True):
                    pe.wait_ge(xst_done, CREDIT + TILES0 + t + 1)
                    pe.wait_ge(ag_done, CREDIT + TILES0 + t)
                    up(t, slot, 0)
                    if before:
                        down(t - 1, (slot + 2) % 3)
                    pe.wait_ge(pl_done, CREDIT + TILES0 + t)
                    up(t, slot, 1)
                    if after:
                        tile_rows(t + 1, (slot + 1) % 3, use + (slot == 2), uses0, 1)

                tile_rows(0, 0, 0, uses0, 1)
                over_tiles(pe, E1, lambda t, s_, u: body(t, s_, u, before=False), body,
                           lambda t, s_, u: body(t, s_, u, after=False))
                down(E1 - 1, (E1 - 1) % 3)

            def combine(f):
                with pe.Fori(0, NCH) as c:
                    pe.wait_ge(y_done, CREDIT + NCH * f + c + 1)
                    pe.wait_ge(x_done, CREDIT + NCH * (1 + 2 * f) + c)
                    for m in range(KD):
                        for t in range(TPC):
                            last = nc.tensor.transpose(ps[:, m, t * P:(t + 1) * P], ya[:, t, m * P:(m + 1) * P], ident)
                    last.then_inc(comb_done, 1)

            def turn_weights():
                pe.wait_ge(wround_done, 1)
                for k in range(KD):
                    for m in range(F2 // P):
                        nc.tensor.transpose(ps[:, k, :].bitcast(BF16)[:, m * P:(m + 1) * P],
                                            wq1[:, m, k * P:(k + 1) * P], identb)
                for k in range(F2 // P):
                    for m in range(KD):
                        at = k * D + m * P
                        last = nc.tensor.transpose(ps[:, 2 + at // 1024, :].bitcast(BF16)[:, at % 1024:at % 1024 + P],
                                                   wq2[:, m, k * P:(k + 1) * P], identb)
                last.then_inc(wturn_done, 1)
                pe.wait_ge(wturned_done, 1)

            def quantized():
                with pe.Fori(0, NCH) as c:
                    pe.wait_ge(xq_done, CREDIT + c + 1)
                    for m in range(F2 // P):
                        if m % 4 == 0:
                            pe.wait_ge(hact_done, CREDIT + 8 * c + m)
                        for k in range(KD):
                            last = mm(ps[:, m, :], wt1q[:, k, m * P:(m + 1) * P], xq[:, k, chunk(c)],
                                      start=k == 0, stop=k == KD - 1)
                        last.then_inc(m1_done, 1)
                pe.wait_ge(hact_done, CREDIT + 4 + 8 * NCH)
                with pe.Fori(0, NCH) as c:
                    pe.wait_ge(hq_done, CREDIT + c + 1)
                    pe.wait_ge(osc2_done, CREDIT + c)
                    for m in range(KD):
                        for k in range(F2 // P):
                            last = mm(ps[:, m, :], wt2q[:, k, m * P:(m + 1) * P], hq[:, k, chunk(c)],
                                      start=k == 0, stop=k == F2 // P - 1)
                    last.then_inc(m2_done, 1)

            def experts3():
                pe.wait_ge(comb3_done, 1)
                nc.tensor.transpose(ps[:, 1, 0:P], combt.rearrange("p e t -> p (e t)"), ident).then_inc(combturn_done, 1)
                pe.wait_ge(w3_in, 16)
                pe.wait_ge(combsb_done, 1)
                with pe.Fori(0, NCH) as c:
                    def up(n):
                        pe.wait_ge(su_done, CREDIT + IM * NCH + E3 * c + max(n - 1, 0))
                        for w_ in range(2):
                            for k in range(KD):
                                last = mm(ps[:, 2 * (n % 2) + w_, :], w3[:, ORDER3[n], (w_ * KD + k) * P:(w_ * KD + k + 1) * P],
                                          xn[:, k, chunk(c)], start=k == 0, stop=k == KD - 1)
                        last.then_inc(spair_done, 1)

                    up(0)
                    for n in range(E3):
                        if n + 1 < E3:
                            up(n + 1)
                        pe.wait_ge(sh_done, CREDIT + IM * NCH + E3 * c + n + 1)
                        if n == 0:
                            pe.wait_ge(x_done, CREDIT + NCH * 7 + c)
                        for m in range(KD):
                            last = mm(ps[:, 4 + m, :], w3[:, ORDER3[n], 2 * D + m * P:2 * D + (m + 1) * P], h3[:, n % 2, :],
                                      start=n == 0, stop=n == E3 - 1)
                        last.then_inc(so_done, 1)

            pe.wait_ge(tanh_done, 1)
            for s in range(stages):
                l = s // 2
                if s % 2 == 0 and l in MHA:
                    kv(l)
                if s == 2:
                    kv_single()
                if s == 5:
                    turn_weights()
                layer_norm(s)
                if s % 2 == 0 and l in MHA:
                    heads(l)
                if s == 2:
                    single()
                if s == 5:
                    quantized()
                if s == 7:
                    pe.wait_ge(xn_done, CREDIT + NCH * 8)
                    front(2, 8, False)
                    experts3()
                if s == 1:
                    pe.wait_ge(xn_done, CREDIT + NCH * 2)
                    front(0, R0, True)
                    ranks(0, R0)
                    shared0()
                    tiles0()
                    combine(0)
                if s == 3:
                    pe.wait_ge(xn_done, CREDIT + NCH * 4)
                    front(1, E1, True)
                    ranks(1, E1)
                    tiles1()
                    combine(1)

        @block.scalar
        def _(act):
            A = nc.scalar.activation

            def layer_norm(s):
                b0 = CREDIT + NCH * s
                with act.Fori(0, NCH) as c:
                    act.wait_ge(cent_done, b0 + c + 1)
                    act.wait_ge(var_done, b0 + c)
                    A(sq[:, :, :], xn[:, :, chunk(c)], ACT.Square).then_inc(sq_done, 1)

            def heads(l):
                a = MHA.index(l)

                def exponentials(i, n):
                    act.wait_ge(sub_done, CREDIT + 8 * i + n + 1)
                    act.wait_ge(turn_done, CREDIT + 8 * i + max(n - 1, 0))
                    A(pm[:, n % 2, :, :].rearrange("p j (h i) -> p h j i", i=16),
                      dif[:, n % 2, :, :].rearrange("p h (j i) -> p h j i", i=16), ACT.Exp).then_inc(exp_done, 1)

                def turned(i, n):
                    hf, t = divmod(n, TPC)
                    act.wait_ge(turn_done, CREDIT + 8 * i + n + 1)
                    act.wait_ge(pv_done, CREDIT + 2 * i)
                    act.wait_ge(padd_done, CREDIT + 6 * i)
                    A(ptk[:, hf, :, t * P:(t + 1) * P],
                      ps[:, 4:6, :].rearrange("p b n -> p (b n)")[:, 0:JG * P].rearrange("p (j n) -> p j n", j=JG),
                      ACT.Copy).then_inc(turned_done, 1)

                def numerators(i, hf):
                    act.wait_ge(pv_done, CREDIT + 2 * i + hf + 1)
                    A(num[:, hf, :], ps[:, 6 + hf, :], ACT.Copy).then_inc(num_done, 1)

                def gated_out(i):
                    act.wait_ge(proj_done, CREDIT + i + 1)
                    act.wait_ge(x_done, CREDIT + NCH * (2 * l - a) + i)
                    for m in range(KD):
                        last = A(osc[:, m, :], ps[:, 6 + m, :], ACT.Identity, bias=gbo[:, l, m:m + 1],
                                 scale=gts[:, l:l + 1])
                    last.then_inc(osc_done, 1)

                def queries(i):
                    if l == 2:
                        return
                    act.wait_ge(q_done, CREDIT + i + 1)
                    for m in range(KD):
                        last = A(q[:, m, :], ps[:, 2 + m, :], ACT.Identity,
                                 bias=cols[:, V_ATT * l + V_Q + m:V_ATT * l + V_Q + m + 1])
                    last.then_inc(qsb_done, 1)

                def spread(i):
                    act.wait_ge(rd_done, CREDIT + i + 1)
                    A(rde[:, :, :].rearrange("p t (h i) -> p t h i", i=16),
                      rd[:, :, :].unsqueeze(3).broadcast_to([P, TPC, 2 * HH, 16]), ACT.Copy).then_inc(rde_done, 1)

                def body(b, cc, before=True, after=True):
                    i = NCH * a + CPB * b + cc
                    for n in range(8):
                        if n == 6 and before:
                            gated_out(i - 1)
                        if n > 1:
                            turned(i, n - 2)
                        exponentials(i, n)
                        if n == 2 and before:
                            spread(i - 1)
                    numerators(i, 0)
                    turned(i, 6)
                    turned(i, 7)
                    if after:
                        queries(i + 1)
                    numerators(i, 1)

                queries(NCH * a)
                over_chunks(act, body)
                i = NCH * (a + 1) - 1
                spread(i)
                gated_out(i)

            def single():
                for b in range(NB):
                    with act.Fori(0, CPB) as cc:
                        i = CPB * b + cc
                        act.wait_ge(q1_done, CREDIT + i + 1)
                        for m in range(KD):
                            last = A(q[:, m, :], ps[:, m, :], ACT.Identity,
                                     bias=cols[:, V_ATT + V_Q + m:V_ATT + V_Q + m + 1])
                        last.then_inc(qsb1_done, 1)
                        act.wait_ge(neg1_done, CREDIT + i + 1)
                        act.wait_ge(pt_done, CREDIT + i)
                        for t in range(TPC):
                            last = A(p1[:, t, 0:KEYS], ps[:, 2, t * KP:t * KP + KEYS], ACT.Exp, bias=neg4[:, 0, t:t + 1],
                                     scale=1.0 / 16, accum_out=neg4[:, 1, t:t + 1])
                        last.then_inc(exp1_done, 1)
                        act.wait_ge(pt_done, CREDIT + i + 1)
                        A(pt[0:KEYS, :], ps[0:KEYS, 3, :], ACT.Copy).then_inc(ptsb_done, 1)
                        act.wait_ge(att1_done, CREDIT + i + 1)
                        act.wait_ge(x_done, CREDIT + NCH * 2 + i)
                        for m in range(KD):
                            last = A(osc[:, m, :], ps[:, 4 + m, :], ACT.Copy, scale=gts[:, 1:2])
                        last.then_inc(osc1_done, 1)

            def front(s, f, with_rows):
                with act.Fori(0, NCH) as c:
                    act.wait_ge(xn_done, CREDIT + NCH * s + c + 1)
                    act.wait_ge(front_done, CREDIT + NCH * f + c)
                    A(xc[:, :, :], xn[:, :, chunk(c)], ACT.Copy).then_inc(xc_done, 1)
                    if with_rows:
                        act.wait_ge(front_done, CREDIT + NCH * f + c + 1)
                        A(rows_[:, ds(c * TPC, TPC), :].rearrange("p t n -> p (t n)"),
                          ps[:, 1:3, :].rearrange("p b n -> p (b n)"), ACT.Copy).then_inc(rows_done, 1)

            def shared0():
                with act.Fori(0, NCH) as c:
                    for n in range(2 * IM):
                        m, lin = divmod(n, 2)
                        at = V_F0 + 2 * IM * lin + m
                        act.wait_ge(spair_done, CREDIT + 8 * c + n + 1)
                        A((al if lin else ag), ps[:, 2 * lin, :], ACT.Identity, bias=cols[:, at:at + 1]).then_inc(sa_done, 1)
                        if not lin:
                            act.wait_ge(spm_done, CREDIT + IM * c + m + 1)
                            act.wait_ge(sh_done, CREDIT + IM * c + m)
                            A(sig, pg, ACT.Sigmoid, scale=1.702).then_inc(ssig_done, 1)
                    act.wait_ge(so_done, CREDIT + c + 1)
                    act.wait_ge(sx_done, CREDIT + c)
                    for m in range(KD):
                        last = A(osc[:, m, :], ps[:, 6 + m, :], ACT.Identity, bias=gbo[:, 1, m:m + 1], scale=gts[:, 4:5])
                    last.then_inc(sosc_done, 1)

            def tile_rows(t, slot):
                act.wait_ge(xt_done, CREDIT + t + 1)
                A(xst[slot].rearrange("p k n -> p (k n)"), ps[:, 5, 0:KD * P], ACT.Copy).then_inc(xst_done, 1)

            def tiles0():
                def biased(dst, slot, lin, done, made):
                    act.wait_ge(done, made)
                    for m in range(IM):
                        at = W0 + 2 * IM * lin + m
                        last = A(dst[:, m * P:(m + 1) * P], ps[:, 2 * lin, m * P:(m + 1) * P], ACT.Identity,
                                 bias=w0[slot][:, at:at + 1])
                    last.then_inc(al_done if lin else ag_done, 1)

                def out(t, slot, use):
                    act.wait_ge(o2_done, CREDIT + t + 1)
                    if not (isinstance(use, int) and use == 0):
                        act.wait_ge(out_in[slot], 16 * use)
                    A(os_[slot], ps[:, 4, 0:D], ACT.Copy).then_inc(os_done, 1)

                def body(t, slot, use, before=True, after=True):
                    biased(ag, slot, 0, g_done, CREDIT + t + 1)
                    act.wait_ge(pgm_done, CREDIT + t + 1)
                    A(sig, pg, ACT.Sigmoid, scale=1.702).then_inc(sig_done, 1)
                    if before:
                        out(t - 1, (slot + 2) % 3, use - (slot == 0))
                    biased(al, slot, 1, l_done, CREDIT + t + 1)
                    if after:
                        tile_rows(t + 1, (slot + 1) % 3)

                tile_rows(0, 0)
                over_tiles(act, TILES0, lambda t, s_, u: body(t, s_, u, before=False), body,
                           lambda t, s_, u: body(t, s_, u, after=False))
                out(TILES0 - 1, (TILES0 - 1) % 3, (TILES0 - 1) // 3)

            def tiles1():
                def out(t, slot, use):
                    act.wait_ge(o2_done, CREDIT + TILES0 + t + 1)
                    act.wait_ge(out_in[slot], 16 * (TILES0 // 3 + use))
                    A(os_[slot], ps[:, 4, 0:D], ACT.Copy).then_inc(os_done, 1)

                def body(t, slot, use, before=True, after=True):
                    act.wait_ge(g_done, CREDIT + TILES0 + t + 1)
                    A(hh[slot][:, 0:CH], ps[:, 0, :], ACT.Relu).then_inc(ag_done, 1)
                    if before:
                        out(t - 1, (slot + 2) % 3, use - (slot == 0))
                    if after:
                        tile_rows(TILES0 + t + 1, (slot + 1) % 3)

                tile_rows(TILES0, 0)
                over_tiles(act, E1, lambda t, s_, u: body(t, s_, u, before=False), body,
                           lambda t, s_, u: body(t, s_, u, after=False))
                out(E1 - 1, (E1 - 1) % 3, (E1 - 1) // 3)

            def quantized():
                magic = cf[:, C_MAGIC:C_MAGIC + 1]
                act.wait_ge(xscale_done, 1)
                with act.Fori(0, NCH) as c:
                    A(xn[:, :, chunk(c)], xn[:, :, chunk(c)], ACT.Identity, bias=magic, scale=qv[:, 3:4]).then_inc(xrnd_done, 1)
                with act.Fori(0, NCH) as c:
                    for m in range(F2 // P):
                        act.wait_ge(m1_done, CREDIT + 8 * c + m + 1)
                        A(hbig[:, m, chunk(c)], ps[:, m, :], ACT.Relu, bias=qs[:, 4, m:m + 1], scale=qs[:, 2, m:m + 1]
                          ).then_inc(hact_done, 1)
                act.wait_ge(hscale_done, 1)
                with act.Fori(0, NCH) as c:
                    A(hbig[:, :, chunk(c)], hbig[:, :, chunk(c)], ACT.Identity, bias=magic, scale=qv[:, 7:8]).then_inc(hrnd_done, 1)
                with act.Fori(0, NCH) as c:
                    act.wait_ge(m2_done, CREDIT + c + 1)
                    act.wait_ge(x_done, CREDIT + NCH * 5 + c)
                    for m in range(KD):
                        last = A(osc[:, m, :], ps[:, m, :], ACT.Identity, bias=qs[:, 7, 2 + m:3 + m], scale=qs[:, 7, m:m + 1])
                    last.then_inc(osc2_done, 1)

            def experts3():
                act.wait_ge(front_done, CREDIT + NCH * 3)
                A(lg3[1].rearrange("p t e -> p (t e)"), ps[:, 0, 0:NT * 8], ACT.Sigmoid).then_inc(sig3_done, 1)
                act.wait_ge(combturn_done, 1)
                A(combT, ps[:, 1, 0:P], ACT.Copy).then_inc(combsb_done, 1)
                with act.Fori(0, NCH) as c:
                    for n in range(E3):
                        act.wait_ge(spair_done, CREDIT + 8 * NCH + E3 * c + n + 1)
                        A(sg3[:, n % 2, :], ps[:, 2 * (n % 2), :], ACT.Sigmoid).then_inc(ssig_done, 1)

            def route_exp(f, n_exp):
                act.wait_ge(smax_sub, f + 1)
                A(ra[1][:, 0:NT * n_exp], ra[0][:, 0:NT * n_exp], ACT.Exp).then_inc(smax_exp, 1)

            act.wait_ge(const_in, 16 * 10)
            A(gts[:, :], gts[:, :], ACT.Tanh).then_inc(tanh_done, 1)
            act.wait_ge(gbo_done, 1)
            for s in range(stages):
                l = s // 2
                if s % 2 == 0 and l in MHA:
                    act.wait_ge(v80_done, MHA.index(l) + 1)
                    A(v80[0:KP, :, :], ps[0:KP, 4:6, 0:D], ACT.Copy).then_inc(v80sb_done, 1)
                if s == 5:
                    act.wait_ge(wturn_done, 1)
                    A(wt1q.rearrange("p k n -> p (k n)"), ps[:, 0:2, :].rearrange("p b n -> p (b n)").bitcast(BF16), ACT.Copy)
                    A(wt2q.rearrange("p k n -> p (k n)"), ps[:, 2:4, :].rearrange("p b n -> p (b n)").bitcast(BF16), ACT.Copy
                      ).then_inc(wturned_done, 1)
                if s == 2:
                    act.wait_ge(kv1_done, 1)
                    A(v80[0:KP, :, :], ps[0:KP, 4:6, 0:D], ACT.Copy).then_inc(kv1sb_done, 1)
                layer_norm(s)
                if s == 2:
                    single()
                if s % 2 == 0 and l in MHA:
                    heads(l)
                if s == 5:
                    quantized()
                if s == 7:
                    front(7, 2, False)
                    experts3()
                if s == 1:
                    front(1, 0, True)
                    route_exp(0, R0)
                    shared0()
                    tiles0()
                if s == 3:
                    front(3, 1, True)
                    route_exp(1, E1)
                    tiles1()

        @block.gpsimd
        def _(pool):
            def heads(l):
                a = MHA.index(l)

                def body(b, cc):
                    i = NCH * a + CPB * b + cc
                    for hf in range(KD):
                        s0, s1 = psum_[:, hf, 0, :], psum_[:, hf, 1, :]
                        pool.wait_ge(turned_done, CREDIT + 8 * i + TPC * (hf + 1))
                        pool.wait_ge(den_done, CREDIT + i)
                        nc.gpsimd.tensor_tensor(psum_[:, hf, :, :], ptk[:, hf, 0:2, :], ptk[:, hf, 2:4, :], ALU.add
                                                ).then_inc(padd_done, 1)
                        pool.wait_ge(padd_done, CREDIT + 6 * i + 3 * hf + 1)
                        nc.gpsimd.tensor_tensor(s0, s0, s1, ALU.add).then_inc(padd_done, 1)
                        pool.wait_ge(padd_done, CREDIT + 6 * i + 3 * hf + 2)
                        nc.gpsimd.tensor_tensor(s0, s0, ptk[:, hf, 4, :], ALU.add).then_inc(padd_done, 1)

                for b in range(NB):
                    with pool.Fori(0, CPB) as cc:
                        body(b, cc)

            def scatter(dst, index, rest):
                for t in range(NT):
                    nc.gpsimd.indirect_dma_start(dst, bass.IndirectOffsetOnAxis(index[:, t:t + 1], 0), rows_[:, t, :], None
                                                 ).then_inc(scat_in, 16)

            def gather(dst, src, index, c):
                for t in range(c * TPC, (c + 1) * TPC):
                    nc.gpsimd.indirect_dma_start(dst[:, t, :], None, src, bass.IndirectOffsetOnAxis(index[:, t:t + 1], 0)
                                                 ).then_inc(gath_in[c], 16)

            nc.gpsimd.memset(zero[:, :], 0.0).then_inc(zero_set, 1)
            for s in range(stages):
                l = s // 2
                pool.wait_ge(eps_done, s + 1)
                nc.gpsimd.tensor_tensor(stat[:, 1, :], stat[:, 0, :], cf[:, C_MHALF:C_MHALF + NT],
                                        ALU.pow).then_inc(pow_done, 1)
                if s % 2 == 0 and l in MHA:
                    heads(l)
                if s == 5:
                    for n in range(2):
                        pool.wait_ge(tmax_done, n + 1)
                        nc.gpsimd.partition_all_reduce(qv[:, 1 + 4 * n:2 + 4 * n], qv[:, 4 * n:1 + 4 * n], P, RMAX
                                                       ).then_inc(allmax_done, 1)
                if s == 1:
                    pool.wait_ge(zeros_in, 32)
                    pool.wait_ge(rows_done, CREDIT + NCH)
                    pool.wait_ge(index_done, 1)
                    scatter(disp, gix1, 0)
                    scatter(disp, gix2, 0)
                    pool.wait_ge(scat_in, 16 * 2 * NT)
                    for n in range(3):
                        pool.wait_ge(out_in[n], 16 * (TILES0 // 3))
                    for c in range(NCH):
                        gather(ga, outs, gix1, c)
                        gather(gb, outs, gix2, c)
                if s == 3:
                    pool.wait_ge(rows_done, CREDIT + NCH * 2)
                    pool.wait_ge(index_done, 2)
                    scatter(disp1, six, 0)
                    pool.wait_ge(scat_in, 16 * 3 * NT)
                    for n in range(3):
                        pool.wait_ge(out_in[n], 16 * (TILES0 // 3 + (E1 + 2 - n) // 3))
                    for c in range(NCH):
                        gather(ga, outs1, gix1, c)

        @block.vector
        def _(dve):
            V = nc.vector
            count = [0]

            def link(ins):
                count[0] += 1
                ins.then_inc(step, 1)
                dve.wait_ge(step, count[0])

            def layer_norm(s):
                b0 = CREDIT + NCH * s
                with dve.Fori(0, NCH) as c:
                    dve.wait_ge(mean_done, b0 + c + 1)
                    V.tensor_tensor(xn[:, :, chunk(c)], x[:, :, chunk(c)],
                                    ps[:, ds(c, 1), :].broadcast_to([P, KD, CH]), ALU.subtract).then_inc(cent_done, 1)
                dve.wait_ge(var_done, b0 + NCH)
                V.tensor_scalar(stat[:, 0, :], ps[:, 4, 0:NT], EPS, None, ALU.add).then_inc(eps_done, 1)
                dve.wait_ge(pow_done, s + 1)
                link(V.tensor_tensor(stat[:, 2, :], stat[:, 1, :], stat[:, 1, :], ALU.mult))
                link(V.tensor_tensor(stat[:, 3, :], stat[:, 2, :], stat[:, 0, :], ALU.mult))
                link(V.tensor_scalar(stat[:, 2, :], stat[:, 3, :], -0.5, 1.5, ALU.mult, ALU.add))
                V.tensor_tensor(stat[:, 1, :], stat[:, 1, :], stat[:, 2, :], ALU.mult).then_inc(rstd_done, 1)
                with dve.Fori(0, NCH) as c:
                    dve.wait_ge(rstdb_done, b0 + c + 1)
                    V.tensor_tensor(xn[:, :, chunk(c)], xn[:, :, chunk(c)],
                                    ps[:, ds(c + 4, 1), :].broadcast_to([P, KD, CH]), ALU.mult).then_inc(xn_done, 1)

            def kv(l):
                a = MHA.index(l)
                v0 = V_ATT * l
                if l != 0:
                    dve.wait_ge(mask_in, 16 * (l - 1))
                    how = (NEG, None, ALU.mult) if l == 2 else (0.0, NEG, ALU.is_equal, ALU.mult)
                    V.tensor_scalar(mtok[:, :, 0:KEYS], mtok_raw[l][:, :, 0:KEYS], *how)
                    V.memset(mtok[:, :, KEYS:KP], FLOOR).then_inc(mask_done, 1)
                if l == 2:
                    dve.wait_ge(rope_in, 16)
                dve.wait_ge(k_done, a + 1)
                for m in range(KD):
                    if l == 2:
                        r = [rt[:, n, 0:NB * KP].rearrange("p (b k) -> p b k", b=NB) for n in range(2)]
                        for n, w in enumerate((V_K, V_KS)):
                            link(V.tensor_scalar(r[n], ps[:, 2 * n + m, 0:NB * KP].rearrange("p (b k) -> p b k", b=NB),
                                                 cols[:, v0 + w + m:v0 + w + m + 1], None, ALU.add))
                            link(V.tensor_tensor(r[n], r[n], rope[:, n:n + 1, 0:KP].broadcast_to([P, NB, KP]), ALU.mult))
                        link(V.tensor_tensor(kt[:, m, :], rt[:, 0, 0:NB * KP], rt[:, 1, 0:NB * KP], ALU.add))
                    else:
                        link(V.tensor_scalar(kt[:, m, :], ps[:, m, 0:NB * KP], cols[:, v0 + V_K + m:v0 + V_K + m + 1],
                                             0.25, ALU.add, ALU.mult))
                V.sem_inc(kt_done, 1)
                V.memset(kbd[:, :, :, :, KEYS:KP].rearrange("p m b h k -> p (m b h) k"), 0.0)
                V.memset(dif[:, :, :, KEYS:KP].rearrange("p n h k -> p (n h) k"), FLOOR)
                for m in range(KD):
                    for b in range(NB):
                        last = V.tensor_tensor(kbd[:, m, b, :, 0:KEYS],
                                               kt[:, m:m + 1, b * KP:b * KP + KEYS].broadcast_to([P, HH, KEYS]),
                                               blk.unsqueeze(2).broadcast_to([P, HH, KEYS]), ALU.mult)
                last.then_inc(kbd_done, 1)
                for n in range(NB * JG):
                    b, j = divmod(n, JG)
                    bank, half = (6, 7, 4, 5, 0)[n // 2], n % 2
                    dve.wait_ge(vrep_done, NB * JG * a + n - half + 2)
                    V.tensor_tensor(vbd[:, b, j, :].rearrange("p (m h i) -> p m h i", m=KD, i=16),
                                    ps[:, bank, half * D:(half + 1) * D].rearrange("p (m h i) -> p m h i", m=KD, i=16),
                                    blk.unsqueeze(1).unsqueeze(3).broadcast_to([P, KD, HH, 16]),
                                    ALU.mult).then_inc(vbd_done, 1)

            def heads(l):
                a = MHA.index(l)

                def rotate(i, cc):
                    dve.wait_ge(q_done, CREDIT + i + 1)
                    for m in range(KD):
                        for n, w in enumerate((V_Q, V_QS)):
                            k_ = V_ATT * l + w + m
                            if m:
                                dve.wait_ge(rope_done, CREDIT + 6 * (i - NCH) + 3)
                            V.scalar_tensor_tensor(rt[:, n, :], ps[:, (2, 0)[n] + m, :], cols[:, k_:k_ + 1],
                                                   rope[:, n, ds(cc * CH, CH)], ALU.add, ALU.mult
                                                   ).then_inc(rope_done, 1)
                        dve.wait_ge(rope_done, CREDIT + 6 * (i - NCH) + 3 * m + 2)
                        V.tensor_tensor(q[:, m, :], rt[:, 0, :], rt[:, 1, :], ALU.add).then_inc(rope_done, 1)
                    dve.wait_ge(rope_done, CREDIT + 6 * (i - NCH) + 6)
                    V.sem_inc(qsb_done, 1)

                def subtract(i, n):
                    hf, t = divmod(n, TPC)
                    bank = 2 * ((n + 1) % 2)
                    heads_ = slice(HH * hf, HH * (hf + 1))
                    sc = ps[:, bank:bank + 2, 0:SL].rearrange("p g (h k) -> p g h k", k=KP)
                    dve.wait_ge(score_done, CREDIT + 8 * i + n + 1)
                    m_ = smax[:, t, heads_].rearrange("p (g h) -> p g h", g=2)
                    V.tensor_reduce(m_, sc[:, :, :, 0:KEYS] if l == 0 else sc, AX.X, ALU.max).then_inc(max_done, 1)
                    dve.wait_ge(max_done, CREDIT + 8 * i + n + 1)
                    dve.wait_ge(exp_done, CREDIT + 8 * i + max(n - 1, 0))
                    V.tensor_tensor(dif[:, n % 2, :, 0:KEYS].rearrange("p (g h) k -> p g h k", g=2), sc[:, :, :, 0:KEYS],
                                    m_.unsqueeze(3).broadcast_to([P, 2, 4, KEYS]), ALU.subtract).then_inc(sub_done, 1)

                def invert(i):
                    dve.wait_ge(den_done, CREDIT + i + 1)
                    V.tensor_scalar(ssum[:, :, :], ps[:, 6, 0:TPC * 16].rearrange("p (t h) -> p t h", t=TPC),
                                    1e-30 if l == 2 else 0.0, None, ALU.max).then_inc(clamp_done, 1)
                    dve.wait_ge(clamp_done, CREDIT + i + 1)
                    V.reciprocal(rd[:, :, :], ssum[:, :, :]).then_inc(rd_done, 1)

                def divide(i):
                    dve.wait_ge(rb_done, CREDIT + i + 1)
                    V.tensor_tensor(o[:, :, :], num[:, :, :], ps[:, 6:8, :], ALU.mult).then_inc(o_done, 1)

                def body(b, cc, before=True, after=True):
                    c = CPB * b + cc
                    i = NCH * a + c
                    if l == 2:
                        rotate(i, cc)
                    for n in range(8):
                        subtract(i, n)
                        if n == 2 and before:
                            invert(i - 1)
                        if n == 4 and before:
                            divide(i - 1)
                    if before:
                        dve.wait_ge(osc_done, CREDIT + i)
                        add_residual(c - 1)

                over_chunks(dve, body)
                i = NCH * (a + 1) - 1
                invert(i)
                divide(i)
                dve.wait_ge(osc_done, CREDIT + i + 1)
                add_residual(NCH - 1)

            def single():
                for b in range(NB):
                    with dve.Fori(0, CPB) as cc:
                        i = CPB * b + cc
                        dve.wait_ge(score1_done, CREDIT + i + 1)
                        sc = ps[:, 2, 0:TPC * KP].rearrange("p (t k) -> p t k", t=TPC)
                        V.tensor_reduce(neg4[:, 2, :], sc[:, :, 0:KEYS], AX.X, ALU.max).then_inc(max1_done, 1)
                        dve.wait_ge(max1_done, CREDIT + i + 1)
                        V.tensor_scalar(neg4[:, 0, :], neg4[:, 2, :], -1.0 / 16, None, ALU.mult).then_inc(neg1_done, 1)
                        dve.wait_ge(exp1_done, CREDIT + i + 1)
                        V.reciprocal(neg4[:, 2, :], neg4[:, 1, :]).then_inc(rd1_done, 1)
                        dve.wait_ge(rd1_done, CREDIT + i + 1)
                        V.tensor_tensor(p1[:, :, 0:KEYS], p1[:, :, 0:KEYS],
                                        neg4[:, 2, :].unsqueeze(2).broadcast_to([P, TPC, KEYS]), ALU.mult).then_inc(p1_done, 1)
                        dve.wait_ge(osc1_done, CREDIT + i + 1)
                        add_residual(i)

            def add_residual(c):
                V.tensor_tensor(x[:, :, chunk(c)], x[:, :, chunk(c)], osc[:, :, :], ALU.add).then_inc(x_done, 1)

            def kv_single():
                dve.wait_ge(kv1_done, 1)
                for m in range(KD):
                    last = V.tensor_scalar(kt[:, m, :], ps[:, m, 0:NB * KP],
                                           cols[:, V_ATT + V_K + m:V_ATT + V_K + m + 1], None, ALU.add)
                last.then_inc(kv1sb_done, 1)

            def wide(v, n):
                return v.unsqueeze(2).broadcast_to([P, v.shape[1], n])

            def top(val, oh, n, t1, t2, m):
                link(V.tensor_reduce(m, val, AX.X, ALU.max))
                link(V.tensor_tensor(t1, val, wide(m, n), ALU.is_equal))
                link(V.tensor_tensor(t2, t1, cf[:, C_TIE:C_TIE + n].unsqueeze(1).broadcast_to([P, NT, n]), ALU.mult))
                link(V.tensor_reduce(m, t2, AX.X, ALU.max))
                link(V.tensor_tensor(oh, t2, wide(m, n), ALU.is_equal))

            def dot(dst, a_, b_, tmp):
                link(V.tensor_tensor(tmp, a_, b_, ALU.mult))
                link(V.tensor_reduce(dst, tmp, AX.X, ALU.add))

            def views(n_exp):
                return [a_[:, 0:NT * n_exp].rearrange("p (t e) -> p t e", e=n_exp) for a_ in ra + [oh1, oh2]]

            def bias_row(v, n):
                return v.unsqueeze(1).broadcast_to([P, NT, n])

            def probabilities(f, n_exp, r):
                logits = ps[:, 0, 0:NT * n_exp].rearrange("p (t e) -> p t e", e=n_exp)
                dve.wait_ge(front_done, CREDIT + NCH * (f + 1))
                link(V.tensor_reduce(rv[0], logits, AX.X, ALU.max))
                V.tensor_tensor(r[0], logits, wide(rv[0], n_exp), ALU.subtract).then_inc(smax_sub, 1)
                dve.wait_ge(smax_exp, f + 1)
                link(V.tensor_reduce(rv[1], r[1], AX.X, ALU.add))
                link(V.reciprocal(rv[1], rv[1]))

            def route0():
                n = R0
                r = views(n)
                o1, o2 = r[6], r[7]
                probabilities(0, n, r)
                link(V.tensor_tensor(r[2], r[1], wide(rv[1], n), ALU.mult))
                link(V.tensor_tensor(r[3], r[2], bias_row(gate_b[:, 0, :], n), ALU.add))
                top(r[3], o1, n, r[4], r[5], rv[2])
                link(V.scalar_tensor_tensor(r[0], o1, NEG, r[3], ALU.mult, ALU.add))
                top(r[0], o2, n, r[4], r[5], rv[2])
                V.tensor_tensor(mb16f[0], o1, o2, ALU.add).then_inc(pick_done, 1)
                for w, o_ in ((wt1, o1), (wt2, o2)):
                    dot(rv[3], r[2], o_, r[4])
                    link(V.tensor_scalar(w, rv[3], gts[:, 4:5], None, ALU.mult))
                dve.wait_ge(rank_done, 1)
                link(V.tensor_copy(e8[0], ps[:, 4, 0:n]))
                link(V.tensor_tensor(cmp8, e8[0].unsqueeze(2).broadcast_to([P, n, 16]),
                                     cf[:, C_STEP:C_STEP + 16].unsqueeze(1).broadcast_to([P, n, 16]), ALU.is_gt))
                link(V.tensor_reduce(e8[1], cmp8, AX.X, ALU.add))
                link(V.tensor_tensor(cmp8[:, :, 0:8], cf[:, C_LT:C_LT + 64].rearrange("p (a b) -> p a b", a=8),
                                     e8[1].unsqueeze(1).broadcast_to([P, 8, 8]), ALU.mult))
                link(V.tensor_reduce(e8[2], cmp8[:, :, 0:8], AX.X, ALU.add))
                link(V.tensor_scalar(e8[3], e8[2], float(P), None, ALU.mult))
                V.tensor_tensor(r[0], ps[:, 3, 0:NT * n].rearrange("p (t e) -> p t e", e=n), bias_row(e8[3], n),
                                ALU.add).then_inc(rank_read, 1)
                dve.wait_ge(rank_read, 1)
                dot(rv[4], r[0], o1, r[4])
                dot(rv[5], r[0], o2, r[4])
                link(V.tensor_copy(gix1, rv[4]))
                V.tensor_copy(gix2, rv[5]).then_inc(index_done, 1)
                link(V.tensor_tensor(e8[0], e8[1], e8[2], ALU.add))
                link(V.tensor_tensor(cmpt, e8[0].unsqueeze(1).broadcast_to([P, TILES0, 8]),
                                     cf[:, C_TILE:C_TILE + TILES0].unsqueeze(2).broadcast_to([P, TILES0, 8]), ALU.is_le))
                link(V.tensor_reduce(texf, cmpt, AX.X, ALU.add))
                V.tensor_scalar(tex, texf, float(R0 - 1), None, ALU.min).then_inc(texp_done, 1)

            def route1():
                n = E1
                r = views(n)
                o1 = r[6]
                probabilities(1, n, r)
                link(V.tensor_scalar(r[2], r[0], 0.0, None, ALU.add))
                top(r[2], o1, n, r[4], r[5], rv[2])
                V.tensor_copy(mb16f[1], o1).then_inc(pick_done, 1)
                dot(rv[3], o1, bias_row(cf[:, C_IDX:C_IDX + n], n), r[4])
                dve.wait_ge(rank_done, 2)
                V.tensor_tensor(r[3], ps[:, 3, 0:NT * n].rearrange("p (t e) -> p t e", e=n), o1, ALU.mult
                                ).then_inc(rank_read, 1)
                dve.wait_ge(rank_read, 2)
                link(V.tensor_reduce(rv[4], r[3], AX.X, ALU.add))
                link(V.tensor_scalar(rv[5], rv[4], float(C1), None, ALU.is_lt))
                link(V.tensor_scalar(rv[4], rv[4], float(C1 - 1), None, ALU.min))
                link(V.scalar_tensor_tensor(rv[6], rv[3], float(C1), rv[4], ALU.mult, ALU.add))
                link(V.tensor_copy(gix1, rv[6]))
                tok = cf[:, C_TOK:C_TOK + NT]
                link(V.tensor_tensor(rv[7], rv[6], tok, ALU.subtract))
                link(V.tensor_tensor(rv[7], rv[7], rv[5], ALU.mult))
                link(V.tensor_tensor(rv[7], rv[7], tok, ALU.add))
                V.tensor_copy(six, rv[7]).then_inc(index_done, 1)
                link(V.tensor_tensor(rv[5], rv[5], rv[1], ALU.mult))
                link(V.tensor_scalar(wt1, rv[5], gts[:, 5:6], None, ALU.mult))

            def round_weights():
                dve.wait_ge(wq_in, 32)
                for i, (dst, n, w) in enumerate(((wq1, F2 // P, D), (wq2, KD, F2))):
                    raw = wq_raw[:, 2048 * i:2048 * (i + 1)].rearrange("p (a b) -> p a b", a=n)
                    sw, inv = qs[:, i, 0:n], qs[:, 3, 0:n]
                    link(V.tensor_reduce(sw, raw, AX.X, ALU.max, apply_absolute_value=True))
                    link(V.tensor_scalar(sw, sw, 1e-8, 1.0 / 127, ALU.max, ALU.mult))
                    link(V.reciprocal(inv, sw))
                    link(V.tensor_tensor(raw, raw, wide(inv, w), ALU.mult))
                    link(V.tensor_scalar(raw, raw, MAGIC, MAGIC, ALU.add, ALU.subtract))
                    link(V.tensor_scalar(dst, raw, 127.0, -128.0, ALU.min, ALU.max))
                V.sem_inc(wround_done, 1)

            def scales(n, width, bias_at, sw, ss, qb):
                dve.wait_ge(allmax_done, n + 1)
                o_ = 4 * n
                link(V.tensor_scalar(qv[:, o_ + 2:o_ + 3], qv[:, o_ + 1:o_ + 2], 1e-8, 1.0 / 255, ALU.max, ALU.mult))
                link(V.reciprocal(qv[:, o_ + 3:o_ + 4], qv[:, o_ + 2:o_ + 3]))
                inv = qs[:, 3, 0:width]
                link(V.tensor_scalar(ss, sw, qv[:, o_ + 2:o_ + 3], None, ALU.mult))
                link(V.reciprocal(inv, ss))
                link(V.tensor_tensor(inv, inv, cols[:, bias_at:bias_at + width], ALU.mult))
                link(V.tensor_scalar(inv, inv, MAGIC, MAGIC, ALU.add, ALU.subtract))
                link(V.tensor_tensor(qb, inv, ss, ALU.mult))

            def quantized():
                dve.wait_ge(xn_done, CREDIT + NCH * 6)
                V.tensor_reduce(qv[:, 0:1], xn[:, :, :], AX.XY, ALU.max).then_inc(tmax_done, 1)
                scales(0, F2 // P, V_F2, qs[:, 0, :], qs[:, 2, :], qs[:, 4, :])
                V.sem_inc(xscale_done, 1)
                with dve.Fori(0, NCH) as c:
                    dve.wait_ge(xrnd_done, CREDIT + c + 1)
                    V.tensor_scalar(xn[:, :, chunk(c)], xn[:, :, chunk(c)], MAGIC, MAGIC + 255, ALU.max, ALU.min
                                    ).then_inc(xclip_done, 1)
                    dve.wait_ge(xclip_done, CREDIT + c + 1)
                    V.tensor_scalar(xq[:, :, chunk(c)], xn[:, :, chunk(c)], MAGIC, None, ALU.subtract).then_inc(xq_done, 1)
                with dve.Fori(0, NCH) as c:
                    dve.wait_ge(hact_done, CREDIT + 4 + 8 * c + 8)
                    last = V.tensor_reduce(qs[:, 5, ds(c, 1)], hbig[:, :, chunk(c)], AX.XY, ALU.max).then_inc(hmax_done, 1)
                dve.wait_ge(hmax_done, CREDIT + NCH)
                V.tensor_reduce(qv[:, 4:5], qs[:, 5, 0:NCH], AX.X, ALU.max).then_inc(tmax_done, 1)
                scales(1, KD, V_F2 + F2 // P, qs[:, 1, 0:KD], qs[:, 6, 0:KD], qs[:, 6, KD:2 * KD])
                link(V.tensor_scalar(qs[:, 7, 0:2 * KD], qs[:, 6, 0:2 * KD], gts[:, 6:7], None, ALU.mult))
                V.sem_inc(hscale_done, 1)
                with dve.Fori(0, NCH) as c:
                    dve.wait_ge(hrnd_done, CREDIT + c + 1)
                    V.tensor_scalar(hq[:, :, chunk(c)], hbig[:, :, chunk(c)], MAGIC, 255.0, ALU.subtract, ALU.min
                                    ).then_inc(hq_done, 1)
                with dve.Fori(0, NCH) as c:
                    dve.wait_ge(osc2_done, CREDIT + c + 1)
                    add_residual(c)

            def route3():
                n, half = 8, 4
                sf, tmp, o1, rest, o2, ta, tb = lg3[2], lg3[3], lg3[4], lg3[5], lg3[6], lg3[7], lg3[0]
                dve.wait_ge(sig3_done, 1)
                link(V.tensor_tensor(sf, lg3[1], bias_row(gate_b[:, 1, :], n), ALU.add))
                pairs = sf.rearrange("p t (g i) -> p (t g) i", i=2)
                link(V.tensor_reduce(gr[0].rearrange("p t g -> p (t g)"), pairs, AX.X, ALU.add))
                top(gr[0], gr[1], half, gr[5], gr[6], rv3[0])
                link(V.scalar_tensor_tensor(gr[2], gr[1], NEG, gr[0], ALU.mult, ALU.add))
                top(gr[2], gr[3], half, gr[5], gr[6], rv3[0])
                link(V.tensor_tensor(gr[4], gr[1], gr[3], ALU.add))
                link(V.tensor_tensor(tmp.rearrange("p t (g i) -> p (t g) i", i=2), pairs,
                                     wide(gr[4].rearrange("p t g -> p (t g)"), 2), ALU.mult))
                top(tmp, o1, n, ta, tb, rv3[0])
                link(V.scalar_tensor_tensor(rest, o1, NEG, tmp, ALU.mult, ALU.add))
                top(rest, o2, n, ta, tb, rv3[0])
                dot(rv3[1], sf, o1, ta)
                dot(rv3[2], sf, o2, ta)
                link(V.tensor_tensor(rv3[3], rv3[1], rv3[2], ALU.add))
                link(V.tensor_scalar(rv3[3], rv3[3], 1e-20, None, ALU.add))
                link(V.reciprocal(rv3[4], rv3[3]))
                link(V.tensor_scalar(rv3[4], rv3[4], 2.5, gts[:, 7:8], ALU.mult, ALU.mult))
                link(V.tensor_tensor(rv3[1], rv3[1], rv3[4], ALU.mult))
                link(V.tensor_tensor(rv3[2], rv3[2], rv3[4], ALU.mult))
                link(V.tensor_tensor(ta, o1, wide(rv3[1], n), ALU.mult))
                link(V.tensor_tensor(tb, o2, wide(rv3[2], n), ALU.mult))
                V.tensor_tensor(combt.rearrange("p e t -> p t e"), ta, tb, ALU.add).then_inc(comb3_done, 1)

            def experts3():
                with dve.Fori(0, NCH) as c:
                    for n in range(E3):
                        i = E3 * c + n
                        e = ORDER3[n]
                        dve.wait_ge(ssig_done, CREDIT + IM * NCH + i + 1)
                        V.tensor_tensor(t3, sg3[:, n % 2, :], ps[:, 2 * (n % 2), :], ALU.mult).then_inc(spc_done, 1)
                        dve.wait_ge(spc_done, CREDIT + IM * NCH + i + 1)
                        V.tensor_tensor(u3, t3, ps[:, 2 * (n % 2) + 1, :], ALU.mult).then_inc(su_done, 1)
                        dve.wait_ge(su_done, CREDIT + IM * NCH + i + 1)
                        dve.wait_ge(so_done, CREDIT + NCH + E3 * c + max(n - 1, 0))
                        if e == 0:
                            dve.wait_ge(combb_in, 16 * 8 * (c + 1))
                        if e < 8:
                            V.tensor_tensor(h3[:, n % 2, :], u3, combb[:, e, chunk(c)], ALU.mult).then_inc(sh_done, 1)
                        else:
                            V.tensor_scalar(h3[:, n % 2, :], u3, gts[:, 7:8], None, ALU.mult).then_inc(sh_done, 1)
                    dve.wait_ge(so_done, CREDIT + NCH + E3 * c + E3)
                    V.tensor_tensor(x[:, :, chunk(c)], x[:, :, chunk(c)], ps[:, 4:6, :], ALU.add).then_inc(x_done, 1)

            def shared0():
                with dve.Fori(0, NCH) as c:
                    for n in range(2 * IM):
                        m, lin = divmod(n, 2)
                        at = V_F0 + 2 * IM * lin + IM + m
                        dve.wait_ge(sa_done, CREDIT + 8 * c + n + 1)
                        V.scalar_tensor_tensor((pl if lin else pg), ps[:, 2 * lin + 1, :], cols[:, at:at + 1],
                                               (al if lin else ag), ALU.add, ALU.mult).then_inc(sp_done, 1)
                        dve.wait_ge(sp_done, CREDIT + 8 * c + n + 1)
                        if not lin:
                            V.tensor_scalar(pg, pg, 7.0, None, ALU.min).then_inc(spm_done, 1)
                        else:
                            i = IM * c + m
                            V.tensor_scalar(pl, pl, 7.0, -7.0, ALU.min, ALU.max).then_inc(spc_done, 1)
                            dve.wait_ge(spc_done, CREDIT + i + 1)
                            V.scalar_tensor_tensor(uu, pl, 1.0, pg, ALU.add, ALU.mult).then_inc(su_done, 1)
                            dve.wait_ge(su_done, CREDIT + i + 1)
                            dve.wait_ge(ssig_done, CREDIT + i + 1)
                            V.tensor_tensor(hs[:, m, :], uu, sig, ALU.mult).then_inc(sh_done, 1)
                    dve.wait_ge(sosc_done, CREDIT + c + 1)
                    V.tensor_tensor(x[:, :, chunk(c)], x[:, :, chunk(c)], osc[:, :, :], ALU.add).then_inc(sx_done, 1)

            def tiles0():
                def products(dst, a_, slot, lin, done):
                    for m in range(IM):
                        at = W0 + 2 * IM * lin + IM + m
                        last = V.scalar_tensor_tensor(dst[:, m * P:(m + 1) * P], ps[:, 2 * lin + 1, m * P:(m + 1) * P],
                                                      w0[slot][:, at:at + 1], a_[:, m * P:(m + 1) * P], ALU.add, ALU.mult)
                    last.then_inc(done, 1)

                def body(t, slot, use):
                    dve.wait_ge(ag_done, CREDIT + t + 1)
                    products(pg, ag, slot, 0, pg_done)
                    dve.wait_ge(pg_done, CREDIT + t + 1)
                    V.tensor_scalar(pg, pg, 7.0, None, ALU.min).then_inc(pgm_done, 1)
                    dve.wait_ge(al_done, CREDIT + t + 1)
                    products(pl, al, slot, 1, pl_done)
                    dve.wait_ge(pl_done, CREDIT + t + 1)
                    V.tensor_scalar(pl, pl, 7.0, -7.0, ALU.min, ALU.max).then_inc(plc_done, 1)
                    dve.wait_ge(plc_done, CREDIT + t + 1)
                    V.scalar_tensor_tensor(uu, pl, 1.0, pg, ALU.add, ALU.mult).then_inc(u_done, 1)
                    dve.wait_ge(u_done, CREDIT + t + 1)
                    dve.wait_ge(sig_done, CREDIT + t + 1)
                    V.tensor_tensor(hh[slot][:, 0:CH], uu, sig, ALU.mult).then_inc(h_done, 1)

                over_tiles(dve, TILES0, body, body, body)

            def tiles1():
                def body(t, slot, use):
                    dve.wait_ge(l_done, CREDIT + TILES0 + t + 1)
                    V.tensor_scalar(hh[slot][:, CH:F1], ps[:, 2, :], 0.0, None, ALU.max).then_inc(pl_done, 1)

                over_tiles(dve, E1, body, body, body)

            def combine(f):
                for c in range(NCH):
                    n = NCH * f + c
                    sl = slice(c * TPC, (c + 1) * TPC)
                    dve.wait_ge(gath_in[c], 16 * TPC * (2 if f == 0 else 3))
                    if n:
                        dve.wait_ge(comb_done, CREDIT + n)
                    if f == 0:
                        link(V.tensor_tensor(yb, gb[:, sl, :], wide(wt2[:, sl], D), ALU.mult))
                        link(V.tensor_tensor(ya, ga[:, sl, :], wide(wt1[:, sl], D), ALU.mult))
                        V.tensor_tensor(ya, ya, yb, ALU.add).then_inc(y_done, 1)
                    else:
                        V.tensor_tensor(ya, ga[:, sl, :], wide(wt1[:, sl], D), ALU.mult).then_inc(y_done, 1)
                    dve.wait_ge(comb_done, CREDIT + n + 1)
                    V.tensor_tensor(x[:, :, c * CH:(c + 1) * CH], x[:, :, c * CH:(c + 1) * CH], ps[:, 0:2, :],
                                    ALU.add).then_inc(x_done, 1)

            dve.wait_ge(const_in, 16 * 10)
            V.tensor_copy(cb[:, :], cb_raw)
            dve.wait_ge(tanh_done, 1)
            for l in MHA:
                last = V.tensor_scalar(gbo[:, l, :], cols[:, V_ATT * l + V_O:V_ATT * l + V_O + KD], gts[:, l:l + 1], None,
                                       ALU.mult)
            last = V.tensor_scalar(gbo[:, 1, :], cols[:, V_F0 + 4 * IM:V_F0 + 4 * IM + KD], gts[:, 4:5], None, ALU.mult)
            last.then_inc(gbo_done, 1)
            for s in range(stages):
                l = s // 2
                if s % 2 == 0 and l in MHA:
                    kv(l)
                if s == 2:
                    kv_single()
                if s == 5:
                    round_weights()
                layer_norm(s)
                if s % 2 == 0 and l in MHA:
                    heads(l)
                if s == 2:
                    single()
                if s == 5:
                    quantized()
                if s == 7:
                    route3()
                    experts3()
                if s == 1:
                    route0()
                    shared0()
                    tiles0()
                    combine(0)
                if s == 3:
                    route1()
                    tiles1()
                    combine(1)


STAGES = 8


def kernel(**inputs):
    import concourse.bacc as bacc
    from concourse.bass_utils import run_bass_kernel_spmd

    arrays = host_layout(inputs)
    nc = bacc.Bacc("TRN2", target_bir_lowering=False, num_devices=1)
    dram = {n: nc.dram_tensor(f"in_{n}", a.shape, mybir.dt.from_np(a.dtype), kind="ExternalInput").ap()
            for n, a in arrays.items()}
    out = nc.dram_tensor("out_x", (P, KD, T), F32, kind="ExternalOutput").ap()
    program(nc, dram, out, STAGES)
    r = run_bass_kernel_spmd(nc, [{f"in_{n}": a for n, a in arrays.items()}], core_ids=[0])
    y = r.results[0]["out_x"]
    return np.ascontiguousarray(y.transpose(1, 0, 2).reshape(D, T).T.reshape(NB, S, D))
```

```python
from contextlib import ExitStack

import numpy as np

import concourse.bass as bass
from concourse import mybir

ALU = mybir.AluOpType
ACT = mybir.ActivationFunctionType
AX = mybir.AxisListType
F32 = mybir.dt.float32
BF16 = mybir.dt.bfloat16
I32 = mybir.dt.int32
U8 = mybir.dt.uint8
U32 = mybir.dt.uint32
ds = bass.ds
RMAX = bass.bass_isa.ReduceOp.max

P = 128
D = 256
KD = D // P
NB, S = 2, 1024
T = NB * S
CH = 512
NCH = T // CH
CPB = S // CH
TPC = CH // P
NT = T // P
KEYS = 77
KP = 80
JG = KP // 16
HH = 8
NEG = -3.0e38
FLOOR = -1.0e30
SL = 4 * KP
EPS = 1e-5
LN_STAGES = 8

C_ID, C_MEAN, C_ONE = 0, 128, 256
C_BLK, C_MHALF, C_TIE, C_IDX, C_SEL = 384, 392, 408, 424, 440
C_MAGIC = C_SEL + JG * P
C_TOK = C_MAGIC + 1
C_STEP = C_TOK + 16
C_LT = C_STEP + 16
C_TILE = C_LT + 64
C_N = C_TILE + 40
MAGIC = 12582912.0
B_ID, B_TRI, B_ONE = 0, 128, 256
B_N = B_ONE + 128
V_Q, V_K, V_O, V_QS, V_KS = 0, 2, 4, 6, 8
V_ATT = 10
V_F0 = 4 * V_ATT
E0, I0 = 9, 512
V_F2 = V_F0 + 4 * (I0 // P) + KD
F2 = 1024
V_N = V_F2 + F2 // P + KD
R0 = 8
W0 = KD * 4 * I0 + (I0 // P) * D
BC0 = 4 * (I0 // P)
TILES0 = (2 * T) // P + R0 - 1
E1, F1, C1 = 16, 1024, T // 16
E3 = 10
SPLIT = NCH // 2
SHARED3, ROUTED3 = [8, 9], list(range(8))
W_Q, W_K, W_V, W_O, W_QS, W_KS = range(6)


def host_constants():
    cf = np.zeros((P, C_N), np.float32)
    p = np.arange(P)
    cf[:, C_ID:C_ID + P] = np.eye(P)
    cf[:, C_MEAN:C_MEAN + P] = 1.0 / D
    cf[:, C_ONE:C_ONE + P] = 1.0
    cf[:, C_BLK:C_BLK + HH] = p[:, None] // 16 == np.arange(HH)
    cf[:, C_MHALF:C_MHALF + 16] = -0.5
    cf[:, C_TIE:C_TIE + 16] = 16 - np.arange(16)
    cf[:, C_IDX:C_IDX + 16] = np.arange(16)
    cf[:, C_MAGIC] = MAGIC
    cf[:, C_TOK:C_TOK + NT] = T + np.arange(NT) * P + p[:, None]
    cf[:, C_STEP:C_STEP + 16] = np.arange(16) * P
    cf[:, C_LT:C_LT + 64] = np.tril(np.ones((8, 8)), -1).reshape(-1)
    cf[:, C_TILE:C_TILE + 40] = np.arange(40)
    cb = np.zeros((P, B_N), np.float32)
    cb[:, B_ID:B_ID + P] = np.eye(P)
    for j in range(JG):
        hit = np.arange(KP)[:, None] == 16 * j + p[None] % 16
        cf[:KP, C_SEL + j * P:C_SEL + (j + 1) * P] = hit
    cb[:, B_TRI:B_TRI + P] = p[:, None] < p[None]
    cb[:, B_ONE:B_ONE + P] = 1.0
    freq = np.exp(np.arange(0, 16, 2, dtype=np.float32) * (-(np.float32(4.0) * np.log(np.float32(10.0))) / np.float32(16)))
    ang = np.arange(S, dtype=np.float32)[None, :] * freq.astype(np.float32)[(p % 16) // 2][:, None]
    sign = np.where(p % 2 == 0, 1.0, -1.0).astype(np.float32)
    rope = np.stack([np.sin(ang) * sign[:, None], -np.cos(ang)], 1).astype(np.float32)
    return cf, cb, rope


def host_layout(i):
    a = {k: np.asarray(v) for k, v in i.items()}

    def rows(w):
        return w.reshape(-1, P, w.shape[-1]).transpose(1, 0, 2)

    def col(v):
        return v.reshape(-1, P).T

    cf, cb, rope = host_constants()
    swap = np.arange(D) ^ 1
    pad = list(range(KEYS)) + list(range(KP - KEYS))
    o = {"cf": cf, "cb": cb, "rope": rope}
    o["x"] = rows(a["x"].reshape(T, D).T)
    o["ctx"] = rows(a["ctx_1024"][:, pad].reshape(NB * KP, D).T)
    L = lambda l, n: a[f"L{l}_xattn_{n}"]
    att = {0: [L(0, "Wq"), L(0, "Wk"), L(0, "Wv"), L(0, "Wo")],
           1: [L(1, "Wq").T, L(1, "Wk").T, L(1, "Wv").T],
           2: [L(2, "Wq").T, L(2, "Wk").T, L(2, "Wv").T, L(2, "Wo").T, L(2, "Wq").T[:, swap], L(2, "Wk").T[:, swap]],
           3: [L(3, "Wq").T, L(3, "Wk").T, L(3, "Wv").T, L(3, "Wo").T]}
    for l, ws in att.items():
        o[f"aw{l}"] = np.stack([rows(w) for w in ws], 1)
        o[f"bv{l}"] = L(l, "bv")[None]
    cols = []
    for l in range(4):
        bo = L(l, "bo") if l != 1 else L(l, "bq")
        cols += [col(L(l, "bq")), col(L(l, "bk")), col(bo), col(L(l, "bq")[swap]), col(L(l, "bk")[swap])]
    F = lambda l, n: a[f"L{l}_ffn_{n}"]
    w1 = np.concatenate([F(0, "w1"), F(0, "sw1")[None]])
    w3 = np.concatenate([F(0, "w3"), F(0, "sw3")[None]])
    w2 = np.concatenate([F(0, "w2"), F(0, "sw2")[None]])
    b1 = np.concatenate([F(0, "b1"), F(0, "sb1")[None]])
    b3 = np.concatenate([F(0, "b3"), F(0, "sb3")[None]])
    b2 = np.concatenate([F(0, "b2"), F(0, "sb2")[None]])
    o["f0w"] = np.stack([np.concatenate(
        [rows(w[e]).reshape(P, -1) for w in (w1[:, :, ::2], w3[:, :, ::2], w1[:, :, 1::2], w3[:, :, 1::2], w2)]
        + [col(v) for v in (b1[e, ::2], b3[e, ::2], b1[e, 1::2], b3[e, 1::2])], 1) for e in range(E0)])
    o["f0b"] = b2
    cols += [col(b1[R0, ::2]), col(b3[R0, ::2]), col(b1[R0, 1::2]), col(b3[R0, 1::2]), col(b2[R0])]
    cols += [col(F(2, "b1")), col(F(2, "b2"))]
    o["cols"] = np.concatenate(cols, 1)
    o["g"] = np.concatenate([a["g_xattn"], a["g_ffn"]])[None]
    o["gate0"] = rows(F(0, "gate_w").T)
    o["gb0"] = F(0, "gate_b")[None]
    o["gate1"] = rows(F(1, "Wg"))
    o["gate3"] = rows(F(3, "gate_w"))
    o["gb3"] = F(3, "gate_bias")[None]
    o["f1w"] = np.stack([np.concatenate([rows(F(1, "w1")[e]).reshape(P, -1), rows(F(1, "w2")[e]).reshape(P, -1)], 1)
                         for e in range(E1)])
    o["f2w1"] = rows(F(2, "w1"))
    o["f2w2"] = rows(F(2, "w2"))
    wg = list(F(3, "w_gate")) + [F(3, "sw_gate")[:, :P], F(3, "sw_gate")[:, P:]]
    wu = list(F(3, "w_up")) + [F(3, "sw_up")[:, :P], F(3, "sw_up")[:, P:]]
    wd = list(F(3, "w_down")) + [F(3, "sw_down")[:P], F(3, "sw_down")[P:]]
    o["f3w"] = np.stack([np.concatenate([rows(g).reshape(P, -1), rows(u).reshape(P, -1), d], 1)
                         for g, u, d in zip(wg, wu, wd)], 1)
    m2 = np.pad(a["mask_1x1xSxS2_bk1"][0, 0], ((0, 0), (0, KP - KEYS)), constant_values=True)
    m3 = np.pad(a["mask_SxS2_ik0"], ((0, 0), (0, KP - KEYS)))
    for n, m in (("2", m2), ("3", m3)):
        o["mtok" + n] = m.reshape(S // P, P, KP).transpose(1, 0, 2)
    return {k: np.ascontiguousarray(v) for k, v in o.items()}


def program(nc, d, out, stages):
    with ExitStack() as ctx:
        def sb(name, shape, dt=F32):
            return ctx.enter_context(nc.sbuf_tensor(name, shape, dt))

        sems = {}

        def sem(name):
            sems[name] = ctx.enter_context(nc.semaphore(name))
            return sems[name]

        def carver(arena):
            at = [0]

            def take(shape, dt=F32, parts=P):
                n = int(np.prod(shape))
                words = n if dt in (F32, I32, U32) else (n + 1) // 2 if dt == BF16 else (n + 3) // 4
                v = arena[0:parts, at[0]:at[0] + words]
                at[0] += words
                assert at[0] <= arena.shape[1], (at[0], arena.shape)
                if dt != F32:
                    v = v.bitcast(dt)
                if len(shape) > 1:
                    names = "abcde"[:len(shape)]
                    v = v.rearrange(f"p ({' '.join(names)}) -> p {' '.join(names)}",
                                    **{c: s for c, s in zip(names[1:], shape[1:])})
                return v
            return take

        x = sb("x_res", [P, KD, T])
        xn = sb("x_norm", [P, KD, T])
        cf = sb("const_f", [P, C_N])
        cb = sb("const_b", [P, B_N], BF16)
        cols = sb("cols_sb", [P, V_N])
        ctxk = sb("ctx_sb", [P, KD, NB * KP])
        gts = sb("gates_tanh", [P, 8])
        gbo = sb("gated_bias", [P, 4, KD])
        aw_even = sb("aw_even", [P, 6 * KD * D + D])
        aw_odd = sb("aw_odd", [P, 4 * KD * D + D])
        gate_w = sb("gate_w", [P, 3, KD * 16])
        gate_b = sb("gate_b", [P, 2, 8])
        mtok = sb("mask_tok", [P, S // P, KP], BF16)
        big = sb("big", [P, 16384])
        work = sb("work", [P, 18900])
        zero = sb("zero", [P, D])

        aw, bv = {}, {}
        for l in range(4):
            arena, n = (aw_even, (4, 0, 6)[l]) if l % 2 == 0 else (aw_odd, (0, 3, 0, 4)[l])
            aw[l] = arena[:, 0:n * KD * D].rearrange("p (w k n) -> p w k n", w=n, k=KD)
            bv[l] = arena[0:1, arena.shape[1] - D:arena.shape[1]]

        ident = cf[:, C_ID:C_ID + P]
        mean_w = cf[:, C_MEAN:C_MEAN + P]
        ones_row = cf[0:1, C_ONE:C_ONE + P]
        blk = cf[:, C_BLK:C_BLK + HH]
        identb = cb[:, B_ID:B_ID + P]

        ps = ctx.enter_context(nc.psum_tensor("ps", [P, 8, CH], F32))

        take = carver(work)
        sq = take([KD, CH])
        stat = take([4, NT])
        osc = take([KD, CH])
        turns = [sq, osc]
        kbd = take([KD, NB, HH, KP])
        vbd = take([NB, JG, D])
        v80 = take([NB, D])
        kt = take([KD, NB * KP])
        q = take([KD, CH])
        smax = take([TPC, 2 * HH])
        psum_ = take([KD, 2, CH])
        ssum = take([TPC, 2 * HH])
        rd = take([TPC, 2 * HH])
        rde = take([TPC, KD * P])
        dif = take([2, HH, KP])
        pm = take([2, JG, HH * 16])
        rt = take([2, CH])
        num = take([KD, CH])
        neg4 = take([3, TPC])
        p1 = take([TPC, KP])
        q1 = [q, num]
        pt = take([CH])
        o = take([KD, CH])
        take = carver(big)
        ptk = take([KD, JG, CH])
        cb_raw = big[:, KD * JG * CH:KD * JG * CH + B_N]
        rope = take([2, S])
        mtok_raw = {2: take([S // P, KP], U8), 3: take([S // P, KP], I32)}

        IM = I0 // P
        ring = carver(big)
        w0 = [ring([W0 + BC0]) for _ in range(3)]
        w1m = [w[:, 0:4096] for w in w0]
        hbig = big[:, 0:16384].rearrange("p (m t) -> p m t", m=F2 // P)
        combb = big[:, 0:16384].rearrange("p (e t) -> p e t", e=8)
        wq_raw = big[:, 8192:12288]
        wq_rounded = big[:, 12288:14336]

        take = carver(work)
        take([KD, CH]), take([4, NT]), take([KD, CH])
        rows_ = take([NT, D])
        ra = [take([NT * 16]) for _ in range(6)]
        rv = [take([NT]) for _ in range(8)]
        oh1, oh2 = take([NT * 16]), take([NT * 16])
        mb16 = take([NT, 16], BF16)
        wt1, wt2 = take([NT]), take([NT])
        gix1, gix2 = take([NT], U32), take([NT], U32)
        six = take([NT], U32)
        e8 = [take([8]) for _ in range(4)]
        cmp8 = take([8, 16])
        cmpt = take([TILES0, 8])
        texf, tex = take([TILES0]), take([TILES0], I32)
        b2row = [take([D]) for _ in range(3)]
        xs = [take([D]) for _ in range(3)]
        xst = [take([KD * P]).rearrange("p (k n) -> p k n", k=KD) for _ in range(3)]
        os_ = [take([D]) for _ in range(3)]
        tail = take([6 * CH + 3 * F1])
        ag, al, pg, pl, sig, uu = (tail[:, n * CH:(n + 1) * CH] for n in range(6))
        hall = tail[:, 6 * CH:]
        hh = [hall[:, n * F1:(n + 1) * F1] for n in range(3)]
        hs = hall[:, 0:IM * CH].rearrange("p (m n) -> p m n", m=IM)
        ga = rows_
        gb = w0[(TILES0 - 1) % 3][:, 0:NT * D].rearrange("p (t n) -> p t n", t=NT)

        take = carver(work)
        take([KD, CH]), take([4, NT]), take([KD, CH])
        take_r = carver(wq_rounded)
        wq1, wq2 = take_r([F2 // P, D], BF16), take_r([KD, F2], BF16)
        wt1q, wt2q = take([KD, F2], BF16), take([F2 // P, D], BF16)
        xq = take([KD, T], BF16)
        hq = take([F2 // P, T], BF16)
        qv = take([12])
        qs = sb("scales2", [P, 8, F2 // P])
        take = carver(work)
        take([KD, CH]), take([4, NT]), take([KD, CH])
        w3 = take([E3, 3 * D])
        lg3 = [take([NT, 8]) for _ in range(8)]
        rv3 = [take([NT]) for _ in range(8)]
        gr = [take([NT, 4]) for _ in range(7)]
        combt = take([8, NT])
        combT = take([P])
        sg3, t3, u3, h3 = take([2, CH]), take([CH]), take([CH]), take([2, CH])

        disp = nc.dram_tensor("dispatched", (TILES0 * P, D), F32, kind="Internal").ap()
        outs = nc.dram_tensor("expert_out", (TILES0 * P, D), F32, kind="Internal").ap()
        disp1 = nc.dram_tensor("dispatched1", (2 * T, D), F32, kind="Internal").ap()
        outs1 = nc.dram_tensor("expert_out1", (T, D), F32, kind="Internal").ap()
        comb3 = nc.dram_tensor("comb3", (P, P), F32, kind="Internal").ap()

        CREDIT = 1
        loop_sems = [sem(n) for n in (
            "x_done mean_done cent_done sq_done var_done rstdb_done xn_done "
            "q_done qsb_done score_done max_done sub_done exp_done padd_done den_done turn_done turned_done pv_done "
            "rd_done rde_done rb_done num_done o_done proj_done osc_done rope_done clamp_done "
            "q1_done qsb1_done score1_done max1_done neg1_done exp1_done rd1_done p1_done pt_done ptsb_done att1_done osc1_done "
            "xc_done front_done rows_done "
            "sa_done sp_done spm_done spc_done su_done sh_done ssig_done spair_done so_done sosc_done sx_done "
            "xt_done xst_done g_done ag_done pg_done pgm_done l_done al_done pl_done plc_done u_done h_done sig_done o2_done "
            "os_done y_done comb_done "
            "m1_done hact_done hrnd_done m2_done osc2_done xrnd_done xclip_done xq_done hq_done hmax_done "
            
            ).split()]
        (x_done, mean_done, cent_done, sq_done, var_done, rstdb_done, xn_done,
         q_done, qsb_done, score_done, max_done, sub_done, exp_done, padd_done, den_done, turn_done, turned_done, pv_done,
         rd_done, rde_done, rb_done, num_done, o_done, proj_done, osc_done, rope_done, clamp_done,
         q1_done, qsb1_done, score1_done, max1_done, neg1_done, exp1_done, rd1_done, p1_done, pt_done, ptsb_done,
         att1_done, osc1_done,
         xc_done, front_done, rows_done,
         sa_done, sp_done, spm_done, spc_done, su_done, sh_done, ssig_done, spair_done, so_done, sosc_done, sx_done,
         xt_done, xst_done, g_done, ag_done, pg_done, pgm_done, l_done, al_done, pl_done, plc_done, u_done, h_done,
         sig_done, o2_done, os_done, y_done, comb_done,
         m1_done, hact_done, hrnd_done, m2_done, osc2_done, xrnd_done, xclip_done, xq_done, hq_done, hmax_done,
         ) = loop_sems
        first_in, const_in, cb_in = sem("first_in"), sem("const_in"), sem("cb_in")
        x_in = [sem(f"x_in{c}") for c in range(NCH)]
        aw_in = [sem("aw_in_even"), sem("aw_in_odd")] * 2
        mask_in = sem("mask_in")
        rope_in = sem("rope_in")
        x_out = sem("x_out")
        tanh_done = sem("tanh_done")
        step = sem("dve_step")
        gbo_done, eps_done, rstd_done = sem("gbo_done"), sem("eps_done"), sem("rstd_done")
        pow_done = sem("pow_done")
        k_done, kt_done, v80_done, v80sb_done, vrep_done, kbd_done, vbd_done, mask_done = (
            sem(n) for n in "k_done kt_done v80_done v80sb_done vrep_done kbd_done vbd_done mask_done".split())

        zero_set, zeros_in = sem("zero_set"), sem("zeros_in")
        shared_in = sem("shared_in")
        w_in = [sem(f"w_in{n}") for n in range(3)]
        out_in = [sem(f"out_in{n}") for n in range(3)]
        smax_sub, smax_exp = sem("route_sub"), sem("route_exp")
        pick_done, rank_done, rank_read, index_done, texp_done = (
            sem(n) for n in "pick_done rank_done rank_read index_done tile_expert_done".split())
        scat_in = sem("scat_in")
        weigh_step = sem("weigh_step")
        gath_in = [sem(f"gath_in{c}") for c in range(NCH)]

        wq_in, wround_done, wturn_done, wturned_done = (sem(n) for n in "wq_in wround_done wturn_done wturned_done".split())
        tmax_done, allmax_done, xscale_done, hscale_done = (
            sem(n) for n in "tmax_done allmax_done xscale_done hscale_done".split())
        w3_in, sig3_done, comb3_done, combturn_done, combsb_done, comb3_in, combb_in = (
            sem(n) for n in "w3_in sig3_done comb3_done combturn_done combsb_done comb3_in combb_in".split())

        MHA = (0, 2, 3)
        VB = (3, 0, 1, 6, 7)
        EARLY = 6
        mb16f = [mb16.rearrange("p t e -> p (t e)")[:, 0:NT * n].rearrange("p (t e) -> p t e", e=n) for n in (R0, E1)]
        block = ctx.enter_context(nc.Block())

        def chunk(c):
            return ds(c * CH, CH)

        def over_tiles(eng, n, first, body, last):
            first(0, 0, 0)
            loops = (n - 2) // 3
            with eng.Fori(0, loops) as it:
                for r in range(3):
                    body(3 * it + 1 + r, (1 + r) % 3, it + (1 + r) // 3)
            for t in range(1 + 3 * loops, n - 1):
                body(t, t % 3, t // 3)
            last(n - 1, (n - 1) % 3, (n - 1) // 3)

        def over_chunks(eng, body, meanwhile=None):
            body(0, 0, before=False)
            if meanwhile:
                meanwhile()
            with eng.Fori(1, CPB) as cc:
                body(0, cc)
            for b in range(1, NB):
                with eng.Fori(0, CPB - (b == NB - 1)) as cc:
                    body(b, cc)
            body(NB - 1, CPB - 1, after=False)

        def stage_ready(eng, s):
            if s:
                eng.wait_ge(x_done, CREDIT + NCH * s)

        @block.sync
        def _(sp):
            for s_ in loop_sems:
                sp.sem_inc(s_, CREDIT)
            for s_ in (var_done, front_done, rows_done):
                sp.sem_inc(s_, 1)
            sp.sem_inc(hact_done, 4)
            for dst, src in [(ctxk[:], d["ctx"]), (cf[:], d["cf"])]:
                sp.dma_start(dst, src).then_inc(first_in, 16)
            sp.dma_start(aw[0], d["aw0"]).then_inc(aw_in[0], 16)
            sp.dma_start(bv[0], d["bv0"]).then_inc(aw_in[0], 16)
            for c in range(NCH):
                sp.dma_start(x[:, :, c * CH:(c + 1) * CH], d["x"][:, :, c * CH:(c + 1) * CH]).then_inc(x_in[c], 16)
            sp.dma_start(cb_raw, d["cb"]).then_inc(cb_in, 16)
            sp.dma_start(aw[1], d["aw1"]).then_inc(aw_in[1], 16)
            sp.dma_start(bv[1], d["bv1"]).then_inc(aw_in[1], 16)

            def reload(l):
                sp.wait_ge(x_done, CREDIT + NCH * (2 * (l - 2) + 1))
                sp.dma_start(aw[l], d[f"aw{l}"]).then_inc(aw_in[l], 16)
                sp.dma_start(bv[l], d[f"bv{l}"]).then_inc(aw_in[l], 16)

            def masks(l):
                sp.wait_ge(x_done, CREDIT + NCH * 2 * l)
                sp.dma_start(mtok_raw[l], d[f"mtok{l}"]).then_inc(mask_in, 16)
                if l == 2:
                    sp.dma_start(rope, d["rope"]).then_inc(rope_in, 16)

            def feed_tiles(n, base, load, then=None):
                dst = outs1 if base else outs

                def store(t, slot):
                    sp.wait_ge(os_done, CREDIT + base + t + 1)
                    sp.dma_start(dst[ds(t * P, P), :], os_[slot]).then_inc(out_in[slot], 16)

                def both(t, slot):
                    sp.wait_ge(l_done, CREDIT + base + t - 2)
                    rest = load(t, slot)
                    sp.wait_ge(o2_done, CREDIT + base + t - 2)
                    rest()
                    store(t - 3, slot)

                for t in range(3):
                    load(t, t)()
                with sp.Fori(1, n // 3) as it:
                    for r in range(3):
                        both(3 * it + r, r)
                for t in range(3 * (n // 3), n):
                    both(t, t % 3)
                for t in range(n - 3, n):
                    store(t, t % 3)
                    if then and t == n - 3:
                        then()

            if stages > 1:
                sp.wait_ge(zero_set, 1)
                for dst in (disp, disp1):
                    sp.dma_start(dst.rearrange("(n p) d -> p n d", p=P),
                                 zero[:, :].unsqueeze(1).broadcast_to([P, dst.shape[0] // P, D])).then_inc(zeros_in, 16)
                sp.dma_start(w0[2], d["f0w"][R0]).then_inc(shared_in, 16)
                sp.wait_ge(texp_done, 1)
                sp.wait_ge(scat_in, 16 * 2 * NT)

                def load0(t, slot):
                    if isinstance(t, int) and t == 2:
                        sp.wait_ge(sx_done, CREDIT + SPLIT)
                    e = sp.value_load(tex[0:1, ds(t, 1)], min_val=0, max_val=R0 - 1)
                    src = d["f0w"][ds(e, 1)].rearrange("e p n -> (e p) n")
                    up = 4 * KD * I0
                    sp.dma_start(w0[slot][:, 0:up], src[:, 0:up]).then_inc(w_in[slot], 16)
                    sp.dma_start(xs[slot], disp[ds(t * P, P), :]).then_inc(w_in[slot], 16)

                    def rest():
                        sp.dma_start(w0[slot][:, up:W0 + BC0], src[:, up:W0 + BC0]).then_inc(w_in[slot], 16)
                        sp.dma_start(b2row[slot][0:1, :], d["f0b"][ds(e, 1)]).then_inc(w_in[slot], 16)

                    return rest

                feed_tiles(TILES0, 0, load0,
                           lambda: sp.dma_start(w0[(TILES0 - 3) % 3], d["f0w"][R0]).then_inc(shared_in, 16))
            if stages > 3:
                sp.wait_ge(x_done, CREDIT + NCH * 2)
                sp.wait_ge(scat_in, 16 * 3 * NT)

                def load1(t, slot):
                    src = d["f1w"][ds(t, 1)].rearrange("e p n -> (e p) n")
                    up = KD * F1
                    sp.dma_start(w1m[slot][:, 0:up], src[:, 0:up]).then_inc(w_in[slot], 16)
                    sp.dma_start(xs[slot], disp1[ds(t * P, P), :]).then_inc(w_in[slot], 16)
                    return lambda: sp.dma_start(w1m[slot][:, up:4096], src[:, up:4096]).then_inc(w_in[slot], 16)

                feed_tiles(E1, TILES0, load1)
            if stages > 4:
                reload(2)
                masks(2)
                sp.dma_start(wq_raw[:, 0:2048], d["f2w1"].rearrange("p a b -> p (a b)")).then_inc(wq_in, 16)
                sp.dma_start(wq_raw[:, 2048:4096], d["f2w2"].rearrange("p a b -> p (a b)")).then_inc(wq_in, 16)
            if stages == 5:
                sp.wait_ge(wq_in, 32)
            if stages > 6:
                reload(3)
                masks(3)
            if stages > 7:
                sp.wait_ge(x_done, CREDIT + NCH * 7)
                sp.dma_start(w3, d["f3w"]).then_inc(w3_in, 16)
                sp.wait_ge(combsb_done, 1)
                sp.dma_start(comb3, combT).then_inc(comb3_in, 16)
                sp.wait_ge(comb3_in, 16)
                rows3 = comb3.rearrange("(e c t) p -> e c (t p)", e=8, c=NCH)
                for c in range(NCH):
                    for e in range(8):
                        sp.dma_start(combb[:, e, c * CH:(c + 1) * CH], rows3[e:e + 1, c, :].partition_broadcast(P)
                                     ).then_inc(combb_in, 16)
                    sp.wait_ge(combb_in, 16 * 8 * (c + 1))
            sp.wait_ge(aw_in[1], 32)
            for c in range(NCH):
                sp.wait_ge(x_done, CREDIT + NCH * (stages - 1) + c + 1)
                sp.dma_start(out[:, :, c * CH:(c + 1) * CH], x[:, :, c * CH:(c + 1) * CH]).then_inc(x_out, 16)
            sp.wait_ge(x_out, 16 * NCH)

        @block.tensor
        def _(pe):
            mm = nc.tensor.matmul

            means = {}

            def mean(s, c, counts=True):
                if s:
                    pe.wait_ge(x_done, CREDIT + NCH * (s - 1) + c + 1)
                for k in range(KD):
                    last = mm(ps[:, 4 + c, :] if isinstance(c, int) else ps[:, ds(c + 4, 1), :].rearrange("p b n -> p (b n)"),
                              mean_w, x[:, k, chunk(c)], start=k == 0, stop=k == KD - 1)
                last.then_inc(mean_done, 1)
                if counts:
                    means[s] = means.get(s, 0) + 1

            def layer_norm(s):
                b0 = CREDIT + NCH * s
                l = s // 2
                mha = s % 2 == 0 and l in MHA
                stage_ready(pe, s)
                if s == 0:
                    pe.wait_ge(first_in, 16 * 2)
                    project_kv(l)
                for c in range(means.get(s, 0), NCH):
                    if s == 0:
                        pe.wait_ge(x_in[c], 16)
                    mean(s, c)
                if s % 2 == 0 and s:
                    project_kv(l)
                with pe.Fori(0, NCH // 2) as it:
                    for r in range(2):
                        c = 2 * it + r
                        pe.wait_ge(sq_done, b0 + c + 1)
                        for t in range(TPC):
                            for k in range(KD):
                                last = mm(ps[:, 4, ds(c * TPC + t, 1)], turns[r][:, k, t * P:(t + 1) * P], mean_w[:, 0:1],
                                          start=k == 0, stop=k == KD - 1)
                        last.then_inc(var_done, 1)
                if mha:
                    pe.wait_ge(kt_done, l + 1)
                    pe.wait_ge(v80sb_done, l + 1)
                    spread_values(range(EARLY))
                pe.wait_ge(rstd_done, s + 1)
                for c in range(NCH):
                    for t in range(TPC):
                        n = c * TPC + t
                        last = nc.tensor.transpose(ps[:, 4 + c, t * P:(t + 1) * P], stat[:, 1, n:n + 1].broadcast_to([P, P]),
                                                   ident)
                    last.then_inc(rstdb_done, 1)

            def project_kv(l):
                pe.wait_ge(aw_in[l], 32 * (1 + l // 2))
                for w, bank in [(W_K, 0)] + ([(W_KS, 1)] if l == 2 else []):
                    for m in range(KD):
                        for k in range(KD):
                            last = mm(ps[:, bank, m * NB * KP:(m + 1) * NB * KP], aw[l][:, w, k, m * P:(m + 1) * P],
                                      ctxk[:, k, :], start=k == 0, stop=k == KD - 1)
                last.then_inc(k_done, 1)
                for b in range(NB):
                    for k in range(KD):
                        mm(ps[0:KP, 2, b * D:(b + 1) * D], ctxk[:, k, b * KP:(b + 1) * KP], aw[l][:, W_V, k, :],
                           start=k == 0, stop=False)
                    last = mm(ps[0:KP, 2, b * D:(b + 1) * D], ones_row[:, 0:KP], bv[l], start=False, stop=True)
                last.then_inc(v80_done, 1)

            def spread_values(groups):
                for n in groups:
                    b, j = divmod(n, JG)
                    bank, half = VB[n // 2], n % 2
                    mm(ps[:, bank, half * D:(half + 1) * D], cf[0:KP, C_SEL + j * P:C_SEL + (j + 1) * P],
                       v80[0:KP, b, :], start=True, stop=True).then_inc(vrep_done, 1)

            def heads(l):
                a = MHA.index(l)
                rot, masked = l == 2, l != 0

                def queries(i, c):
                    pe.wait_ge(sub_done, CREDIT + 8 * i)
                    for w, bank in [(W_Q, 2)] + ([(W_QS, 0)] if rot else []):
                        for m in range(KD):
                            for k in range(KD):
                                last = mm(ps[:, bank + m, :], aw[l][:, w, k, m * P:(m + 1) * P], xn[:, k, chunk(c)],
                                          start=k == 0, stop=k == KD - 1)
                    last.then_inc(q_done, 1)

                def scores(i, cc, b, n):
                    hf, t = divmod(n, TPC)
                    bank = 2 * ((n + 1) % 2)
                    if n > 1:
                        pe.wait_ge(sub_done, CREDIT + 8 * i + n - 1)
                    for g in range(2):
                        last = mm(ps[:, bank + g, 0:SL], q[:, hf, t * P:(t + 1) * P],
                                  kbd[:, hf, b, 4 * g:4 * (g + 1), :].rearrange("p h k -> p (h k)"),
                                  start=True, stop=not masked)
                    if masked:
                        for g in range(2):
                            last = mm(ps[:, bank + g, 0:SL], identb,
                                      mtok[:, ds(cc * TPC + t, 1), :].broadcast_to([P, 4, KP]), start=False, stop=True)
                    last.then_inc(score_done, 1)

                def turn(i, n):
                    pe.wait_ge(exp_done, CREDIT + 8 * i + n + 1)
                    pe.wait_ge(turned_done, CREDIT + 8 * i + n)
                    wide_ = ps[:, 4:6, :].rearrange("p b n -> p (b n)")
                    for j in range(JG):
                        last = nc.tensor.transpose(wide_[:, j * P:(j + 1) * P], pm[:, n % 2, j, :], ident)
                    last.then_inc(turn_done, 1)

                def values(i, b, hf):
                    pe.wait_ge(turned_done, CREDIT + 8 * i + TPC * (hf + 1))
                    for j in range(JG):
                        last = mm(ps[:, 6 + hf, :], vbd[:, b, j, hf * P:(hf + 1) * P], ptk[:, hf, j, :],
                                  start=j == 0, stop=j == JG - 1)
                    last.then_inc(pv_done, 1)

                def denominators(i):
                    pe.wait_ge(num_done, CREDIT + 2 * i + 2)
                    pe.wait_ge(padd_done, CREDIT + 6 * i + 6)
                    for t in range(TPC):
                        for hf in range(KD):
                            last = mm(ps[:, 6, t * 16 + hf * HH:t * 16 + (hf + 1) * HH],
                                      psum_[:, hf, 0, t * P:(t + 1) * P], blk, start=True, stop=True)
                    last.then_inc(den_done, 1)

                def inverses(i):
                    pe.wait_ge(rde_done, CREDIT + i + 1)
                    for hf in range(KD):
                        for t in range(TPC):
                            last = nc.tensor.transpose(ps[:, 6 + hf, t * P:(t + 1) * P], rde[:, t, hf * P:(hf + 1) * P], ident)
                    last.then_inc(rb_done, 1)

                def project(i):
                    pe.wait_ge(o_done, CREDIT + i + 1)
                    for m in range(KD):
                        for k in range(KD):
                            last = mm(ps[:, 6 + m, :], aw[l][:, W_O, k, m * P:(m + 1) * P], o[:, k, :],
                                      start=k == 0, stop=k == KD - 1)
                    last.then_inc(proj_done, 1)

                def body(b, cc, before=True, after=True):
                    c = CPB * b + cc
                    i = NCH * a + c
                    pe.wait_ge(qsb_done, CREDIT + i + 1)
                    scores(i, cc, b, 0)
                    scores(i, cc, b, 1)
                    if before:
                        denominators(i - 1)
                    for n in range(2, 8):
                        scores(i, cc, b, n)
                        turn(i, n - 2)
                        if n == 4 and before:
                            inverses(i - 1)
                        if n == 5 and before:
                            project(i - 1)
                    pe.wait_ge(osc_done, CREDIT + i)
                    if not before:
                        pe.wait_ge(vbd_done, NB * JG * (a + 1))
                    values(i, b, 0)
                    turn(i, 6)
                    turn(i, 7)
                    if after:
                        queries(i + 1, c + 1)
                    values(i, b, 1)

                pe.wait_ge(kbd_done, a + 1)
                if masked:
                    pe.wait_ge(mask_done, a)
                pe.wait_ge(xn_done, CREDIT + NCH * 2 * l + 1)
                pe.wait_ge(vbd_done, NB * JG * a + EARLY)
                queries(NCH * a, 0)
                pe.wait_ge(xn_done, CREDIT + NCH * (2 * l + 1))
                spread_values(range(EARLY, NB * JG))
                over_chunks(pe, body)
                i = NCH * (a + 1) - 1
                for c in range(2):
                    pe.wait_ge(turned_done, CREDIT + 8 * (i + 1))
                    mean(2 * l + 1, c)
                denominators(i)
                inverses(i)
                project(i)

            def single():
                def queries(c):
                    for m in range(KD):
                        for k in range(KD):
                            last = mm(ps[:, 6 * (c % 2) + m, :], aw[1][:, W_Q, k, m * P:(m + 1) * P],
                                      xn[:, k, c * CH:(c + 1) * CH], start=k == 0, stop=k == KD - 1)
                    last.then_inc(q1_done, 1)

                pe.wait_ge(xn_done, CREDIT + NCH * 2 + 1)
                pe.wait_ge(kt_done, 2)
                pe.wait_ge(v80sb_done, 2)
                queries(0)
                for c in range(NCH):
                    b = c // CPB
                    pe.wait_ge(qsb1_done, CREDIT + c + 1)
                    pe.wait_ge(exp1_done, CREDIT + c)
                    for t in range(TPC):
                        for k in range(KD):
                            last = mm(ps[:, 2, t * KP:t * KP + KEYS], q1[c % 2][:, k, t * P:(t + 1) * P],
                                      kt[:, k, b * KP:b * KP + KEYS], start=k == 0, stop=k == KD - 1)
                    last.then_inc(score1_done, 1)
                    if c + 1 < NCH:
                        pe.wait_ge(xn_done, CREDIT + NCH * 3)
                        queries(c + 1)
                    pe.wait_ge(p1_done, CREDIT + c + 1)
                    for t in range(TPC):
                        last = nc.tensor.transpose(ps[0:KEYS, 3, t * P:(t + 1) * P], p1[:, t, 0:KEYS], ident)
                    last.then_inc(pt_done, 1)
                    pe.wait_ge(ptsb_done, CREDIT + c + 1)
                    pe.wait_ge(osc1_done, CREDIT + c)
                    for m in range(KD):
                        last = mm(ps[:, 4 + m, :], v80[0:KEYS, b, m * P:(m + 1) * P], pt[0:KEYS, :],
                                  start=True, stop=True)
                    last.then_inc(att1_done, 1)

            def front(f, n_exp, with_rows):
                w = gate_w[:, f, 0:KD * n_exp].rearrange("p (k e) -> p k e", k=KD)
                with pe.Fori(0, NCH // 2) as it:
                    for r in range(2):
                        c = 2 * it + r
                        bank = (1, 6)[r]
                        xc = turns[r]
                        pe.wait_ge(xc_done, CREDIT + NCH * f + c + 1)
                        if r:
                            pe.wait_ge(xn_done, CREDIT + NCH * (2, 4, 8)[f])
                        if with_rows:
                            pe.wait_ge(rows_done, CREDIT + NCH * f + c)
                        for t in range(TPC):
                            for k in range(KD):
                                last = mm(ps[:, 0, ds((c * TPC + t) * n_exp, n_exp)], xc[:, k, t * P:(t + 1) * P],
                                          w[:, k, :], start=k == 0, stop=k == KD - 1)
                            if with_rows:
                                for k in range(KD):
                                    at = (t % 2) * D + k * P
                                    last = nc.tensor.transpose(ps[:, bank + t // 2, at:at + P],
                                                               xc[:, k, t * P:(t + 1) * P], ident)
                        last.then_inc(front_done, 1)

            def ranks(f, n_exp):
                pe.wait_ge(pick_done, f + 1)
                picks = mb16f[f]
                n = NT * n_exp
                mm(ps[:, 3, 0:n], cb[:, B_TRI:B_TRI + P], picks.rearrange("p t e -> p (t e)"), start=True, stop=False)
                for t in range(NT - 1):
                    mm(ps[:, 3, (t + 1) * n_exp:n].rearrange("p (t e) -> p t e", e=n_exp), cb[:, B_ONE:B_ONE + P],
                       picks[:, t:t + 1, :].broadcast_to([P, NT - 1 - t, n_exp]), start=False, stop=t == NT - 2)
                for t in range(NT):
                    last = mm(ps[:, 4, 0:n_exp], cb[:, B_ONE:B_ONE + P], picks[:, t, :], start=t == 0, stop=t == NT - 1)
                last.then_inc(rank_done, 1)
                pe.wait_ge(rank_read, f + 1)

            def part(w, n, k, m):
                at = (n * KD + k) * I0 + m * P
                return w[:, at:at + P]

            def down0(w, k):
                at = 4 * KD * I0 + k * D
                return w[:, at:at + D]

            def shared0(part_):
                w = w0[(2, (TILES0 - 3) % 3)[part_]]
                first, end = ((0, SPLIT), (SPLIT, NCH))[part_]
                pe.wait_ge(shared_in, 16 * (part_ + 1))

                def up(c, steps):
                    for n in steps:
                        m, lin = divmod(n, 2)
                        pe.wait_ge(sp_done, CREDIT + 8 * c + max(n - 1, 0))
                        for w_ in range(2):
                            for k in range(KD):
                                last = mm(ps[:, 2 * lin + w_, :], part(w, 2 * lin + w_, k, m), xn[:, k, chunk(c)],
                                          start=k == 0, stop=k == KD - 1)
                        last.then_inc(spair_done, 1)

                def down(c):
                    pe.wait_ge(sh_done, CREDIT + IM * c + IM)
                    pe.wait_ge(sosc_done, CREDIT + c)
                    for m in range(KD):
                        for k in range(IM):
                            last = mm(ps[:, 6 + m, :], down0(w, k)[:, m * P:(m + 1) * P], hs[:, k, :],
                                      start=k == 0, stop=k == IM - 1)
                    last.then_inc(so_done, 1)

                up(first, range(2 * IM))
                with pe.Fori(first + 1, end) as c:
                    up(c, (0,))
                    down(c - 1)
                    up(c, range(1, 2 * IM))
                down(end - 1)

            def tile_rows(t, slot, use, uses0, b0):
                pe.wait_ge(w_in[slot], uses0 + (48 if b0 else 64) * (use + 1))
                for k in range(KD):
                    last = nc.tensor.transpose(ps[:, 5, k * P:(k + 1) * P], xs[slot][:, k * P:(k + 1) * P], ident)
                last.then_inc(xt_done, 1)

            def tiles0():
                def up(t, slot, lin, which=(0, 1)):
                    for w_ in which:
                        for m in range(IM):
                            for k in range(KD):
                                last = mm(ps[:, 2 * lin + w_, m * P:(m + 1) * P], part(w0[slot], 2 * lin + w_, k, m),
                                          xst[slot][:, k, :], start=k == 0, stop=k == KD - 1)
                    if 1 in which:
                        last.then_inc(l_done if lin else g_done, 1)

                def down(t, slot):
                    pe.wait_ge(h_done, CREDIT + t + 1)
                    pe.wait_ge(os_done, CREDIT + t)
                    mm(ps[:, 4, 0:D], ones_row, b2row[slot][0:1, :], start=True, stop=False)
                    for k in range(IM):
                        last = mm(ps[:, 4, 0:D], hh[slot][:, k * P:(k + 1) * P], down0(w0[slot], k),
                                  start=False, stop=k == IM - 1)
                    last.then_inc(o2_done, 1)

                def body(t, slot, use, before=True, after=True):
                    pe.wait_ge(xst_done, CREDIT + t + 1)
                    pe.wait_ge(pg_done, CREDIT + t)
                    up(t, slot, 0)
                    pe.wait_ge(pl_done, CREDIT + t)
                    up(t, slot, 1, (0,))
                    if before:
                        down(t - 1, (slot + 2) % 3)
                    if after:
                        tile_rows(t + 1, (slot + 1) % 3, use + (slot == 2), 0, 0)
                    up(t, slot, 1, (1,))

                tile_rows(0, 0, 0, 0, 0)
                over_tiles(pe, TILES0, lambda t, s_, u: body(t, s_, u, before=False), body,
                           lambda t, s_, u: body(t, s_, u, after=False))
                down(TILES0 - 1, (TILES0 - 1) % 3)

            def tiles1():
                uses0 = 64 * (TILES0 // 3)

                def up(t, slot, half):
                    for m in range(4):
                        for k in range(KD):
                            at = k * F1 + (4 * half + m) * P
                            last = mm(ps[:, 2 * half, m * P:(m + 1) * P], w1m[slot][:, at:at + P], xst[slot][:, k, :],
                                      start=k == 0, stop=k == KD - 1)
                    last.then_inc(l_done if half else g_done, 1)

                def down(t, slot):
                    pe.wait_ge(ag_done, CREDIT + TILES0 + t + 1)
                    pe.wait_ge(pl_done, CREDIT + TILES0 + t + 1)
                    pe.wait_ge(os_done, CREDIT + TILES0 + t)
                    for k in range(F1 // P):
                        last = mm(ps[:, 4, 0:D], hh[slot][:, k * P:(k + 1) * P],
                                  w1m[slot][:, KD * F1 + k * D:KD * F1 + (k + 1) * D], start=k == 0, stop=k == F1 // P - 1)
                    last.then_inc(o2_done, 1)

                def body(t, slot, use, before=True, after=True):
                    pe.wait_ge(xst_done, CREDIT + TILES0 + t + 1)
                    pe.wait_ge(ag_done, CREDIT + TILES0 + t)
                    up(t, slot, 0)
                    if before:
                        down(t - 1, (slot + 2) % 3)
                    if after:
                        tile_rows(t + 1, (slot + 1) % 3, use + (slot == 2), uses0, 1)
                    pe.wait_ge(pl_done, CREDIT + TILES0 + t)
                    up(t, slot, 1)

                tile_rows(0, 0, 0, uses0, 1)
                over_tiles(pe, E1, lambda t, s_, u: body(t, s_, u, before=False), body,
                           lambda t, s_, u: body(t, s_, u, after=False))
                down(E1 - 1, (E1 - 1) % 3)

            def combine(f):
                for c in range(NCH):
                    pe.wait_ge(y_done, CREDIT + NCH * f + c + 1)
                    if c > 1:
                        pe.wait_ge(x_done, CREDIT + NCH * (1 + 2 * f) + c - 1)
                    for m in range(KD):
                        for t in range(TPC):
                            last = nc.tensor.transpose(ps[:, 2 * (c % 2) + m, t * P:(t + 1) * P],
                                                       ga[:, c * TPC + t, m * P:(m + 1) * P], ident)
                    last.then_inc(comb_done, 1)
                    if c:
                        mean(2 * f + 2, c - 1)

            def turn_weights():
                pe.wait_ge(wround_done, 1)
                for k in range(KD):
                    for m in range(F2 // P):
                        nc.tensor.transpose(ps[:, k, :].bitcast(BF16)[:, m * P:(m + 1) * P],
                                            wq1[:, m, k * P:(k + 1) * P], identb)
                for k in range(F2 // P):
                    for m in range(KD):
                        at = k * D + m * P
                        last = nc.tensor.transpose(ps[:, 2 + at // 1024, :].bitcast(BF16)[:, at % 1024:at % 1024 + P],
                                                   wq2[:, m, k * P:(k + 1) * P], identb)
                last.then_inc(wturn_done, 1)
                pe.wait_ge(wturned_done, 1)

            def quantized():
                with pe.Fori(0, NCH) as c:
                    pe.wait_ge(xq_done, CREDIT + c + 1)
                    for m in range(F2 // P):
                        if m % 4 == 0:
                            pe.wait_ge(hact_done, CREDIT + 8 * c + m)
                        for k in range(KD):
                            last = mm(ps[:, m, :], wt1q[:, k, m * P:(m + 1) * P], xq[:, k, chunk(c)],
                                      start=k == 0, stop=k == KD - 1)
                        last.then_inc(m1_done, 1)
                pe.wait_ge(hact_done, CREDIT + 4 + 8 * NCH)

                def second(c):
                    pe.wait_ge(hq_done, CREDIT + c + 1)
                    pe.wait_ge(osc2_done, CREDIT + c)
                    for m in range(KD):
                        for k in range(F2 // P):
                            last = mm(ps[:, m, :], wt2q[:, k, m * P:(m + 1) * P], hq[:, k, chunk(c)],
                                      start=k == 0, stop=k == F2 // P - 1)
                    last.then_inc(m2_done, 1)

                second(0)
                with pe.Fori(1, NCH) as c:
                    second(c)
                    mean(6, c - 1, counts=False)
                means[6] = NCH - 1

            def experts3():
                def chunk_of(first, experts, c):
                    i = first + len(experts) * c

                    def up(n):
                        pe.wait_ge(su_done, CREDIT + IM * NCH + i + max(n - 1, 0))
                        for w_ in range(2):
                            for k in range(KD):
                                last = mm(ps[:, 2 * (n % 2) + w_, :], w3[:, experts[n], (w_ * KD + k) * P:(w_ * KD + k + 1) * P],
                                          xn[:, k, chunk(c)], start=k == 0, stop=k == KD - 1)
                        last.then_inc(spair_done, 1)

                    up(0)
                    for n in range(len(experts)):
                        if n + 1 < len(experts):
                            up(n + 1)
                        pe.wait_ge(sh_done, CREDIT + IM * NCH + i + n + 1)
                        if n == 0 and experts is SHARED3:
                            pe.wait_ge(sx_done, CREDIT + NCH + c)
                        elif n == 0:
                            pe.wait_ge(x_done, CREDIT + NCH * 7 + c)
                        for m in range(KD):
                            last = mm(ps[:, 4 + m, :], w3[:, experts[n], 2 * D + m * P:2 * D + (m + 1) * P], h3[:, n % 2, :],
                                      start=n == 0, stop=n == len(experts) - 1)
                        last.then_inc(so_done, 1)

                pe.wait_ge(w3_in, 16)
                pe.wait_ge(sig3_done, 1)
                with pe.Fori(0, NCH - 1) as c:
                    chunk_of(0, SHARED3, c)
                pe.wait_ge(comb3_done, 1)
                nc.tensor.transpose(ps[:, 6, 0:P], combt.rearrange("p e t -> p (e t)"), ident).then_inc(combturn_done, 1)
                chunk_of(0, SHARED3, NCH - 1)
                pe.wait_ge(sx_done, CREDIT + 2 * NCH)
                with pe.Fori(0, NCH) as c:
                    chunk_of(NCH * len(SHARED3), ROUTED3, c)

            for s in range(stages):
                l = s // 2
                if s == 5:
                    turn_weights()
                layer_norm(s)
                if s % 2 == 0 and l in MHA:
                    heads(l)
                if s == 2:
                    single()
                if s == 5:
                    quantized()
                if s == 7:
                    front(2, 8, False)
                    experts3()
                if s == 1:
                    front(0, R0, True)
                    ranks(0, R0)
                    shared0(0)
                    tiles0()
                    shared0(1)
                    combine(0)
                if s == 3:
                    front(1, E1, True)
                    ranks(1, E1)
                    tiles1()
                    combine(1)

        @block.scalar
        def _(act):
            A = nc.scalar.activation

            def layer_norm(s):
                b0 = CREDIT + NCH * s
                with act.Fori(0, NCH // 2) as it:
                    for r in range(2):
                        c = 2 * it + r
                        act.wait_ge(cent_done, b0 + c + 1)
                        act.wait_ge(var_done, b0 + c)
                        A(turns[r], xn[:, :, chunk(c)], ACT.Square).then_inc(sq_done, 1)

            def heads(l):
                a = MHA.index(l)

                def exponentials(i, n):
                    act.wait_ge(sub_done, CREDIT + 8 * i + n + 1)
                    act.wait_ge(turn_done, CREDIT + 8 * i + max(n - 1, 0))
                    A(pm[:, n % 2, :, :].rearrange("p j (h i) -> p h j i", i=16),
                      dif[:, n % 2, :, :].rearrange("p h (j i) -> p h j i", i=16), ACT.Exp).then_inc(exp_done, 1)

                def turned(i, n):
                    hf, t = divmod(n, TPC)
                    act.wait_ge(turn_done, CREDIT + 8 * i + n + 1)
                    act.wait_ge(pv_done, CREDIT + 2 * i)
                    act.wait_ge(padd_done, CREDIT + 6 * i)
                    A(ptk[:, hf, :, t * P:(t + 1) * P],
                      ps[:, 4:6, :].rearrange("p b n -> p (b n)")[:, 0:JG * P].rearrange("p (j n) -> p j n", j=JG),
                      ACT.Copy).then_inc(turned_done, 1)

                def numerators(i, hf):
                    act.wait_ge(pv_done, CREDIT + 2 * i + hf + 1)
                    A(num[:, hf, :], ps[:, 6 + hf, :], ACT.Copy).then_inc(num_done, 1)

                def gated_out(i):
                    act.wait_ge(proj_done, CREDIT + i + 1)
                    act.wait_ge(x_done, CREDIT + NCH * (2 * l - a) + i)
                    for m in range(KD):
                        last = A(osc[:, m, :], ps[:, 6 + m, :], ACT.Identity, bias=gbo[:, l, m:m + 1],
                                 scale=gts[:, l:l + 1])
                    last.then_inc(osc_done, 1)

                def queries(i):
                    if l == 2:
                        return
                    act.wait_ge(q_done, CREDIT + i + 1)
                    for m in range(KD):
                        last = A(q[:, m, :], ps[:, 2 + m, :], ACT.Identity,
                                 bias=cols[:, V_ATT * l + V_Q + m:V_ATT * l + V_Q + m + 1])
                    last.then_inc(qsb_done, 1)

                def spread(i):
                    act.wait_ge(rd_done, CREDIT + i + 1)
                    A(rde[:, :, :].rearrange("p t (h i) -> p t h i", i=16),
                      rd[:, :, :].unsqueeze(3).broadcast_to([P, TPC, 2 * HH, 16]), ACT.Copy).then_inc(rde_done, 1)

                def body(b, cc, before=True, after=True):
                    i = NCH * a + CPB * b + cc
                    for n in range(8):
                        if n == 6 and before:
                            gated_out(i - 1)
                        if n > 1:
                            turned(i, n - 2)
                        exponentials(i, n)
                        if n == 2 and before:
                            spread(i - 1)
                    numerators(i, 0)
                    turned(i, 6)
                    turned(i, 7)
                    if after:
                        queries(i + 1)
                    numerators(i, 1)

                queries(NCH * a)
                over_chunks(act, body)
                i = NCH * (a + 1) - 1
                spread(i)
                gated_out(i)

            def single():
                def queries(c):
                    act.wait_ge(q1_done, CREDIT + c + 1)
                    for m in range(KD):
                        last = A(q1[c % 2][:, m, :], ps[:, 6 * (c % 2) + m, :], ACT.Identity,
                                 bias=cols[:, V_ATT + V_Q + m:V_ATT + V_Q + m + 1])
                    last.then_inc(qsb1_done, 1)

                def out(c):
                    act.wait_ge(att1_done, CREDIT + c + 1)
                    act.wait_ge(x_done, CREDIT + NCH * 2 + c)
                    for m in range(KD):
                        last = A(osc[:, m, :], ps[:, 4 + m, :], ACT.Copy, scale=gts[:, 1:2])
                    last.then_inc(osc1_done, 1)

                queries(0)
                for c in range(NCH):
                    act.wait_ge(neg1_done, CREDIT + c + 1)
                    act.wait_ge(pt_done, CREDIT + c)
                    for t in range(TPC):
                        last = A(p1[:, t, 0:KEYS], ps[:, 2, t * KP:t * KP + KEYS], ACT.Exp, bias=neg4[:, 0, t:t + 1],
                                 scale=1.0 / 16, accum_out=neg4[:, 1, t:t + 1])
                    last.then_inc(exp1_done, 1)
                    if c + 1 < NCH:
                        queries(c + 1)
                    act.wait_ge(pt_done, CREDIT + c + 1)
                    A(pt[0:KEYS, :], ps[0:KEYS, 3, :], ACT.Copy).then_inc(ptsb_done, 1)
                    out(c)

            def front(s, f):
                with act.Fori(0, NCH // 2) as it:
                    for r in range(2):
                        c = 2 * it + r
                        act.wait_ge(xn_done, CREDIT + NCH * s + c + 1)
                        act.wait_ge(front_done, CREDIT + NCH * f + c)
                        A(turns[r], xn[:, :, chunk(c)], ACT.Copy).then_inc(xc_done, 1)

            def shared0(part_):
                first, end = ((0, SPLIT), (SPLIT, NCH))[part_]

                def out(c):
                    act.wait_ge(so_done, CREDIT + c + 1)
                    act.wait_ge(sx_done, CREDIT + c)
                    for m in range(KD):
                        last = A(osc[:, m, :], ps[:, 6 + m, :], ACT.Identity, bias=gbo[:, 1, m:m + 1], scale=gts[:, 4:5])
                    last.then_inc(sosc_done, 1)

                def body(c, before=True):
                    for n in range(2 * IM):
                        m, lin = divmod(n, 2)
                        at = V_F0 + 2 * IM * lin + m
                        act.wait_ge(spair_done, CREDIT + 8 * c + n + 1)
                        A((al if lin else ag), ps[:, 2 * lin, :], ACT.Identity, bias=cols[:, at:at + 1]).then_inc(sa_done, 1)
                        if not lin:
                            act.wait_ge(spm_done, CREDIT + IM * c + m + 1)
                            act.wait_ge(sh_done, CREDIT + IM * c + m)
                            A(sig, pg, ACT.Sigmoid, scale=1.702).then_inc(ssig_done, 1)
                        if n == 1 and before:
                            out(c - 1)

                body(first, before=False)
                with act.Fori(first + 1, end) as c:
                    body(c)
                out(end - 1)

            def tile_rows(t, slot):
                act.wait_ge(xt_done, CREDIT + t + 1)
                A(xst[slot].rearrange("p k n -> p (k n)"), ps[:, 5, 0:KD * P], ACT.Copy).then_inc(xst_done, 1)

            def tiles0():
                def biased(dst, slot, lin, done, made):
                    act.wait_ge(done, made)
                    for m in range(IM):
                        at = W0 + 2 * IM * lin + m
                        last = A(dst[:, m * P:(m + 1) * P], ps[:, 2 * lin, m * P:(m + 1) * P], ACT.Identity,
                                 bias=w0[slot][:, at:at + 1])
                    last.then_inc(al_done if lin else ag_done, 1)

                def out(t, slot, use):
                    act.wait_ge(o2_done, CREDIT + t + 1)
                    if not (isinstance(use, int) and use == 0):
                        act.wait_ge(out_in[slot], 16 * use)
                    A(os_[slot], ps[:, 4, 0:D], ACT.Copy).then_inc(os_done, 1)

                def body(t, slot, use, before=True, after=True):
                    biased(ag, slot, 0, g_done, CREDIT + t + 1)
                    act.wait_ge(pgm_done, CREDIT + t + 1)
                    A(sig, pg, ACT.Sigmoid, scale=1.702).then_inc(sig_done, 1)
                    if before:
                        out(t - 1, (slot + 2) % 3, use - (slot == 0))
                    if after:
                        tile_rows(t + 1, (slot + 1) % 3)
                    biased(al, slot, 1, l_done, CREDIT + t + 1)

                tile_rows(0, 0)
                over_tiles(act, TILES0, lambda t, s_, u: body(t, s_, u, before=False), body,
                           lambda t, s_, u: body(t, s_, u, after=False))
                out(TILES0 - 1, (TILES0 - 1) % 3, (TILES0 - 1) // 3)

            def tiles1():
                def out(t, slot, use):
                    act.wait_ge(o2_done, CREDIT + TILES0 + t + 1)
                    act.wait_ge(out_in[slot], 16 * (TILES0 // 3 + use))
                    A(os_[slot], ps[:, 4, 0:D], ACT.Copy).then_inc(os_done, 1)

                def body(t, slot, use, before=True, after=True):
                    act.wait_ge(g_done, CREDIT + TILES0 + t + 1)
                    A(hh[slot][:, 0:CH], ps[:, 0, :], ACT.Relu).then_inc(ag_done, 1)
                    if before:
                        out(t - 1, (slot + 2) % 3, use - (slot == 0))
                    if after:
                        tile_rows(TILES0 + t + 1, (slot + 1) % 3)

                tile_rows(TILES0, 0)
                over_tiles(act, E1, lambda t, s_, u: body(t, s_, u, before=False), body,
                           lambda t, s_, u: body(t, s_, u, after=False))
                out(E1 - 1, (E1 - 1) % 3, (E1 - 1) // 3)

            def quantized():
                magic = cf[:, C_MAGIC:C_MAGIC + 1]
                act.wait_ge(xscale_done, 1)
                with act.Fori(0, NCH) as c:
                    A(xn[:, :, chunk(c)], xn[:, :, chunk(c)], ACT.Identity, bias=magic, scale=qv[:, 3:4]).then_inc(xrnd_done, 1)
                with act.Fori(0, NCH) as c:
                    for m in range(F2 // P):
                        act.wait_ge(m1_done, CREDIT + 8 * c + m + 1)
                        A(hbig[:, m, chunk(c)], ps[:, m, :], ACT.Relu, bias=qs[:, 4, m:m + 1], scale=qs[:, 2, m:m + 1]
                          ).then_inc(hact_done, 1)
                act.wait_ge(hscale_done, 1)
                with act.Fori(0, NCH) as c:
                    A(hbig[:, :, chunk(c)], hbig[:, :, chunk(c)], ACT.Identity, bias=magic, scale=qv[:, 7:8]).then_inc(hrnd_done, 1)
                with act.Fori(0, NCH) as c:
                    act.wait_ge(m2_done, CREDIT + c + 1)
                    act.wait_ge(x_done, CREDIT + NCH * 5 + c)
                    for m in range(KD):
                        last = A(osc[:, m, :], ps[:, m, :], ACT.Identity, bias=qs[:, 7, 2 + m:3 + m], scale=qs[:, 7, m:m + 1])
                    last.then_inc(osc2_done, 1)

            def experts3():
                act.wait_ge(front_done, CREDIT + 1 + NCH * 3)
                A(lg3[1].rearrange("p t e -> p (t e)"), ps[:, 0, 0:NT * 8], ACT.Sigmoid).then_inc(sig3_done, 1)

                def chunk_of(first, experts, c):
                    for n in range(len(experts)):
                        act.wait_ge(spair_done, CREDIT + 8 * NCH + first + len(experts) * c + n + 1)
                        A(sg3[:, n % 2, :], ps[:, 2 * (n % 2), :], ACT.Sigmoid).then_inc(ssig_done, 1)

                with act.Fori(0, NCH - 1) as c:
                    chunk_of(0, SHARED3, c)
                act.wait_ge(combturn_done, 1)
                A(combT, ps[:, 6, 0:P], ACT.Copy).then_inc(combsb_done, 1)
                chunk_of(0, SHARED3, NCH - 1)
                with act.Fori(0, NCH) as c:
                    chunk_of(NCH * len(SHARED3), ROUTED3, c)

            def route_exp(f, n_exp):
                act.wait_ge(smax_sub, f + 1)
                A(ra[1][:, 0:NT * n_exp], ra[0][:, 0:NT * n_exp], ACT.Exp).then_inc(smax_exp, 1)

            consts = [(gts[:], d["g"].partition_broadcast(P)), (cols[:], d["cols"]),
                      (gate_w[:, 0, 0:16], d["gate0"].rearrange("p k e -> p (k e)")),
                      (gate_w[:, 1, :], d["gate1"].rearrange("p k e -> p (k e)")),
                      (gate_w[:, 2, 0:16], d["gate3"].rearrange("p k e -> p (k e)")),
                      (gate_b[:, 0, :], d["gb0"].partition_broadcast(P)), (gate_b[:, 1, :], d["gb3"].partition_broadcast(P))]
            for dst, src in consts:
                act.dma_start(dst, src).then_inc(const_in, 16)
            act.wait_ge(const_in, 16 * len(consts))
            A(gts[:, :], gts[:, :], ACT.Tanh).then_inc(tanh_done, 1)
            act.wait_ge(gbo_done, 1)
            for s in range(stages):
                l = s // 2
                if s == 5:
                    act.wait_ge(wturn_done, 1)
                    A(wt1q.rearrange("p k n -> p (k n)"), ps[:, 0:2, :].rearrange("p b n -> p (b n)").bitcast(BF16), ACT.Copy)
                    A(wt2q.rearrange("p k n -> p (k n)"), ps[:, 2:4, :].rearrange("p b n -> p (b n)").bitcast(BF16), ACT.Copy
                      ).then_inc(wturned_done, 1)
                layer_norm(s)
                if s % 2 == 0:
                    act.wait_ge(v80_done, l + 1)
                    A(v80[0:KP, :, :].rearrange("p b n -> p (b n)"), ps[0:KP, 2, :], ACT.Copy).then_inc(v80sb_done, 1)
                if s == 2:
                    single()
                if s % 2 == 0 and l in MHA:
                    heads(l)
                if s == 5:
                    quantized()
                if s == 7:
                    front(7, 2)
                    experts3()
                if s == 1:
                    front(1, 0)
                    route_exp(0, R0)
                    shared0(0)
                    tiles0()
                    shared0(1)
                if s == 3:
                    front(3, 1)
                    route_exp(1, E1)
                    tiles1()

        @block.gpsimd
        def _(pool):
            def heads(l):
                a = MHA.index(l)

                def body(b, cc):
                    i = NCH * a + CPB * b + cc
                    for hf in range(KD):
                        s0, s1 = psum_[:, hf, 0, :], psum_[:, hf, 1, :]
                        pool.wait_ge(turned_done, CREDIT + 8 * i + TPC * (hf + 1))
                        pool.wait_ge(den_done, CREDIT + i)
                        nc.gpsimd.tensor_tensor(psum_[:, hf, :, :], ptk[:, hf, 0:2, :], ptk[:, hf, 2:4, :], ALU.add
                                                ).then_inc(padd_done, 1)
                        pool.wait_ge(padd_done, CREDIT + 6 * i + 3 * hf + 1)
                        nc.gpsimd.tensor_tensor(s0, s0, s1, ALU.add).then_inc(padd_done, 1)
                        pool.wait_ge(padd_done, CREDIT + 6 * i + 3 * hf + 2)
                        nc.gpsimd.tensor_tensor(s0, s0, ptk[:, hf, 4, :], ALU.add).then_inc(padd_done, 1)

                for b in range(NB):
                    with pool.Fori(0, CPB) as cc:
                        body(b, cc)

            def scatter(dst, index, rest):
                for t in range(NT):
                    nc.gpsimd.indirect_dma_start(dst, bass.IndirectOffsetOnAxis(index[:, t:t + 1], 0), rows_[:, t, :], None
                                                 ).then_inc(scat_in, 16)

            def gather(dst, src, index, c):
                for t in range(c * TPC, (c + 1) * TPC):
                    nc.gpsimd.indirect_dma_start(dst[:, t, :], None, src, bass.IndirectOffsetOnAxis(index[:, t:t + 1], 0)
                                                 ).then_inc(gath_in[c], 16)

            def weigh0(c):
                sl = slice(c * TPC, (c + 1) * TPC)
                pool.wait_ge(gath_in[c], 16 * TPC * 2)
                for n, (y, w) in enumerate(((ga, wt1), (gb, wt2))):
                    nc.gpsimd.tensor_tensor(y[:, sl, :], y[:, sl, :], w[:, sl].unsqueeze(2).broadcast_to([P, TPC, D]),
                                            ALU.mult).then_inc(weigh_step, 1)
                pool.wait_ge(weigh_step, 2 * (c + 1))
                nc.gpsimd.tensor_tensor(ga[:, sl, :], ga[:, sl, :], gb[:, sl, :], ALU.add).then_inc(y_done, 1)

            nc.gpsimd.memset(zero[:, :], 0.0).then_inc(zero_set, 1)
            for s in range(stages):
                l = s // 2
                pool.wait_ge(eps_done, s + 1)
                nc.gpsimd.tensor_tensor(stat[:, 1, :], stat[:, 0, :], cf[:, C_MHALF:C_MHALF + NT],
                                        ALU.pow).then_inc(pow_done, 1)
                if s % 2 == 0 and l in MHA:
                    heads(l)
                if s == 5:
                    for n in range(2):
                        pool.wait_ge(tmax_done, n + 1)
                        nc.gpsimd.partition_all_reduce(qv[:, 1 + 4 * n:2 + 4 * n], qv[:, 4 * n:1 + 4 * n], P, RMAX
                                                       ).then_inc(allmax_done, 1)
                if s == 1:
                    pool.wait_ge(zeros_in, 32)
                    pool.wait_ge(rows_done, CREDIT + 1 + NCH)
                    pool.wait_ge(index_done, 1)
                    scatter(disp, gix1, 0)
                    scatter(disp, gix2, 0)
                    pool.wait_ge(scat_in, 16 * 2 * NT)
                    for n in range(3):
                        pool.wait_ge(out_in[n], 16 * (TILES0 // 3))
                    for c in range(NCH):
                        gather(ga, outs, gix1, c)
                        gather(gb, outs, gix2, c)
                    for c in range(NCH):
                        weigh0(c)
                if s == 3:
                    pool.wait_ge(rows_done, CREDIT + 1 + NCH * 2)
                    pool.wait_ge(index_done, 2)
                    scatter(disp1, six, 0)
                    pool.wait_ge(scat_in, 16 * 3 * NT)
                    for n in range(3):
                        pool.wait_ge(out_in[n], 16 * (TILES0 // 3 + (E1 + 2 - n) // 3))
                    for c in range(NCH):
                        gather(ga, outs1, gix1, c)

        @block.vector
        def _(dve):
            V = nc.vector
            count = [0]

            def link(ins):
                count[0] += 1
                ins.then_inc(step, 1)
                dve.wait_ge(step, count[0])

            def centre(s):
                b0 = CREDIT + NCH * s
                with dve.Fori(0, NCH) as c:
                    dve.wait_ge(mean_done, b0 + c + 1)
                    V.tensor_tensor(xn[:, :, chunk(c)], x[:, :, chunk(c)],
                                    ps[:, ds(c + 4, 1), :].broadcast_to([P, KD, CH]), ALU.subtract).then_inc(cent_done, 1)

            def variance(s):
                dve.wait_ge(var_done, CREDIT + NCH * s + 1 + NCH)
                V.tensor_scalar(stat[:, 0, :], ps[:, 4, 0:NT], EPS, None, ALU.add).then_inc(eps_done, 1)

            def newton(s):
                dve.wait_ge(pow_done, s + 1)
                link(V.tensor_tensor(stat[:, 2, :], stat[:, 1, :], stat[:, 1, :], ALU.mult))
                link(V.tensor_tensor(stat[:, 3, :], stat[:, 2, :], stat[:, 0, :], ALU.mult))
                link(V.tensor_scalar(stat[:, 2, :], stat[:, 3, :], -0.5, 1.5, ALU.mult, ALU.add))
                V.tensor_tensor(stat[:, 1, :], stat[:, 1, :], stat[:, 2, :], ALU.mult).then_inc(rstd_done, 1)

            def scale(s):
                b0 = CREDIT + NCH * s
                with dve.Fori(0, NCH) as c:
                    dve.wait_ge(rstdb_done, b0 + c + 1)
                    V.tensor_tensor(xn[:, :, chunk(c)], xn[:, :, chunk(c)],
                                    ps[:, ds(c + 4, 1), :].broadcast_to([P, KD, CH]), ALU.mult).then_inc(xn_done, 1)

            def keys(l):
                v0 = V_ATT * l
                if l in (2, 3):
                    dve.wait_ge(mask_in, 16 * (l - 1))
                    how = (NEG, None, ALU.mult) if l == 2 else (0.0, NEG, ALU.is_equal, ALU.mult)
                    V.tensor_scalar(mtok[:, :, 0:KEYS], mtok_raw[l][:, :, 0:KEYS], *how)
                    V.memset(mtok[:, :, KEYS:KP], FLOOR).then_inc(mask_done, 1)
                if l == 2:
                    dve.wait_ge(rope_in, 16)
                dve.wait_ge(k_done, l + 1)
                for m in range(KD):
                    if l == 2:
                        r = [rt[:, n, 0:NB * KP].rearrange("p (b k) -> p b k", b=NB) for n in range(2)]
                        for n, w in enumerate((V_K, V_KS)):
                            link(V.tensor_scalar(r[n], ps[:, n, m * NB * KP:(m + 1) * NB * KP].rearrange("p (b k) -> p b k", b=NB),
                                                 cols[:, v0 + w + m:v0 + w + m + 1], None, ALU.add))
                            link(V.tensor_tensor(r[n], r[n], rope[:, n:n + 1, 0:KP].broadcast_to([P, NB, KP]), ALU.mult))
                        link(V.tensor_tensor(kt[:, m, :], rt[:, 0, 0:NB * KP], rt[:, 1, 0:NB * KP], ALU.add))
                    else:
                        link(V.tensor_scalar(kt[:, m, :], ps[:, 0, m * NB * KP:(m + 1) * NB * KP],
                                             cols[:, v0 + V_K + m:v0 + V_K + m + 1], 1.0 if l == 1 else 0.25,
                                             ALU.add, ALU.mult))
                V.sem_inc(kt_done, 1)

            def spread_keys():
                V.memset(kbd[:, :, :, :, KEYS:KP].rearrange("p m b h k -> p (m b h) k"), 0.0)
                V.memset(dif[:, :, :, KEYS:KP].rearrange("p n h k -> p (n h) k"), FLOOR)
                for m in range(KD):
                    for b in range(NB):
                        last = V.tensor_tensor(kbd[:, m, b, :, 0:KEYS],
                                               kt[:, m:m + 1, b * KP:b * KP + KEYS].broadcast_to([P, HH, KEYS]),
                                               blk.unsqueeze(2).broadcast_to([P, HH, KEYS]), ALU.mult)
                last.then_inc(kbd_done, 1)

            def spread_values(l, groups):
                a = MHA.index(l)
                for n in groups:
                    b, j = divmod(n, JG)
                    bank, half = VB[n // 2], n % 2
                    dve.wait_ge(vrep_done, NB * JG * a + n - half + 2)
                    V.tensor_tensor(vbd[:, b, j, :].rearrange("p (m h i) -> p m h i", m=KD, i=16),
                                    ps[:, bank, half * D:(half + 1) * D].rearrange("p (m h i) -> p m h i", m=KD, i=16),
                                    blk.unsqueeze(1).unsqueeze(3).broadcast_to([P, KD, HH, 16]),
                                    ALU.mult).then_inc(vbd_done, 1)

            def heads(l):
                a = MHA.index(l)

                def rotate(i, cc):
                    dve.wait_ge(q_done, CREDIT + i + 1)
                    for m in range(KD):
                        for n, w in enumerate((V_Q, V_QS)):
                            k_ = V_ATT * l + w + m
                            if m:
                                dve.wait_ge(rope_done, CREDIT + 6 * (i - NCH) + 3)
                            V.scalar_tensor_tensor(rt[:, n, :], ps[:, (2, 0)[n] + m, :], cols[:, k_:k_ + 1],
                                                   rope[:, n, ds(cc * CH, CH)], ALU.add, ALU.mult
                                                   ).then_inc(rope_done, 1)
                        dve.wait_ge(rope_done, CREDIT + 6 * (i - NCH) + 3 * m + 2)
                        V.tensor_tensor(q[:, m, :], rt[:, 0, :], rt[:, 1, :], ALU.add).then_inc(rope_done, 1)
                    dve.wait_ge(rope_done, CREDIT + 6 * (i - NCH) + 6)
                    V.sem_inc(qsb_done, 1)

                def subtract(i, n):
                    hf, t = divmod(n, TPC)
                    bank = 2 * ((n + 1) % 2)
                    heads_ = slice(HH * hf, HH * (hf + 1))
                    sc = ps[:, bank:bank + 2, 0:SL].rearrange("p g (h k) -> p g h k", k=KP)
                    dve.wait_ge(score_done, CREDIT + 8 * i + n + 1)
                    m_ = smax[:, t, heads_].rearrange("p (g h) -> p g h", g=2)
                    V.tensor_reduce(m_, sc[:, :, :, 0:KEYS] if l == 0 else sc, AX.X, ALU.max).then_inc(max_done, 1)
                    dve.wait_ge(max_done, CREDIT + 8 * i + n + 1)
                    dve.wait_ge(exp_done, CREDIT + 8 * i + max(n - 1, 0))
                    V.tensor_tensor(dif[:, n % 2, :, 0:KEYS].rearrange("p (g h) k -> p g h k", g=2), sc[:, :, :, 0:KEYS],
                                    m_.unsqueeze(3).broadcast_to([P, 2, 4, KEYS]), ALU.subtract).then_inc(sub_done, 1)

                def invert(i):
                    dve.wait_ge(den_done, CREDIT + i + 1)
                    V.tensor_scalar(ssum[:, :, :], ps[:, 6, 0:TPC * 16].rearrange("p (t h) -> p t h", t=TPC),
                                    1e-30 if l == 2 else 0.0, None, ALU.max).then_inc(clamp_done, 1)
                    dve.wait_ge(clamp_done, CREDIT + i + 1)
                    V.reciprocal(rd[:, :, :], ssum[:, :, :]).then_inc(rd_done, 1)

                def divide(i):
                    dve.wait_ge(rb_done, CREDIT + i + 1)
                    V.tensor_tensor(o[:, :, :], num[:, :, :], ps[:, 6:8, :], ALU.mult).then_inc(o_done, 1)

                def body(b, cc, before=True, after=True):
                    c = CPB * b + cc
                    i = NCH * a + c
                    if l == 2:
                        rotate(i, cc)
                    for n in range(8):
                        subtract(i, n)
                        if n == 2 and before:
                            invert(i - 1)
                        if n == 4 and before:
                            divide(i - 1)
                    if before:
                        dve.wait_ge(osc_done, CREDIT + i)
                        add_residual(c - 1)

                over_chunks(dve, body, round_weights if l == 2 else None)
                i = NCH * (a + 1) - 1
                invert(i)
                divide(i)
                dve.wait_ge(osc_done, CREDIT + i + 1)
                add_residual(NCH - 1)

            def single():
                for c in range(NCH):
                    dve.wait_ge(score1_done, CREDIT + c + 1)
                    sc = ps[:, 2, 0:TPC * KP].rearrange("p (t k) -> p t k", t=TPC)
                    V.tensor_reduce(neg4[:, 2, :], sc[:, :, 0:KEYS], AX.X, ALU.max).then_inc(max1_done, 1)
                    dve.wait_ge(max1_done, CREDIT + c + 1)
                    V.tensor_scalar(neg4[:, 0, :], neg4[:, 2, :], -1.0 / 16, None, ALU.mult).then_inc(neg1_done, 1)
                    dve.wait_ge(exp1_done, CREDIT + c + 1)
                    V.reciprocal(neg4[:, 2, :], neg4[:, 1, :]).then_inc(rd1_done, 1)
                    dve.wait_ge(rd1_done, CREDIT + c + 1)
                    V.tensor_tensor(p1[:, :, 0:KEYS], p1[:, :, 0:KEYS],
                                    neg4[:, 2, :].unsqueeze(2).broadcast_to([P, TPC, KEYS]), ALU.mult).then_inc(p1_done, 1)
                    if c:
                        dve.wait_ge(osc1_done, CREDIT + c)
                        add_residual(c - 1)
                dve.wait_ge(osc1_done, CREDIT + NCH)
                add_residual(NCH - 1)

            def add_residual(c):
                V.tensor_tensor(x[:, :, chunk(c)], x[:, :, chunk(c)], osc[:, :, :], ALU.add).then_inc(x_done, 1)

            def wide(v, n):
                return v.unsqueeze(2).broadcast_to([P, v.shape[1], n])

            def top(val, oh, n, t1, t2, m):
                link(V.tensor_reduce(m, val, AX.X, ALU.max))
                link(V.tensor_tensor(t1, val, wide(m, n), ALU.is_equal))
                link(V.tensor_tensor(t2, t1, cf[:, C_TIE:C_TIE + n].unsqueeze(1).broadcast_to([P, NT, n]), ALU.mult))
                link(V.tensor_reduce(m, t2, AX.X, ALU.max))
                link(V.tensor_tensor(oh, t2, wide(m, n), ALU.is_equal))

            def dot(dst, a_, b_, tmp):
                link(V.tensor_tensor(tmp, a_, b_, ALU.mult))
                link(V.tensor_reduce(dst, tmp, AX.X, ALU.add))

            def views(n_exp):
                return [a_[:, 0:NT * n_exp].rearrange("p (t e) -> p t e", e=n_exp) for a_ in ra + [oh1, oh2]]

            def bias_row(v, n):
                return v.unsqueeze(1).broadcast_to([P, NT, n])

            def probabilities(f, n_exp, r):
                logits = ps[:, 0, 0:NT * n_exp].rearrange("p (t e) -> p t e", e=n_exp)
                dve.wait_ge(front_done, CREDIT + 1 + NCH * (f + 1))
                link(V.tensor_reduce(rv[0], logits, AX.X, ALU.max))
                V.tensor_tensor(r[0], logits, wide(rv[0], n_exp), ALU.subtract).then_inc(smax_sub, 1)
                dve.wait_ge(smax_exp, f + 1)
                link(V.tensor_reduce(rv[1], r[1], AX.X, ALU.add))
                link(V.reciprocal(rv[1], rv[1]))

            def rows_of(f):
                with dve.Fori(0, NCH // 2) as it:
                    for r in range(2):
                        c = 2 * it + r
                        bank = (1, 6)[r]
                        dve.wait_ge(front_done, CREDIT + 1 + NCH * f + c + 1)
                        V.tensor_copy(rows_[:, ds(c * TPC, TPC), :].rearrange("p t n -> p (t n)"),
                                      ps[:, bank:bank + 2, :].rearrange("p b n -> p (b n)")).then_inc(rows_done, 1)

            def route0():
                n = R0
                r = views(n)
                o1, o2 = r[6], r[7]
                probabilities(0, n, r)
                link(V.tensor_tensor(r[2], r[1], wide(rv[1], n), ALU.mult))
                link(V.tensor_tensor(r[3], r[2], bias_row(gate_b[:, 0, :], n), ALU.add))
                top(r[3], o1, n, r[4], r[5], rv[2])
                link(V.scalar_tensor_tensor(r[0], o1, NEG, r[3], ALU.mult, ALU.add))
                top(r[0], o2, n, r[4], r[5], rv[2])
                V.tensor_tensor(mb16f[0], o1, o2, ALU.add).then_inc(pick_done, 1)
                for w, o_ in ((wt1, o1), (wt2, o2)):
                    dot(rv[3], r[2], o_, r[4])
                    link(V.tensor_scalar(w, rv[3], gts[:, 4:5], None, ALU.mult))
                dve.wait_ge(rank_done, 1)
                link(V.tensor_copy(e8[0], ps[:, 4, 0:n]))
                link(V.tensor_tensor(cmp8, e8[0].unsqueeze(2).broadcast_to([P, n, 16]),
                                     cf[:, C_STEP:C_STEP + 16].unsqueeze(1).broadcast_to([P, n, 16]), ALU.is_gt))
                link(V.tensor_reduce(e8[1], cmp8, AX.X, ALU.add))
                link(V.tensor_tensor(cmp8[:, :, 0:8], cf[:, C_LT:C_LT + 64].rearrange("p (a b) -> p a b", a=8),
                                     e8[1].unsqueeze(1).broadcast_to([P, 8, 8]), ALU.mult))
                link(V.tensor_reduce(e8[2], cmp8[:, :, 0:8], AX.X, ALU.add))
                link(V.tensor_scalar(e8[3], e8[2], float(P), None, ALU.mult))
                V.tensor_tensor(r[0], ps[:, 3, 0:NT * n].rearrange("p (t e) -> p t e", e=n), bias_row(e8[3], n),
                                ALU.add).then_inc(rank_read, 1)
                dve.wait_ge(rank_read, 1)
                dot(rv[4], r[0], o1, r[4])
                dot(rv[5], r[0], o2, r[4])
                link(V.tensor_copy(gix1, rv[4]))
                V.tensor_copy(gix2, rv[5]).then_inc(index_done, 1)
                link(V.tensor_tensor(e8[0], e8[1], e8[2], ALU.add))
                link(V.tensor_tensor(cmpt, e8[0].unsqueeze(1).broadcast_to([P, TILES0, 8]),
                                     cf[:, C_TILE:C_TILE + TILES0].unsqueeze(2).broadcast_to([P, TILES0, 8]), ALU.is_le))
                link(V.tensor_reduce(texf, cmpt, AX.X, ALU.add))
                V.tensor_scalar(tex, texf, float(R0 - 1), None, ALU.min).then_inc(texp_done, 1)

            def route1():
                n = E1
                r = views(n)
                o1 = r[6]
                probabilities(1, n, r)
                link(V.tensor_scalar(r[2], r[0], 0.0, None, ALU.add))
                top(r[2], o1, n, r[4], r[5], rv[2])
                V.tensor_copy(mb16f[1], o1).then_inc(pick_done, 1)
                dot(rv[3], o1, bias_row(cf[:, C_IDX:C_IDX + n], n), r[4])
                dve.wait_ge(rank_done, 2)
                V.tensor_tensor(r[3], ps[:, 3, 0:NT * n].rearrange("p (t e) -> p t e", e=n), o1, ALU.mult
                                ).then_inc(rank_read, 1)
                dve.wait_ge(rank_read, 2)
                link(V.tensor_reduce(rv[4], r[3], AX.X, ALU.add))
                link(V.tensor_scalar(rv[5], rv[4], float(C1), None, ALU.is_lt))
                link(V.tensor_scalar(rv[4], rv[4], float(C1 - 1), None, ALU.min))
                link(V.scalar_tensor_tensor(rv[6], rv[3], float(C1), rv[4], ALU.mult, ALU.add))
                link(V.tensor_copy(gix1, rv[6]))
                tok = cf[:, C_TOK:C_TOK + NT]
                link(V.tensor_tensor(rv[7], rv[6], tok, ALU.subtract))
                link(V.tensor_tensor(rv[7], rv[7], rv[5], ALU.mult))
                link(V.tensor_tensor(rv[7], rv[7], tok, ALU.add))
                V.tensor_copy(six, rv[7]).then_inc(index_done, 1)
                link(V.tensor_tensor(rv[5], rv[5], rv[1], ALU.mult))
                link(V.tensor_scalar(wt1, rv[5], gts[:, 5:6], None, ALU.mult))

            def round_weights():
                dve.wait_ge(wq_in, 32)
                for i, (dst, n, w) in enumerate(((wq1, F2 // P, D), (wq2, KD, F2))):
                    raw = wq_raw[:, 2048 * i:2048 * (i + 1)].rearrange("p (a b) -> p a b", a=n)
                    sw, inv = qs[:, i, 0:n], qs[:, 3, 0:n]
                    link(V.tensor_reduce(sw, raw, AX.X, ALU.max, apply_absolute_value=True))
                    link(V.tensor_scalar(sw, sw, 1e-8, 1.0 / 127, ALU.max, ALU.mult))
                    link(V.reciprocal(inv, sw))
                    link(V.tensor_tensor(raw, raw, wide(inv, w), ALU.mult))
                    link(V.tensor_scalar(raw, raw, MAGIC, MAGIC, ALU.add, ALU.subtract))
                    link(V.tensor_scalar(dst, raw, 127.0, -128.0, ALU.min, ALU.max))
                V.sem_inc(wround_done, 1)

            def scales(n, width, bias_at, sw, ss, qb):
                dve.wait_ge(allmax_done, n + 1)
                o_ = 4 * n
                link(V.tensor_scalar(qv[:, o_ + 2:o_ + 3], qv[:, o_ + 1:o_ + 2], 1e-8, 1.0 / 255, ALU.max, ALU.mult))
                link(V.reciprocal(qv[:, o_ + 3:o_ + 4], qv[:, o_ + 2:o_ + 3]))
                inv = qs[:, 3, 0:width]
                link(V.tensor_scalar(ss, sw, qv[:, o_ + 2:o_ + 3], None, ALU.mult))
                link(V.reciprocal(inv, ss))
                link(V.tensor_tensor(inv, inv, cols[:, bias_at:bias_at + width], ALU.mult))
                link(V.tensor_scalar(inv, inv, MAGIC, MAGIC, ALU.add, ALU.subtract))
                link(V.tensor_tensor(qb, inv, ss, ALU.mult))

            def quantized():
                dve.wait_ge(xn_done, CREDIT + NCH * 6)
                V.tensor_reduce(qv[:, 0:1], xn[:, :, :], AX.XY, ALU.max).then_inc(tmax_done, 1)
                scales(0, F2 // P, V_F2, qs[:, 0, :], qs[:, 2, :], qs[:, 4, :])
                V.sem_inc(xscale_done, 1)
                with dve.Fori(0, NCH) as c:
                    dve.wait_ge(xrnd_done, CREDIT + c + 1)
                    V.tensor_scalar(xn[:, :, chunk(c)], xn[:, :, chunk(c)], MAGIC, MAGIC + 255, ALU.max, ALU.min
                                    ).then_inc(xclip_done, 1)
                    dve.wait_ge(xclip_done, CREDIT + c + 1)
                    V.tensor_scalar(xq[:, :, chunk(c)], xn[:, :, chunk(c)], MAGIC, None, ALU.subtract).then_inc(xq_done, 1)
                with dve.Fori(0, NCH) as c:
                    dve.wait_ge(hact_done, CREDIT + 4 + 8 * c + 8)
                    last = V.tensor_reduce(qs[:, 5, ds(c, 1)], hbig[:, :, chunk(c)], AX.XY, ALU.max).then_inc(hmax_done, 1)
                dve.wait_ge(hmax_done, CREDIT + NCH)
                V.tensor_reduce(qv[:, 4:5], qs[:, 5, 0:NCH], AX.X, ALU.max).then_inc(tmax_done, 1)
                scales(1, KD, V_F2 + F2 // P, qs[:, 1, 0:KD], qs[:, 6, 0:KD], qs[:, 6, KD:2 * KD])
                link(V.tensor_scalar(qs[:, 7, 0:2 * KD], qs[:, 6, 0:2 * KD], gts[:, 6:7], None, ALU.mult))
                V.sem_inc(hscale_done, 1)
                with dve.Fori(0, NCH) as c:
                    dve.wait_ge(hrnd_done, CREDIT + c + 1)
                    V.tensor_scalar(hq[:, :, chunk(c)], hbig[:, :, chunk(c)], MAGIC, 255.0, ALU.subtract, ALU.min
                                    ).then_inc(hq_done, 1)
                with dve.Fori(0, NCH) as c:
                    dve.wait_ge(osc2_done, CREDIT + c + 1)
                    add_residual(c)

            def routing3():
                n, half = 8, 4
                sf, tmp, o1, rest, o2, ta, tb = lg3[2], lg3[3], lg3[4], lg3[5], lg3[6], lg3[7], lg3[0]
                pairs = sf.rearrange("p t (g i) -> p (t g) i", i=2)

                def best_group():
                    dve.wait_ge(sig3_done, 1)
                    link(V.tensor_tensor(sf, lg3[1], bias_row(gate_b[:, 1, :], n), ALU.add))
                    link(V.tensor_reduce(gr[0].rearrange("p t g -> p (t g)"), pairs, AX.X, ALU.add))
                    top(gr[0], gr[1], half, gr[5], gr[6], rv3[0])

                def second_group():
                    link(V.scalar_tensor_tensor(gr[2], gr[1], NEG, gr[0], ALU.mult, ALU.add))
                    top(gr[2], gr[3], half, gr[5], gr[6], rv3[0])
                    link(V.tensor_tensor(gr[4], gr[1], gr[3], ALU.add))
                    link(V.tensor_tensor(tmp.rearrange("p t (g i) -> p (t g) i", i=2), pairs,
                                         wide(gr[4].rearrange("p t g -> p (t g)"), 2), ALU.mult))

                def best_expert():
                    top(tmp, o1, n, ta, tb, rv3[0])
                    link(V.scalar_tensor_tensor(rest, o1, NEG, tmp, ALU.mult, ALU.add))

                def second_expert():
                    top(rest, o2, n, ta, tb, rv3[0])

                def weights():
                    dot(rv3[1], sf, o1, ta)
                    dot(rv3[2], sf, o2, ta)
                    link(V.tensor_tensor(rv3[3], rv3[1], rv3[2], ALU.add))
                    link(V.tensor_scalar(rv3[3], rv3[3], 1e-20, None, ALU.add))
                    link(V.reciprocal(rv3[4], rv3[3]))
                    link(V.tensor_scalar(rv3[4], rv3[4], 2.5, gts[:, 7:8], ALU.mult, ALU.mult))

                def table():
                    link(V.tensor_tensor(rv3[1], rv3[1], rv3[4], ALU.mult))
                    link(V.tensor_tensor(rv3[2], rv3[2], rv3[4], ALU.mult))
                    link(V.tensor_tensor(ta, o1, wide(rv3[1], n), ALU.mult))
                    link(V.tensor_tensor(tb, o2, wide(rv3[2], n), ALU.mult))
                    V.tensor_tensor(combt.rearrange("p e t -> p t e"), ta, tb, ALU.add).then_inc(comb3_done, 1)

                return best_group, second_group, best_expert, second_expert, weights, table

            def experts3():
                def expert(first, experts, c, n):
                    i = first + len(experts) * c + n
                    e = experts[n]
                    dve.wait_ge(ssig_done, CREDIT + IM * NCH + i + 1)
                    V.tensor_tensor(t3, sg3[:, n % 2, :], ps[:, 2 * (n % 2), :], ALU.mult).then_inc(spc_done, 1)
                    dve.wait_ge(spc_done, CREDIT + IM * NCH + i + 1)
                    V.tensor_tensor(u3, t3, ps[:, 2 * (n % 2) + 1, :], ALU.mult).then_inc(su_done, 1)
                    dve.wait_ge(su_done, CREDIT + IM * NCH + i + 1)
                    dve.wait_ge(so_done, CREDIT + NCH + i - n + max(n - 1, 0))
                    if e == 0:
                        dve.wait_ge(combb_in, 16 * 8 * (c + 1))
                    if e < 8:
                        V.tensor_tensor(h3[:, n % 2, :], u3, combb[:, e, chunk(c)], ALU.mult).then_inc(sh_done, 1)
                    else:
                        V.tensor_scalar(h3[:, n % 2, :], u3, gts[:, 7:8], None, ALU.mult).then_inc(sh_done, 1)

                def add(first, experts, c, done):
                    dve.wait_ge(so_done, CREDIT + NCH + first + len(experts) * (c + 1))
                    V.tensor_tensor(x[:, :, chunk(c)], x[:, :, chunk(c)], ps[:, 4:6, :], ALU.add).then_inc(done, 1)

                parts = routing3()
                for c in range(NCH):
                    for n in range(len(SHARED3)):
                        expert(0, SHARED3, c, n)
                        if 2 * c + n < len(parts):
                            parts[2 * c + n]()
                    add(0, SHARED3, c, sx_done)
                first = NCH * len(SHARED3)
                with dve.Fori(0, NCH) as c:
                    for n in range(len(ROUTED3)):
                        expert(first, ROUTED3, c, n)
                    add(first, ROUTED3, c, x_done)

            def shared0(part_):
                first, end = ((0, SPLIT), (SPLIT, NCH))[part_]

                def add(c):
                    dve.wait_ge(sosc_done, CREDIT + c + 1)
                    V.tensor_tensor(x[:, :, chunk(c)], x[:, :, chunk(c)], osc[:, :, :], ALU.add).then_inc(sx_done, 1)

                def body(c, before=True):
                    for n in range(2 * IM):
                        m, lin = divmod(n, 2)
                        at = V_F0 + 2 * IM * lin + IM + m
                        dve.wait_ge(sa_done, CREDIT + 8 * c + n + 1)
                        V.scalar_tensor_tensor((pl if lin else pg), ps[:, 2 * lin + 1, :], cols[:, at:at + 1],
                                               (al if lin else ag), ALU.add, ALU.mult).then_inc(sp_done, 1)
                        dve.wait_ge(sp_done, CREDIT + 8 * c + n + 1)
                        if not lin:
                            V.tensor_scalar(pg, pg, 7.0, None, ALU.min).then_inc(spm_done, 1)
                        else:
                            i = IM * c + m
                            V.tensor_scalar(pl, pl, 7.0, -7.0, ALU.min, ALU.max).then_inc(spc_done, 1)
                            dve.wait_ge(spc_done, CREDIT + i + 1)
                            V.scalar_tensor_tensor(uu, pl, 1.0, pg, ALU.add, ALU.mult).then_inc(su_done, 1)
                            dve.wait_ge(su_done, CREDIT + i + 1)
                            dve.wait_ge(ssig_done, CREDIT + i + 1)
                            if m == 0:
                                dve.wait_ge(so_done, CREDIT + c)
                            V.tensor_tensor(hs[:, m, :], uu, sig, ALU.mult).then_inc(sh_done, 1)
                        if n == 3 and before:
                            add(c - 1)

                if part_:
                    dve.wait_ge(o2_done, CREDIT + TILES0)
                body(first, before=False)
                with dve.Fori(first + 1, end) as c:
                    body(c)
                add(end - 1)

            def tiles0():
                def products(dst, a_, slot, lin, done):
                    for m in range(IM):
                        at = W0 + 2 * IM * lin + IM + m
                        last = V.scalar_tensor_tensor(dst[:, m * P:(m + 1) * P], ps[:, 2 * lin + 1, m * P:(m + 1) * P],
                                                      w0[slot][:, at:at + 1], a_[:, m * P:(m + 1) * P], ALU.add, ALU.mult)
                    last.then_inc(done, 1)

                def body(t, slot, use):
                    dve.wait_ge(ag_done, CREDIT + t + 1)
                    products(pg, ag, slot, 0, pg_done)
                    dve.wait_ge(pg_done, CREDIT + t + 1)
                    V.tensor_scalar(pg, pg, 7.0, None, ALU.min).then_inc(pgm_done, 1)
                    dve.wait_ge(al_done, CREDIT + t + 1)
                    products(pl, al, slot, 1, pl_done)
                    dve.wait_ge(pl_done, CREDIT + t + 1)
                    V.tensor_scalar(pl, pl, 7.0, -7.0, ALU.min, ALU.max).then_inc(plc_done, 1)
                    dve.wait_ge(plc_done, CREDIT + t + 1)
                    V.scalar_tensor_tensor(uu, pl, 1.0, pg, ALU.add, ALU.mult).then_inc(u_done, 1)
                    dve.wait_ge(u_done, CREDIT + t + 1)
                    dve.wait_ge(sig_done, CREDIT + t + 1)
                    V.tensor_tensor(hh[slot][:, 0:CH], uu, sig, ALU.mult).then_inc(h_done, 1)

                over_tiles(dve, TILES0, body, body, body)

            def tiles1():
                def body(t, slot, use):
                    dve.wait_ge(l_done, CREDIT + TILES0 + t + 1)
                    V.tensor_scalar(hh[slot][:, CH:F1], ps[:, 2, :], 0.0, None, ALU.max).then_inc(pl_done, 1)

                over_tiles(dve, E1, body, body, body)

            def combine(f):
                def weigh(c):
                    if f == 0:
                        return
                    sl = slice(c * TPC, (c + 1) * TPC)
                    dve.wait_ge(gath_in[c], 16 * TPC * 3)
                    V.tensor_tensor(ga[:, sl, :], ga[:, sl, :], wide(wt1[:, sl], D), ALU.mult).then_inc(y_done, 1)

                weigh(0)
                for c in range(NCH):
                    if c + 1 < NCH:
                        weigh(c + 1)
                    b0 = 2 * (c % 2)
                    dve.wait_ge(comb_done, CREDIT + NCH * f + c + 1)
                    V.tensor_tensor(x[:, :, c * CH:(c + 1) * CH], x[:, :, c * CH:(c + 1) * CH], ps[:, b0:b0 + 2, :],
                                    ALU.add).then_inc(x_done, 1)

            dve.wait_ge(const_in, 16 * 7)
            dve.wait_ge(first_in, 16 * 2)
            dve.wait_ge(tanh_done, 1)
            for l in MHA:
                last = V.tensor_scalar(gbo[:, l, :], cols[:, V_ATT * l + V_O:V_ATT * l + V_O + KD], gts[:, l:l + 1], None,
                                       ALU.mult)
            last = V.tensor_scalar(gbo[:, 1, :], cols[:, V_F0 + 4 * IM:V_F0 + 4 * IM + KD], gts[:, 4:5], None, ALU.mult)
            last.then_inc(gbo_done, 1)
            for s in range(stages):
                l = s // 2
                mha = s % 2 == 0 and l in MHA
                if s == 0:
                    keys(l)
                if s == 1:
                    dve.wait_ge(cb_in, 16)
                    V.tensor_copy(cb[:, :], cb_raw)
                centre(s)
                if s % 2 == 0 and s:
                    keys(l)
                variance(s)
                if mha:
                    spread_keys()
                newton(s)
                if mha:
                    spread_values(l, range(EARLY))
                scale(s)
                if mha:
                    spread_values(l, range(EARLY, NB * JG))
                if s % 2 == 0 and l in MHA:
                    heads(l)
                if s == 2:
                    single()
                if s == 5:
                    quantized()
                if s == 7:
                    experts3()
                if s == 1:
                    rows_of(0)
                    route0()
                    shared0(0)
                    tiles0()
                    shared0(1)
                    combine(0)
                if s == 3:
                    rows_of(1)
                    route1()
                    tiles1()
                    combine(1)


STAGES = 8


def kernel(**inputs):
    import concourse.bacc as bacc
    from concourse.bass_utils import run_bass_kernel_spmd

    arrays = host_layout(inputs)
    nc = bacc.Bacc("TRN2", target_bir_lowering=False, num_devices=1)
    dram = {n: nc.dram_tensor(f"in_{n}", a.shape, mybir.dt.from_np(a.dtype), kind="ExternalInput").ap()
            for n, a in arrays.items()}
    out = nc.dram_tensor("out_x", (P, KD, T), F32, kind="ExternalOutput").ap()
    program(nc, dram, out, STAGES)
    r = run_bass_kernel_spmd(nc, [{f"in_{n}": a for n, a in arrays.items()}], core_ids=[0])
    y = r.results[0]["out_x"]
    return np.ascontiguousarray(y.transpose(1, 0, 2).reshape(D, T).T.reshape(NB, S, D))
```
